# Optimizing a Trainium2 kernel written in Bass

```python
import numpy as np
import jax
import jax.numpy as jnp

def _softmax(x, axis=-1):
    return jax.nn.softmax(x, axis=axis)
def _gelu(x):
    return jax.nn.gelu(x, approximate=True)
def _silu(x):
    return jax.nn.silu(x)
def _sigmoid(x):
    return jax.nn.sigmoid(x)
def _layernorm(x, axis=-1, eps=1e-5):
    m = jnp.mean(x, axis=axis, keepdims=True)
    v = jnp.var(x, axis=axis, keepdims=True)
    return (x - m) / jnp.sqrt(v + eps)
def _scatter_add(tgt, idx, src, axis=0):
    return tgt.at[idx].add(src)
def _segment_sum(src, seg, n):
    return jax.ops.segment_sum(src, seg, n)

kernel_name = 'mk_adj_resnorm_d4_adj_256_80f1c6'

def setup_inputs(seed: int = 0):
    np.random.seed(seed)
    _w = jnp.asarray
    def _rec_inputs():
        import jax
        import jax.numpy as jnp
        _gk = jax.random.key(seed)
        x = -0.0005207 + 1.001 * jax.random.normal(jax.random.fold_in(_gk, 1), (128, 64, 256), jnp.float32)
        _a = jax.random.bernoulli(jax.random.fold_in(_gk, 2), 0.0625, (64, 64))
        _a = jnp.logical_or(_a, jnp.swapaxes(_a, -1, -2))
        _a = jnp.logical_or(_a, jnp.eye(64, dtype=bool))
        _af = _a.astype(jnp.float32)
        _af = _af * jax.random.uniform(jax.random.fold_in(_gk, 3), (64, 64), jnp.float32, 0.05, 32)
        adj = _af
        return x, adj
    x, adj = _rec_inputs()
    def _L0_gnn_setup():
        import jax, jax.numpy as jnp
        import numpy as np
        EPS_LN = 1e-05

        def _layernorm(x, g, b):
            mu = x.mean(-1, keepdims=True)
            var = ((x - mu) ** 2).mean(-1, keepdims=True)
            return (x - mu) / jnp.sqrt(var + EPS_LN) * g + b
        key = jax.random.key(seed)
        B, N, D, H = (4, 2048, 256, 4)
        hid = int(D * 2.0)
        ks = jax.random.split(key, 12)
        x = jax.random.normal(ks[0], (B, N, D), jnp.float32)
        Au = jax.random.uniform(ks[1], (N, N)) < 0.004
        A = jnp.logical_or(Au, Au.T)
        A = A.at[jnp.arange(N), jnp.arange(N)].set(False)
        Af = A.astype(jnp.float32)
        deg = Af.sum(axis=1)
        L = jnp.diag(deg) - Af
        adjacency = Af + jnp.eye(N, dtype=jnp.float32)
        s = lambda k, sh, f: jax.random.normal(k, sh, jnp.float32) * f
        sc = 1.0 / np.sqrt(D)
        Wc = s(ks[2], (D, D), sc)
        bc = jnp.zeros((D,), jnp.float32)
        Wq = s(ks[3], (D, D), sc)
        Wk = s(ks[4], (D, D), sc)
        Wv = s(ks[5], (D, D), sc)
        Wo = s(ks[6], (D, D), sc)
        bo = jnp.zeros((D,), jnp.float32)
        W1 = s(ks[7], (D, hid), sc)
        b1 = jnp.zeros((hid,), jnp.float32)
        W2 = s(ks[8], (hid, D), 1.0 / np.sqrt(hid))
        b2 = jnp.zeros((D,), jnp.float32)
        g1 = jnp.ones((D,), jnp.float32)
        be1 = jnp.zeros((D,), jnp.float32)
        g2 = jnp.ones((D,), jnp.float32)
        be2 = jnp.zeros((D,), jnp.float32)
        g3 = jnp.ones((D,), jnp.float32)
        be3 = jnp.zeros((D,), jnp.float32)
        return dict(x=x, L=L, adjacency=adjacency, Wc=Wc, bc=bc, g1=g1, be1=be1, Wq=Wq, Wk=Wk, Wv=Wv, Wo=Wo, bo=bo, g2=g2, be2=be2, W1=W1, b1=b1, W2=W2, b2=b2, g3=g3, be3=be3)
    _L0_gnn_all = _L0_gnn_setup()
    _L0_gnn_in = {k: v for k, v in _L0_gnn_all.items() if k in ('Wc', 'bc', 'g1', 'be1', 'Wq', 'Wk', 'Wv', 'Wo', 'bo', 'g2', 'be2', 'W1', 'b1', 'W2', 'b2', 'g3', 'be3', )}
    del _L0_gnn_all

    def _L1_gnn_setup():
        import jax, jax.numpy as jnp
        import numpy as np
        B, T, D, H = (64, 2048, 256, 256)
        MAX_SKIP = 4

        def _lstm_last(Wih, Whh, bih, bhh, xs):
            N, _, Hd = xs.shape
            bias = bih + bhh

            def step(carry, x_t):
                h, c = carry
                g = x_t @ Wih.T + h @ Whh.T + bias
                i, f, gg, o = jnp.split(g, 4, axis=-1)
                c = jax.nn.sigmoid(f) * c + jax.nn.sigmoid(i) * jnp.tanh(gg)
                h = jax.nn.sigmoid(o) * jnp.tanh(c)
                return ((h, c), None)
            init = (jnp.zeros((N, Hd), xs.dtype), jnp.zeros((N, Hd), xs.dtype))
            (h_last, _), _ = jax.lax.scan(step, init, jnp.swapaxes(xs, 0, 1))
            return h_last
        key = jax.random.key(seed)
        ks = jax.random.split(key, 8)
        s = 0.05
        x = jax.random.normal(ks[0], (B, T, D), jnp.float32)
        adj = jax.random.uniform(ks[1], (T, T), jnp.float32) / T
        Wg0 = jax.random.normal(ks[2], (D, H), jnp.float32) * s
        bg0 = jnp.zeros((H,), jnp.float32)
        Wg1 = jax.random.normal(ks[3], (H, H), jnp.float32) * s
        bg1 = jnp.zeros((H,), jnp.float32)
        Wih = jax.random.normal(ks[4], (MAX_SKIP, 4 * H, H), jnp.float32) * s
        Whh = jax.random.normal(ks[5], (MAX_SKIP, 4 * H, H), jnp.float32) * s
        bih = jax.random.normal(ks[6], (MAX_SKIP, 4 * H), jnp.float32) * s
        bhh = jax.random.normal(ks[7], (MAX_SKIP, 4 * H), jnp.float32) * s
        return dict(x=x, adj=adj, Wg0=Wg0, bg0=bg0, Wg1=Wg1, bg1=bg1, Wih=Wih, Whh=Whh, bih=bih, bhh=bhh)
    _L1_gnn_all = _L1_gnn_setup()
    _L1_gnn_in = {k: v for k, v in _L1_gnn_all.items() if k in ('Wg0', 'bg0', 'Wg1', 'bg1', 'Wih', 'Whh', 'bih', 'bhh', )}
    del _L1_gnn_all

    def _L2_gnn_setup():
        import jax, jax.numpy as jnp
        import numpy as np
        EPS = 1e-05

        def _batchnorm(x, gamma, beta):
            mu = jnp.mean(x, axis=0)
            var = jnp.var(x, axis=0)
            return (x - mu) * jax.lax.rsqrt(var + EPS) * gamma + beta
        key = jax.random.key(seed)
        ks = jax.random.split(key, 4)
        b, n, d, h, o = (32, 2048, 256, 512, 256)
        features = jax.random.normal(ks[0], (b, n, d), dtype=jnp.float32)
        A = jax.random.uniform(ks[1], (n, n), dtype=jnp.float32)
        lim1 = float(np.sqrt(6.0 / (d + h)))
        W1 = jax.random.uniform(ks[2], (h, d), minval=-lim1, maxval=lim1, dtype=jnp.float32)
        b1 = jnp.zeros((h,), jnp.float32)
        lim2 = float(np.sqrt(6.0 / (h + o)))
        W2 = jax.random.uniform(ks[3], (o, h), minval=-lim2, maxval=lim2, dtype=jnp.float32)
        b2 = jnp.zeros((o,), jnp.float32)
        g1 = jnp.ones((h,), jnp.float32)
        be1 = jnp.zeros((h,), jnp.float32)
        g2 = jnp.ones((o,), jnp.float32)
        be2 = jnp.zeros((o,), jnp.float32)
        return {'features': features, 'A': A, 'W1': W1, 'b1': b1, 'g1': g1, 'be1': be1, 'W2': W2, 'b2': b2, 'g2': g2, 'be2': be2}
    _L2_gnn_all = _L2_gnn_setup()
    _L2_gnn_in = {k: v for k, v in _L2_gnn_all.items() if k in ('W1', 'b1', 'g1', 'be1', 'W2', 'b2', 'g2', 'be2', )}
    del _L2_gnn_all

    def _L3_gnn_setup():
        import jax, jax.numpy as jnp
        import numpy as np
        B, N, D, H = (4, 4096, 256, 128)
        key = jax.random.key(seed)
        ks = jax.random.split(key, 10)
        base_features = jax.random.normal(ks[0], (B, N, D), dtype=jnp.float32)
        pc = (jax.random.uniform(ks[1], (N, N)) < 8.0 / N).astype(jnp.float32)
        pc = pc * (1.0 - jnp.eye(N, dtype=jnp.float32))
        neighbor_mask = jnp.clip(pc + pc.T + jnp.eye(N, dtype=jnp.float32), 0.0, 1.0)
        s = 1.0 / np.sqrt(D)
        Wq = jax.random.normal(ks[2], (D, H), dtype=jnp.float32) * s
        Wk = jax.random.normal(ks[3], (D, H), dtype=jnp.float32) * s
        Wv = jax.random.normal(ks[4], (D, H), dtype=jnp.float32) * s
        Wo = jax.random.normal(ks[5], (H, D), dtype=jnp.float32) * (1.0 / np.sqrt(H))
        bq = jnp.zeros((H,), jnp.float32)
        bk = jnp.zeros((H,), jnp.float32)
        bv = jnp.zeros((H,), jnp.float32)
        bo = jnp.zeros((D,), jnp.float32)
        alpha = jnp.asarray(2.0, jnp.float32)
        gamma = jnp.asarray(0.3, jnp.float32)
        return dict(base_features=base_features, neighbor_mask=neighbor_mask, parent_child_mask=pc, Wq=Wq, bq=bq, Wk=Wk, bk=bk, Wv=Wv, bv=bv, Wo=Wo, bo=bo, alpha=alpha, gamma=gamma)
    _L3_gnn_all = _L3_gnn_setup()
    _L3_gnn_in = {k: v for k, v in _L3_gnn_all.items() if k in ('Wq', 'bq', 'Wk', 'bk', 'Wv', 'bv', 'Wo', 'bo', 'alpha', 'gamma', )}
    del _L3_gnn_all

    return {
        "x": x,
        "adj": adj,
        "L0_gnn_Wc": _L0_gnn_in["Wc"],
        "L0_gnn_bc": _L0_gnn_in["bc"],
        "L0_gnn_g1": _L0_gnn_in["g1"],
        "L0_gnn_be1": _L0_gnn_in["be1"],
        "L0_gnn_Wq": _L0_gnn_in["Wq"],
        "L0_gnn_Wk": _L0_gnn_in["Wk"],
        "L0_gnn_Wv": _L0_gnn_in["Wv"],
        "L0_gnn_Wo": _L0_gnn_in["Wo"],
        "L0_gnn_bo": _L0_gnn_in["bo"],
        "L0_gnn_g2": _L0_gnn_in["g2"],
        "L0_gnn_be2": _L0_gnn_in["be2"],
        "L0_gnn_W1": _L0_gnn_in["W1"],
        "L0_gnn_b1": _L0_gnn_in["b1"],
        "L0_gnn_W2": _L0_gnn_in["W2"],
        "L0_gnn_b2": _L0_gnn_in["b2"],
        "L0_gnn_g3": _L0_gnn_in["g3"],
        "L0_gnn_be3": _L0_gnn_in["be3"],
        "L1_gnn_Wg0": _L1_gnn_in["Wg0"],
        "L1_gnn_bg0": _L1_gnn_in["bg0"],
        "L1_gnn_Wg1": _L1_gnn_in["Wg1"],
        "L1_gnn_bg1": _L1_gnn_in["bg1"],
        "L1_gnn_Wih": _L1_gnn_in["Wih"],
        "L1_gnn_Whh": _L1_gnn_in["Whh"],
        "L1_gnn_bih": _L1_gnn_in["bih"],
        "L1_gnn_bhh": _L1_gnn_in["bhh"],
        "L2_gnn_W1": _L2_gnn_in["W1"],
        "L2_gnn_b1": _L2_gnn_in["b1"],
        "L2_gnn_g1": _L2_gnn_in["g1"],
        "L2_gnn_be1": _L2_gnn_in["be1"],
        "L2_gnn_W2": _L2_gnn_in["W2"],
        "L2_gnn_b2": _L2_gnn_in["b2"],
        "L2_gnn_g2": _L2_gnn_in["g2"],
        "L2_gnn_be2": _L2_gnn_in["be2"],
        "L3_gnn_Wq": _L3_gnn_in["Wq"],
        "L3_gnn_bq": _L3_gnn_in["bq"],
        "L3_gnn_Wk": _L3_gnn_in["Wk"],
        "L3_gnn_bk": _L3_gnn_in["bk"],
        "L3_gnn_Wv": _L3_gnn_in["Wv"],
        "L3_gnn_bv": _L3_gnn_in["bv"],
        "L3_gnn_Wo": _L3_gnn_in["Wo"],
        "L3_gnn_bo": _L3_gnn_in["bo"],
        "L3_gnn_alpha": _L3_gnn_in["alpha"],
        "L3_gnn_gamma": _L3_gnn_in["gamma"],
    }

def reference(x, adj, L0_gnn_Wc, L0_gnn_bc, L0_gnn_g1, L0_gnn_be1, L0_gnn_Wq, L0_gnn_Wk, L0_gnn_Wv, L0_gnn_Wo, L0_gnn_bo, L0_gnn_g2, L0_gnn_be2, L0_gnn_W1, L0_gnn_b1, L0_gnn_W2, L0_gnn_b2, L0_gnn_g3, L0_gnn_be3, L1_gnn_Wg0, L1_gnn_bg0, L1_gnn_Wg1, L1_gnn_bg1, L1_gnn_Wih, L1_gnn_Whh, L1_gnn_bih, L1_gnn_bhh, L2_gnn_W1, L2_gnn_b1, L2_gnn_g1, L2_gnn_be1, L2_gnn_W2, L2_gnn_b2, L2_gnn_g2, L2_gnn_be2, L3_gnn_Wq, L3_gnn_bq, L3_gnn_Wk, L3_gnn_bk, L3_gnn_Wv, L3_gnn_bv, L3_gnn_Wo, L3_gnn_bo, L3_gnn_alpha, L3_gnn_gamma):
    import jax
    import jax.numpy as jnp
    def _L0_gnn_ref(x, L, adjacency, Wc, bc, g1, be1, Wq, Wk, Wv, Wo, bo, g2, be2, W1, b1, W2, b2, g3, be3):
        import jax, jax.numpy as jnp
        import numpy as np
        EPS_LN = 1e-05

        def _layernorm(x, g, b):
            mu = x.mean(-1, keepdims=True)
            var = ((x - mu) ** 2).mean(-1, keepdims=True)
            return (x - mu) / jnp.sqrt(var + EPS_LN) * g + b
        B, N, D = x.shape
        H = 4
        hd = D // H
        eig = jnp.linalg.eigvalsh(L)
        lam_max = eig[-1] + 1e-08
        L_norm = 2.0 * L / lam_max - jnp.eye(N, dtype=L.dtype)
        xp = jnp.einsum('mn,bnf->bmf', L_norm, x)
        h = xp @ Wc + bc
        h = _layernorm(h, g1, be1)
        h = jax.nn.relu(h)
        x1 = h + x
        q = (x1 @ Wq).reshape(B, N, H, hd).transpose(0, 2, 1, 3)
        k = (x1 @ Wk).reshape(B, N, H, hd).transpose(0, 2, 1, 3)
        v = (x1 @ Wv).reshape(B, N, H, hd).transpose(0, 2, 1, 3)
        scores = jnp.einsum('bhnd,bhmd->bhnm', q, k) / np.sqrt(hd).astype(np.float32)
        scores = jnp.where(adjacency[None, None] > 0, scores, jnp.float32(-1000000000.0))
        attn = jax.nn.softmax(scores, axis=-1)
        o = jnp.einsum('bhnm,bhmd->bhnd', attn, v)
        o = o.transpose(0, 2, 1, 3).reshape(B, N, D)
        o = o @ Wo + bo
        x2 = _layernorm(x1 + o, g2, be2)
        m = jax.nn.gelu(x2 @ W1 + b1, approximate=False) @ W2 + b2
        return _layernorm(x2 + m, g3, be3)

    def _L1_gnn_ref(x, adj, Wg0, bg0, Wg1, bg1, Wih, Whh, bih, bhh):
        import jax, jax.numpy as jnp
        import numpy as np
        B, T, D, H = (64, 2048, 256, 256)
        MAX_SKIP = 4

        def _lstm_last(Wih, Whh, bih, bhh, xs):
            N, _, Hd = xs.shape
            bias = bih + bhh

            def step(carry, x_t):
                h, c = carry
                g = x_t @ Wih.T + h @ Whh.T + bias
                i, f, gg, o = jnp.split(g, 4, axis=-1)
                c = jax.nn.sigmoid(f) * c + jax.nn.sigmoid(i) * jnp.tanh(gg)
                h = jax.nn.sigmoid(o) * jnp.tanh(c)
                return ((h, c), None)
            init = (jnp.zeros((N, Hd), xs.dtype), jnp.zeros((N, Hd), xs.dtype))
            (h_last, _), _ = jax.lax.scan(step, init, jnp.swapaxes(xs, 0, 1))
            return h_last
        h = jax.nn.relu(jnp.einsum('ts,bsh->bth', adj, x @ Wg0 + bg0))
        h = jax.nn.relu(jnp.einsum('ts,bsh->bth', adj, h @ Wg1 + bg1))
        Bv, Tv, Hd = h.shape
        for p in range(1, MAX_SKIP + 1):
            nw = Tv // p
            wins = h[:, :nw * p, :].reshape(Bv * nw, p, Hd)
            last = _lstm_last(Wih[p - 1], Whh[p - 1], bih[p - 1], bhh[p - 1], wins)
            idx = jnp.arange(nw) * p + (p - 1)
            h = h.at[:, idx, :].set(last.reshape(Bv, nw, Hd))
        return h

    def _L2_gnn_ref(features, A, W1, b1, g1, be1, W2, b2, g2, be2):
        import jax, jax.numpy as jnp
        import numpy as np
        EPS = 1e-05

        def _batchnorm(x, gamma, beta):
            mu = jnp.mean(x, axis=0)
            var = jnp.var(x, axis=0)
            return (x - mu) * jax.lax.rsqrt(var + EPS) * gamma + beta
        b, n, d = features.shape
        A_norm = A + jnp.eye(n, dtype=A.dtype)
        deg = jnp.sum(A_norm, axis=0) + jnp.sum(A_norm, axis=1) - jnp.diagonal(A_norm)
        dinv = jax.lax.rsqrt(deg)
        A_hat = A_norm * dinv[:, None] * dinv[None, :]
        agg = jnp.einsum('nm,bmd->bnd', A_hat, features)
        x = agg.reshape(-1, d)
        h = jax.nn.relu(_batchnorm(x @ W1.T + b1, g1, be1))
        out = h @ W2.T + b2
        out = _batchnorm(out, g2, be2)
        return out.reshape(b, n, -1)

    def _L3_gnn_ref(base_features, neighbor_mask, parent_child_mask, Wq, bq, Wk, bk, Wv, bv, Wo, bo, alpha, gamma):
        import jax, jax.numpy as jnp
        import numpy as np
        B, N, D, H = (4, 4096, 256, 128)
        x = base_features
        Q = x @ Wq + bq
        K = x @ Wk + bk
        V = x @ Wv + bv
        scale = 1.0 / jnp.sqrt(jnp.asarray(K.shape[-1], x.dtype))
        scores = jnp.einsum('bnh,bmh->bnm', Q, K) * scale
        scores = scores + parent_child_mask[None] * alpha
        scores = jnp.where(neighbor_mask[None] == 0, jnp.asarray(-1000000000.0, x.dtype), scores)
        attn = jax.nn.softmax(scores, axis=-1)
        attn_out = jnp.einsum('bnm,bmh->bnh', attn, V)
        refined = attn_out @ Wo + bo + x
        child_sum = jnp.einsum('nm,bmd->bnd', parent_child_mask, refined)
        is_parent = (parent_child_mask.sum(axis=1) > 0).astype(x.dtype)
        delta = gamma * (child_sum - refined)
        return refined + delta * is_parent[None, :, None]

    x = _layernorm(x + _L0_gnn_ref(x, adj, adj, L0_gnn_Wc, L0_gnn_bc, L0_gnn_g1, L0_gnn_be1, L0_gnn_Wq, L0_gnn_Wk, L0_gnn_Wv, L0_gnn_Wo, L0_gnn_bo, L0_gnn_g2, L0_gnn_be2, L0_gnn_W1, L0_gnn_b1, L0_gnn_W2, L0_gnn_b2, L0_gnn_g3, L0_gnn_be3), axis=-1)
    x = _layernorm(x + _L1_gnn_ref(x, adj, L1_gnn_Wg0, L1_gnn_bg0, L1_gnn_Wg1, L1_gnn_bg1, L1_gnn_Wih, L1_gnn_Whh, L1_gnn_bih, L1_gnn_bhh), axis=-1)
    x = _layernorm(x + _L2_gnn_ref(x, adj, L2_gnn_W1, L2_gnn_b1, L2_gnn_g1, L2_gnn_be1, L2_gnn_W2, L2_gnn_b2, L2_gnn_g2, L2_gnn_be2), axis=-1)
    x = _layernorm(x + _L3_gnn_ref(x, adj, adj, L3_gnn_Wq, L3_gnn_bq, L3_gnn_Wk, L3_gnn_bk, L3_gnn_Wv, L3_gnn_bv, L3_gnn_Wo, L3_gnn_bo, L3_gnn_alpha, L3_gnn_gamma), axis=-1)
    return x


_drawn_inputs = setup_inputs


def setup_inputs(seed=0):
    import zlib

    import numpy as np

    out = dict(_drawn_inputs(seed))
    spreads = {'L0_gnn_bc': (0.0, 0.1),
     'L0_gnn_g1': (1.0, 0.2),
     'L0_gnn_be1': (0.0, 0.1),
     'L0_gnn_bo': (0.0, 0.1),
     'L0_gnn_g2': (1.0, 0.2),
     'L0_gnn_be2': (0.0, 0.1),
     'L0_gnn_b1': (0.0, 0.1),
     'L0_gnn_b2': (0.0, 0.1),
     'L0_gnn_g3': (1.0, 0.2),
     'L0_gnn_be3': (0.0, 0.1),
     'L1_gnn_bg0': (0.0, 0.1),
     'L1_gnn_bg1': (0.0, 0.433),
     'L2_gnn_b1': (0.0, 0.8),
     'L2_gnn_g1': (1.0, 0.2),
     'L2_gnn_be1': (0.0, 0.1),
     'L2_gnn_b2': (0.0, 0.8),
     'L2_gnn_g2': (1.0, 0.2),
     'L2_gnn_be2': (0.0, 0.1),
     'L3_gnn_bq': (0.0, 0.69),
     'L3_gnn_bk': (0.0, 0.8),
     'L3_gnn_bv': (0.0, 0.1),
     'L3_gnn_bo': (0.0, 0.1)}
    factors = {'L1_gnn_Whh': 3.578, 'L1_gnn_bih': 2.909, 'L1_gnn_bhh': 2.915}
    for name, (base, spread) in spreads.items():
        noise = np.random.default_rng([zlib.crc32(name.encode()), seed]).standard_normal(out[name].shape)
        drawn = base * np.exp(spread * noise) if base else spread * noise
        out[name] = jnp.asarray(drawn.astype(out[name].dtype))
    for name, factor in factors.items():
        out[name] = (out[name] * factor).astype(out[name].dtype)
    return out
```

```python
from contextlib import ExitStack

import concourse.bass as bass
from concourse import mybir

ALU = mybir.AluOpType
ACT = mybir.ActivationFunctionType
F32 = mybir.dt.float32
AX_X = mybir.AxisListType.X

P = 128
BATCH, NODES, D = 128, 64, 256
TOKENS = BATCH * NODES
KD = D // P
HEADS = 4
HEAD_DIM = D // HEADS
HID0 = 2 * D
HID2 = 2 * D
ATT3 = 128
MAX_SKIP = 4
GATES = 4
EPS = 1e-5
NEG = 1e9
SQUARINGS = 24

GROUP = 512
STREAMS = 2
TILES = GROUP // P
TURNS = TOKENS // GROUP // STREAMS
BANKS = 8 // STREAMS
HALF = BANKS // 2


def alone(eng, waits_passed):
    eng.sem_inc(waits_passed, 1)


def ahead(eng, *lists, by=1):
    for group in lists:
        for s in group:
            eng.sem_inc(s, by)


class Chain:

    def __init__(self, eng, sem, per_turn=0):
        self.eng, self.sem, self.per_turn = eng, sem, per_turn
        self.base, self.n = 0, 0

    def turn(self, i):
        assert self.n in (0, self.per_turn), (self.n, self.per_turn)
        self.base, self.n = i * self.per_turn, 0

    def step(self, ins):
        ins.then_inc(self.sem, 1)
        self.n += 1

    def settle(self):
        self.eng.wait_ge(self.sem, self.base + self.n)

    def end(self):
        assert self.n == self.per_turn, (self.n, self.per_turn)


def build_stack(nc, t, out):
    with ExitStack() as ctx:
        build_program(nc, ctx, t, out.rearrange("b n d -> (b n) d"))


def build_program(nc, ctx, t, out_rows):
    def sb(name, shape):
        return ctx.enter_context(nc.sbuf_tensor(name, shape, F32))

    def sem(name):
        return ctx.enter_context(nc.semaphore(name))

    phase_sems = []

    def psem(name):
        phase_sems.append(nc.alloc_semaphore(name))
        return phase_sems[-1]

    def sems(name, n=STREAMS):
        return [psem(f"{name}{s}") for s in range(n)]

    def end_phase():
        nc.clear_and_free_semaphores(list(phase_sems))
        phase_sems.clear()
        nc.all_engine_barrier()

    X = sb("X", [P, TOKENS // P, D])
    H = sb("H", [P, KD, BATCH, NODES])
    Hflat = H[:].rearrange("p k b n -> p k (b n)")
    ARENA = 18432
    arena = sb("arena", [P, ARENA])
    ps = ctx.enter_context(nc.psum_tensor("ps", [P, 8, 512], F32))

    ident = sb("ident", [P, P])
    ones = sb("ones", [P, P])
    adjT = sb("adjT", [P, P])
    lnormT = sb("lnormT", [P, P])
    ahatT = sb("ahatT", [P, P])
    pos_mask = sb("pos_mask", [P, NODES])
    pos_neg = sb("pos_neg", [P, NODES])
    nz_mask = sb("nz_mask", [P, NODES])
    nz_neg = sb("nz_neg", [P, NODES])
    alpha_adj = sb("alpha_adj", [P, NODES])
    parent_gamma = sb("parent_gamma", [P, 1])
    bg0_rows = sb("bg0_rows", [P, KD, NODES])
    lstm_bias = sb("lstm_bias", [P, MAX_SKIP, 2 * GATES])
    b1_col = sb("b1_col", [P, HID0 // P])
    bn1_col = sb("bn1_col", [P, 3, HID2 // P])
    bn2_col = sb("bn2_col", [P, 3, KD])
    qk3_bias = sb("qk3_bias", [P, 2])
    scal = sb("scal", [P, 2])
    bn1_ss = sb("bn1_ss", [P, 2, HID2 // P])
    bn2_ss = sb("bn2_ss", [P, 2, KD])
    minus_half = sb("minus_half", [P, 16])
    eps_tile = sb("eps_tile", [P, TILES])
    bn_mv = sb("bn_mv", [P, 4, 2])
    bn_tmp = sb("bn_tmp", [P, 3, 4])
    ln_stats = sb("ln_stats", [P, STREAMS, TILES, 6])
    ln_mv = sb("ln_mv", [P, STREAMS, TILES, 2])
    ln_veps = sb("ln_veps", [P, STREAMS, TILES])
    ln_rstd = sb("ln_rstd", [P, STREAMS, TILES])

    def region(base, size):
        at = [0]

        def take(*dims):
            n = 1
            for x in dims:
                n *= x
            off = at[0]
            at[0] += n
            assert at[0] <= size, (at[0], size)
            v = base[:, off:off + n]
            if len(dims) == 2:
                v = v.rearrange("p (a b) -> p a b", a=dims[0])
            if len(dims) == 3:
                v = v.rearrange("p (a b c) -> p a b c", a=dims[0], b=dims[1])
            return v

        return take

    W_BASE, SLOT_A, SLOT_B, L2_BASE = 11264, 12288 + 256, 8192, 16384 + 256
    w0 = region(arena[:, 0:W_BASE], W_BASE)
    Wc = w0(KD, D)
    Wq, Wk, Wv, Wo = (w0(KD, D) for _ in range(4))
    W1 = w0(KD, HID0)
    W2 = w0(HID0 // P, D)
    vec0 = w0(9, D)
    bc, g1, be1, bo, g2, be2, b2, g3, be3 = (vec0[:, n, :] for n in range(9))

    wg = region(arena[:, W_BASE:SLOT_A], SLOT_A - W_BASE)
    Wg0, Wg1 = wg(KD, D), wg(KD, D)
    bg1 = wg(D)

    slot_a = region(arena[:, SLOT_A:L2_BASE], L2_BASE - SLOT_A)
    slot_b = region(arena[:, SLOT_B:SLOT_B + 4096], 4096)
    wih_a, whh_a = slot_a(KD, GATES * D), slot_a(KD, GATES * D)
    wih_b, whh_b = slot_b(KD, GATES * D), slot_b(KD, GATES * D)
    wih = [wih_a, wih_b, wih_a, wih_b]
    whh = [whh_a, whh_b, whh_a, whh_b]

    w2r = region(arena[:, L2_BASE:ARENA], ARENA - L2_BASE)
    L2W1 = w2r(KD, HID2)
    w3r = region(arena[:, SLOT_A:L2_BASE], L2_BASE - SLOT_A)
    L2W2 = w3r(HID2 // P, D)
    Wq3, Wk3, Wv3 = w3r(KD, ATT3), w3r(KD, ATT3), w3r(KD, ATT3)
    Wo3 = w3r(D)
    bv3, bo3 = w3r(ATT3), w3r(D)

    def bank(s, b):
        return ps[:, BANKS * s + b, :]

    def half(s, h):
        b = BANKS * s + HALF * h
        return ps[:, b:b + HALF, :].rearrange("p b w -> p (b w)")

    def token_major(s, h, width=D):
        v = half(s, h)
        return v[:, 0:TILES * width].rearrange("p (t d) -> p t d", t=TILES)

    def feature_major(s, h):
        return half(s, h).rearrange("p (k n) -> p k n", k=KD)

    def over_tiles(v, width=D):
        return v.unsqueeze(1).to_broadcast([P, TILES, width])

    waits_passed = sem("waits_passed")
    small_loaded = sem("small_loaded")
    w0_loaded = sem("w0_loaded")
    gcn_loaded = sem("gcn_loaded")
    lstm_loaded = [sem(f"lstm_loaded{p}") for p in range(MAX_SKIP)]
    l2_loaded = sem("l2_loaded")
    l3_loaded = sem("l3_loaded")

    def rows(name):
        return t[name].partition_broadcast(P)

    sq = region(Hflat[:, 0, :], TOKENS)
    adj_bd = sq(P)
    adj2 = sq(NODES)
    lstm_b2 = sq(2, MAX_SKIP, 2 * GATES)
    col = sq(16)
    S64, P64, SP64, M64, eye_s = (sq(NODES) for _ in range(5))
    abd, abdT, diag, ddinv = sq(P), sq(P), sq(P), sq(P)
    big = sq(P)

    zeroed = psem("zeroed")
    small_steps = psem("small_steps")
    small_mm = psem("small_mm")
    pool_made = psem("pool_made")
    adj_loaded = psem("adj_loaded")
    deg_ready = psem("deg_ready")
    sq_ready = psem("sq_ready")
    tr_ready = psem("tr_ready")
    sq_steps = psem("sq_steps")
    p_ready = psem("p_ready")
    q_ready = psem("q_ready")

    with nc.Block() as block:

        @block.sync
        def _(sp):
            sp.wait_ge(zeroed, 2)
            for g in range(2):
                r = slice(NODES * g, NODES * (g + 1))
                sp.dma_start(adjT[r, r], t["adjT"]).then_inc(adj_loaded, 16)
                sp.dma_start(adj_bd[r, r], t["adj"]).then_inc(adj_loaded, 16)
                sp.dma_start(adj2[r, :], t["adj"]).then_inc(adj_loaded, 16)
            for dst, name in ((lstm_b2[:, 0], "lstm_bih"), (lstm_b2[:, 1], "lstm_bhh"), (b1_col[:], "b1"),
                              (bn1_col[:], "bn1"), (bn2_col[:], "bn2"), (qk3_bias[:], "qk3b"), (col[:, 8:10], "bg0")):
                sp.dma_start(dst, t[name]).then_inc(small_loaded, 16)
            sp.dma_start(scal[:, 0:1], rows("alpha")).then_inc(small_loaded, 16)
            sp.dma_start(scal[:, 1:2], rows("gamma")).then_inc(small_loaded, 16)
            for dst, name in ((Wc, "Wc"), (Wq, "Wq"), (Wk, "Wk"), (Wv, "Wv"), (Wo, "Wo"), (W1, "W1"), (W2, "W2")):
                sp.dma_start(dst, t[name]).then_inc(w0_loaded, 16)
            for dst, name in ((bc, "bc"), (g1, "g1"), (be1, "be1"), (bo, "bo"), (g2, "g2"), (be2, "be2"),
                              (b2, "b2"), (g3, "g3"), (be3, "be3")):
                sp.dma_start(dst, rows(name)).then_inc(w0_loaded, 16)
            for dst, name in ((Wg0, "Wg0"), (Wg1, "Wg1")):
                sp.dma_start(dst, t[name]).then_inc(gcn_loaded, 16)
            sp.dma_start(bg1, rows("bg1")).then_inc(gcn_loaded, 16)
            sp.dma_start(wih[0], t["wih"][0]).then_inc(lstm_loaded[0], 16)
            sp.dma_start(L2W1, t["L2W1"]).then_inc(l2_loaded, 16)

        @block.gpsimd
        def _(pool):
            pool.memset(adjT[:], 0.0).then_inc(zeroed, 1)
            pool.memset(adj_bd, 0.0).then_inc(zeroed, 1)
            pool.memset(ident[:], 0.0).then_inc(pool_made, 1)
            pool.memset(minus_half[:], -0.5).then_inc(pool_made, 1)
            pool.memset(eps_tile[:], EPS).then_inc(pool_made, 1)
            pool.wait_ge(pool_made, 3)
            pool.affine_select(out=ident[:], in_=ident[:], compare_op=ALU.not_equal, fill=1.0, base=0,
                               pattern=[[-1, P]], channel_multiplier=1).then_inc(pool_made, 1)
            pool.memset(ones[:], 1.0).then_inc(pool_made, 1)
            pool.wait_ge(deg_ready, 1)
            pool.tensor_tensor(col[:, 5:6], col[:, 4:5], minus_half[:, 0:1], ALU.pow).then_inc(pool_made, 1)

        @block.vector
        def _(dve):
            c = Chain(dve, small_steps)

            def link(ins):
                c.step(ins)
                c.settle()

            dve.wait_ge(adj_loaded, 96)
            dve.wait_ge(small_loaded, 9 * 16)
            dve.wait_ge(pool_made, 5)
            link(dve.tensor_scalar(pos_mask[:], adj2, 0.0, None, ALU.is_gt))
            link(dve.tensor_scalar(nz_mask[:], adj2, 0.0, None, ALU.not_equal))
            link(dve.tensor_scalar(pos_neg[:], pos_mask[:], NEG, -NEG, ALU.mult, ALU.add))
            link(dve.tensor_scalar(nz_neg[:], nz_mask[:], NEG, -NEG, ALU.mult, ALU.add))
            link(dve.tensor_scalar(alpha_adj[:], adj2, scal[:, 0:1], None, ALU.mult))
            link(dve.tensor_reduce(col[:, 0:1], adj2, AX_X, ALU.add))
            link(dve.tensor_scalar(parent_gamma[:], col[:, 0:1], 0.0, scal[:, 1:2], ALU.is_gt, ALU.mult))
            link(dve.tensor_tensor(lstm_bias[:], lstm_b2[:, 0], lstm_b2[:, 1], ALU.add))
            link(dve.tensor_tensor(abd, adj_bd, ident[:], ALU.add))
            link(dve.tensor_tensor(abdT, adjT[:], ident[:], ALU.add))
            link(dve.tensor_tensor(diag, abd, ident[:], ALU.mult))
            link(dve.tensor_reduce(col[:, 1:2], abd, AX_X, ALU.add))
            link(dve.tensor_reduce(col[:, 2:3], abdT, AX_X, ALU.add))
            link(dve.tensor_reduce(col[:, 3:4], diag, AX_X, ALU.add))
            link(dve.tensor_tensor(col[:, 4:5], col[:, 1:2], col[:, 2:3], ALU.add))
            dve.tensor_tensor(col[:, 4:5], col[:, 4:5], col[:, 3:4], ALU.subtract).then_inc(deg_ready, 1)
            dve.wait_ge(pool_made, 6)
            link(dve.tensor_scalar(abdT, abdT, col[:, 5:6], None, ALU.mult))
            link(dve.tensor_scalar(ddinv, ident[:], col[:, 5:6], None, ALU.mult))
            link(dve.tensor_scalar(big, ident[:], col[:, 0:1], None, ALU.mult))
            link(dve.tensor_tensor(S64[0:NODES], adj_bd[0:NODES, 0:NODES], adjT[0:NODES, 0:NODES], ALU.add))
            link(dve.tensor_scalar(S64[0:NODES], S64[0:NODES], 0.5, None, ALU.mult))
            dve.tensor_reduce(col[0:NODES, 6:7], S64[0:NODES], AX_X, ALU.add,
                              apply_absolute_value=True).then_inc(sq_ready, 1)
            dve.wait_ge(small_mm, 1)
            link(dve.tensor_tensor(ahatT[:], abdT, bank(0, 0)[:, 0:P], ALU.mult))
            for k in range(KD):
                link(dve.tensor_scalar(bg0_rows[:, k, :], bank(0, 0)[:, P:P + NODES], col[:, 8 + k:9 + k], None,
                                       ALU.mult))
            dve.wait_ge(small_mm, 2)
            dve.tensor_reduce(col[0:1, 7:8], bank(0, 1)[0:1, 0:NODES], AX_X, ALU.max).then_inc(sq_ready, 1)
            dve.wait_ge(small_mm, 3)
            link(dve.tensor_copy(col[0:NODES, 10:11], bank(0, 2)[0:NODES, 0:1]))
            link(dve.tensor_scalar(eye_s[0:NODES], ident[0:NODES, 0:NODES], col[0:NODES, 10:11], None, ALU.mult))
            link(dve.tensor_tensor(P64[0:NODES], S64[0:NODES], eye_s[0:NODES], ALU.add))
            link(dve.reciprocal(col[0:NODES, 11:12], col[0:NODES, 10:11]))
            dve.tensor_scalar(P64[0:NODES], P64[0:NODES], col[0:NODES, 11:12], None, ALU.mult).then_inc(p_ready, 1)
            ch = Chain(dve, sq_steps, 2)
            with dve.Fori(0, SQUARINGS) as i:
                ch.turn(i)
                dve.wait_ge(p_ready, i + 1)
                ch.step(dve.tensor_tensor(M64[0:NODES], P64[0:NODES], P64[0:NODES], ALU.mult))
                ch.settle()
                dve.tensor_reduce(col[0:NODES, 12:13], M64[0:NODES], AX_X, ALU.add).then_inc(q_ready, 1)
                dve.wait_ge(tr_ready, 2 * i + 2)
                ch.step(dve.reciprocal(col[0:NODES, 13:14], bank(0, 4 % BANKS)[0:NODES, 0:1]))
                ch.settle()
                dve.tensor_scalar(P64[0:NODES], bank(0, 3)[0:NODES, 0:NODES], col[0:NODES, 13:14], None,
                                  ALU.mult).then_inc(p_ready, 1)
            ch.end()
            dve.wait_ge(p_ready, SQUARINGS + 1)
            link(dve.tensor_tensor(M64[0:NODES], P64[0:NODES], P64[0:NODES], ALU.mult))
            link(dve.tensor_reduce(col[0:NODES, 15:16], M64[0:NODES], AX_X, ALU.add))
            dve.wait_ge(small_mm, 4)
            link(dve.tensor_tensor(M64[0:NODES], P64[0:NODES], bank(0, 3)[0:NODES, 0:NODES], ALU.mult))
            dve.tensor_reduce(col[0:NODES, 14:15], M64[0:NODES], AX_X, ALU.add).then_inc(sq_ready, 1)
            dve.wait_ge(small_mm, 5)
            link(dve.reciprocal(col[:, 12:13], bank(0, 2)[:, 1:2]))
            link(dve.tensor_scalar(col[:, 13:14], bank(0, 2)[:, 0:1], col[:, 12:13], 1e-8, ALU.mult, ALU.add))
            link(dve.reciprocal(col[:, 12:13], col[:, 13:14]))
            link(dve.tensor_scalar(big, adjT[:], 2.0, col[:, 12:13], ALU.mult, ALU.mult))
            link(dve.tensor_tensor(lnormT[:], big, ident[:], ALU.subtract))

        @block.tensor
        def _(pe):
            pe.wait_ge(sq_ready, 1)
            pe.matmul(bank(0, 0)[:, 0:P], ones[:], ddinv, start=True, stop=True)
            pe.matmul(bank(0, 0)[:, P:2 * P], ones[:], big, start=True, stop=True).then_inc(small_mm, 1)
            pe.transpose(bank(0, 1)[0:1, 0:NODES], col[0:NODES, 6:7], ident[0:NODES, 0:NODES]).then_inc(small_mm, 1)
            pe.wait_ge(sq_ready, 2)
            pe.matmul(bank(0, 2)[0:NODES, 0:1], ones[0:1, 0:NODES], col[0:1, 7:8], start=True, stop=True)\
              .then_inc(small_mm, 1)
            with pe.Fori(0, SQUARINGS) as i:
                pe.wait_ge(p_ready, i + 1)
                alone(pe, waits_passed)
                pe.matmul(bank(0, 3)[0:NODES, 0:NODES], P64[0:NODES], P64[0:NODES], start=True, stop=True)\
                  .then_inc(tr_ready, 1)
                pe.wait_ge(q_ready, i + 1)
                pe.matmul(bank(0, 4 % BANKS)[:, 0:1], ones[0:NODES, :], col[0:NODES, 12:13],
                          start=True, stop=True).then_inc(tr_ready, 1)
            pe.wait_ge(p_ready, SQUARINGS + 1)
            pe.matmul(bank(0, 3)[0:NODES, 0:NODES], S64[0:NODES], P64[0:NODES], start=True, stop=True)\
              .then_inc(small_mm, 1)
            pe.wait_ge(sq_ready, 3)
            pe.matmul(bank(0, 2)[:, 0:2], ones[0:NODES, :], col[0:NODES, 14:16], start=True, stop=True)\
              .then_inc(small_mm, 1)

    end_phase()

    hb = region(Hflat.rearrange("p k n -> p (k n)"), KD * TOKENS)
    eb = region(arena[:, 6912:W_BASE], W_BASE - 6912)
    G2 = KD * GROUP
    xs, zT, hbuf, x1, x1T, vt = ([hb(G2) for _ in range(STREAMS)] for _ in range(6))
    attn_bd = [hb(HEADS * TILES, P) for _ in range(STREAMS)]
    attnT = [eb(HEADS * TILES, P) for _ in range(STREAMS)]
    tok = [[v.rearrange("p (t d) -> p t d", t=TILES) for v in b] for b in (xs, hbuf, x1, vt)]
    xs_t, hb_t, x1_t, v_t = tok
    zT_f, x1T_f = ([v.rearrange("p (k n) -> p k n", k=KD) for v in b] for b in (zT, x1T))
    sc = [v.rearrange("p (g j m) -> p g j m", g=2, m=NODES) for v in zT]
    qT = [attnT[s].rearrange("p a b -> p (a b)")[:, 0:G2].rearrange("p (k n) -> p k n", k=KD)
          for s in range(STREAMS)]
    kT = [attnT[s].rearrange("p a b -> p (a b)")[:, G2:2 * G2].rearrange("p (k n) -> p k n", k=KD)
          for s in range(STREAMS)]
    mT = [attnT[s].rearrange("p a b -> p (a b)").rearrange("p (m n) -> p m n", m=HID0 // P)
          for s in range(STREAMS)]
    NJ = 2 * TILES
    sm_max = sb("sm_max", [P, STREAMS, 2 * NJ])
    sm_sum = sb("sm_sum", [P, STREAMS, 2 * NJ])
    sm_inv = sb("sm_inv", [P, STREAMS, 2 * NJ])
    x_rows = t["x"].rearrange("(g t p) d -> g p t d", p=P, t=TILES)

    def scores_ps(s):
        return ps[:, BANKS * s:BANKS * s + 2, 0:NJ * NODES].rearrange("p g (j m) -> p g j m", m=NODES)

    def wide(s):
        return ps[:, BANKS * s:BANKS * (s + 1), :].rearrange("p b (c n) -> p (b c) n", n=P)

    def wide_up(s):
        return ps[:, BANKS * s:BANKS * (s + 1), :].rearrange("p b w -> p (b w)").rearrange(
            "p (m n) -> p m n", m=HID0 // P)

    xs_loaded = sems("xs_loaded")
    agg_done, zT_ready, h_done = sems("agg_done"), sems("zT_ready"), sems("h_done")
    var_ready, rstd_ready = sems("var_ready"), sems("rstd_ready")
    x1_ready, x1_turned, x1T_ready = sems("x1_ready"), sems("x1_turned"), sems("x1T_ready")
    q_done, k_done, v_done = sems("q_done"), sems("k_done"), sems("v_done")
    qT_ready, kT_ready, v_ready = sems("qT_ready"), sems("kT_ready"), sems("v_ready")
    sc_done, sc_ready, exp_ready = sems("sc_done"), sems("sc_ready"), sems("exp_ready")
    at_turned, atA_ready, atB_ready = sems("at_turned"), sems("atA_ready"), sems("atB_ready")
    o_done, o_ready, o_turned, oT_ready = sems("o_done"), sems("o_ready"), sems("o_turned"), sems("oT_ready")
    wo_done, x2_ready, x2_turned, x2T_ready = sems("wo_done"), sems("x2_ready"), sems("x2_turned"), sems("x2T_ready")
    up_done, gelu_ready, down_done, y_ready = sems("up_done"), sems("gelu_ready"), sems("down_done"), sems("y_ready")
    l0_steps = psem("l0_steps")
    bd_zero = psem("bd_zero")
    S = range(STREAMS)
    LN0 = 4

    def ln_statistics(dve, c, y, s, ready):
        for n in range(TILES):
            c.step(dve.bn_stats(ln_stats[:, s, n, :], y[:, n, :]))
        c.settle()
        alone(dve, waits_passed)
        for n in range(TILES):
            ins = dve.bn_aggr(ln_mv[:, s, n, :], ln_stats[:, s, n, :])
            if n < TILES - 1:
                c.step(ins)
        ins.then_inc(ready, 1)

    def ln_affine(dve, c, y, s, g, be, rstd, count, mean_at):
        dve.wait_ge(*mean_at)
        for n in range(TILES):
            c.step(dve.scalar_tensor_tensor(out=y[:, n, :], in0=y[:, n, :], scalar=ln_mv[:, s, n, 0:1], in1=g,
                                            op0=ALU.subtract, op1=ALU.mult))
        c.settle()
        dve.wait_ge(rstd, count)
        for n in range(TILES):
            c.step(dve.scalar_tensor_tensor(out=y[:, n, :], in0=y[:, n, :], scalar=ln_rstd[:, s, n:n + 1], in1=be,
                                            op0=ALU.mult, op1=ALU.add))
        c.settle()

    def ln_plain(dve, out_ap, y, s, rstd, count):
        dve.wait_ge(rstd, count)
        for n in range(TILES):
            ins = dve.tensor_scalar(out_ap[:, n, :], y[:, n, :], ln_mv[:, s, n, 0:1], ln_rstd[:, s, n:n + 1],
                                    ALU.subtract, ALU.mult)
        return ins

    def ln_rstd_on_pool(pool, s, ready, rstd, count):
        pool.wait_ge(ready, count)
        pool.tensor_tensor(ln_veps[:, s, :], ln_mv[:, s, :, 1], eps_tile[:, 0:TILES], ALU.add).then_inc(pool_steps, 1)
        pool_count[0] += 1
        pool.wait_ge(pool_steps, pool_base[0] + pool_count[0])
        pool.tensor_tensor(ln_rstd[:, s, :], ln_veps[:, s, :], minus_half[:, 0:TILES], ALU.pow).then_inc(rstd, 1)

    pool_steps = psem("pool_steps")
    pool_count, pool_base = [0], [0]

    with nc.Block() as block:

        @block.sync
        def _(sp):
            with sp.Fori(0, TURNS) as i:
                for s in S:
                    sp.wait_ge(y_ready[s], i + 1)
                    sp.dma_start(xs_t[s], x_rows[bass.ds(i * STREAMS + s, 1)].rearrange("g p t d -> (g p) t d"))\
                      .then_inc(xs_loaded[s], 16)
        @block.gpsimd
        def _(pool):
            for s in S:
                pool.memset(attn_bd[s], 0.0).then_inc(bd_zero, 1)
            with pool.Fori(0, TURNS) as i:
                pool_base[0], pool_count[0] = i * (LN0 * STREAMS), 0
                for ln in range(LN0):
                    for s in S:
                        ln_rstd_on_pool(pool, s, var_ready[s], rstd_ready[s], LN0 * i + ln + 1)
            assert pool_count[0] == LN0 * STREAMS

        @block.scalar
        def _(act):
            act.wait_ge(bd_zero, STREAMS)
            with act.Fori(0, TURNS) as i:
                for s in S:
                    act.wait_ge(agg_done[s], i + 1)
                    act.activation(zT_f[s], feature_major(s, 0), ACT.Copy).then_inc(zT_ready[s], 1)
                for s in S:
                    act.wait_ge(x1_turned[s], i + 1)
                    act.activation(x1T_f[s], feature_major(s, 0), ACT.Copy).then_inc(x1T_ready[s], 1)
                for s in S:
                    act.wait_ge(q_done[s], i + 1)
                    act.activation(qT[s], feature_major(s, 1), ACT.Copy, scale=float(HEAD_DIM) ** -0.5)\
                       .then_inc(qT_ready[s], 1)
                for s in S:
                    act.wait_ge(sc_ready[s], i + 1)
                    for b in range(2):
                        r = slice(NODES * b, NODES * (b + 1))
                        ins = act.activation(attn_bd[s][r, :, r], sc[s].rearrange("p g j m -> p (g j) m")[r], ACT.Exp)
                    ins.then_inc(exp_ready[s], 1)
                for s in S:
                    act.wait_ge(at_turned[s], i + 1)
                    n = HEADS * TILES // 2
                    act.activation(attnT[s][:, 0:n, :], wide(s)[:, 0:n, :], ACT.Copy).then_inc(atA_ready[s], 1)
                for s in S:
                    act.wait_ge(o_turned[s], i + 1)
                    act.activation(zT_f[s], feature_major(s, 1), ACT.Copy).then_inc(oT_ready[s], 1)
                for s in S:
                    act.wait_ge(x2_turned[s], i + 1)
                    act.activation(x1T_f[s], feature_major(s, 1), ACT.Copy).then_inc(x2T_ready[s], 1)
                for s in S:
                    act.wait_ge(up_done[s], i + 1)
                    for m in range(HID0 // P):
                        ins = act.activation(mT[s][:, m, :], wide_up(s)[:, m, :], ACT.Gelu, bias=b1_col[:, m:m + 1])
                    ins.then_inc(gelu_ready[s], 1)

        @block.vector
        def _(dve):
            c = Chain(dve, l0_steps, STREAMS * (1 + (2 * TILES - 1) + 2 * TILES
                                                + 3 + 1
                                                + 2 + (2 * TILES - 1) + 2 * TILES
                                                + 2 + (2 * TILES - 1) + 2 * TILES + 1 + (2 * TILES - 1)
                                                + 2))
            dve.wait_ge(w0_loaded, 16 * 16)
            ahead(dve, y_ready)
            with dve.Fori(0, TURNS) as i:
                c.turn(i)
                for s in S:
                    dve.wait_ge(h_done[s], i + 1)
                    c.step(dve.tensor_tensor(hb_t[s], token_major(s, 1), over_tiles(bc), ALU.add))
                    c.settle()
                    ln_statistics(dve, c, hb_t[s], s, var_ready[s])
                for s in S:
                    ln_affine(dve, c, hb_t[s], s, g1, be1, rstd_ready[s], LN0 * i + 1, (var_ready[s], LN0 * i + 1))
                    dve.wait_ge(xs_loaded[s], 16 * i + 16)
                    dve.scalar_tensor_tensor(out=x1_t[s], in0=hb_t[s], scalar=0.0, in1=xs_t[s],
                                             op0=ALU.max, op1=ALU.add).then_inc(x1_ready[s], 1)
                for s in S:
                    dve.wait_ge(k_done[s], i + 1)
                    dve.tensor_copy(kT[s], feature_major(s, 0)).then_inc(kT_ready[s], 1)
                for s in S:
                    dve.wait_ge(v_done[s], i + 1)
                    dve.tensor_copy(v_t[s], token_major(s, 1)).then_inc(v_ready[s], 1)
                for s in S:
                    dve.wait_ge(sc_done[s], i + 1)
                    full = [P, 2, NJ, NODES]
                    flat = sc[s].rearrange("p g j m -> p (g j) m")
                    c.step(dve.tensor_tensor(sc[s], scores_ps(s),
                                             pos_mask[:].unsqueeze(1).unsqueeze(1).to_broadcast(full), ALU.mult))
                    c.settle()
                    c.step(dve.tensor_tensor(flat, flat, pos_neg[:].unsqueeze(1).to_broadcast([P, 2 * NJ, NODES]),
                                             ALU.add))
                    c.settle()
                    c.step(dve.tensor_reduce(sm_max[:, s, :], flat, AX_X, ALU.max))
                    c.settle()
                    dve.tensor_tensor(flat, flat, sm_max[:, s, :].unsqueeze(2).to_broadcast([P, 2 * NJ, NODES]),
                                      ALU.subtract).then_inc(sc_ready[s], 1)
                for s in S:
                    dve.wait_ge(exp_ready[s], i + 1)
                    c.step(dve.tensor_reduce(sm_sum[:, s, :], attn_bd[s], AX_X, ALU.add))
                    c.settle()
                    c.step(dve.reciprocal(sm_inv[:, s, :], sm_sum[:, s, :]))
                    dve.wait_ge(at_turned[s], i + 1)
                    n = HEADS * TILES // 2
                    dve.tensor_copy(attnT[s][:, n:2 * n, :], wide(s)[:, n:2 * n, :]).then_inc(atB_ready[s], 1)
                for s in S:
                    dve.wait_ge(o_done[s], i + 1)
                    c.settle()
                    for g in range(2):
                        o_ps = half(s, 0).rearrange("p (g j d) -> p g j d", g=2, d=HEAD_DIM)[:, g]
                        o_sb = hbuf[s].rearrange("p (j g d) -> p j g d", g=2, d=HEAD_DIM)[:, :, g]
                        inv = sm_inv[:, s, g * NJ:(g + 1) * NJ].unsqueeze(2).to_broadcast([P, NJ, HEAD_DIM])
                        ins = dve.tensor_tensor(o_sb, o_ps, inv, ALU.mult)
                        if g == 0:
                            c.step(ins)
                    ins.then_inc(o_ready[s], 1)
                for s in S:
                    dve.wait_ge(wo_done[s], i + 1)
                    c.step(dve.tensor_tensor(hb_t[s], token_major(s, 0), over_tiles(bo), ALU.add))
                    c.settle()
                    c.step(dve.tensor_tensor(hb_t[s], hb_t[s], x1_t[s], ALU.add))
                    c.settle()
                    ln_statistics(dve, c, hb_t[s], s, var_ready[s])
                for s in S:
                    ln_affine(dve, c, hb_t[s], s, g2, be2, rstd_ready[s], LN0 * i + 2, (var_ready[s], LN0 * i + 2))
                    dve.sem_inc(x2_ready[s], 1)
                for s in S:
                    dve.wait_ge(down_done[s], i + 1)
                    c.step(dve.tensor_tensor(x1_t[s], token_major(s, 0), over_tiles(b2), ALU.add))
                    c.settle()
                    c.step(dve.tensor_tensor(x1_t[s], x1_t[s], hb_t[s], ALU.add))
                    c.settle()
                    ln_statistics(dve, c, x1_t[s], s, var_ready[s])
                for s in S:
                    ln_affine(dve, c, x1_t[s], s, g3, be3, rstd_ready[s], LN0 * i + 3, (var_ready[s], LN0 * i + 3))
                    c.step(dve.tensor_tensor(x1_t[s], x1_t[s], xs_t[s], ALU.add))
                    c.settle()
                    ln_statistics(dve, c, x1_t[s], s, var_ready[s])
                for s in S:
                    ln_plain(dve, X[:, bass.ds((i * STREAMS + s) * TILES, TILES), :], x1_t[s], s,
                             rstd_ready[s], LN0 * i + 4).then_inc(y_ready[s], 1)
            c.end()

        @block.tensor
        def _(pe):
            pe.wait_ge(w0_loaded, 16 * 16)
            with pe.Fori(0, TURNS) as i:
                for s in S:
                    pe.wait_ge(xs_loaded[s], 16 * i + 16)
                    pe.wait_ge(y_ready[s], i + 1)
                    for n in range(TILES):
                        for k in range(KD):
                            mm = pe.matmul(feature_major(s, 0)[:, k, n * P:(n + 1) * P],
                                           xs_t[s][:, n, k * P:(k + 1) * P], lnormT[:], start=True, stop=True)
                    mm.then_inc(agg_done[s], 1)
                for s in S:
                    pe.wait_ge(zT_ready[s], i + 1)
                    for n in range(TILES):
                        for k in range(KD):
                            mm = pe.matmul(token_major(s, 1)[:, n, :], zT_f[s][:, k, n * P:(n + 1) * P], Wc[:, k, :],
                                           start=(k == 0), stop=(k == KD - 1))
                    mm.then_inc(h_done[s], 1)
                for s in S:
                    pe.wait_ge(x1_ready[s], i + 1)
                    for n in range(TILES):
                        for k in range(KD):
                            mm = pe.transpose(feature_major(s, 0)[:, k, n * P:(n + 1) * P],
                                              x1_t[s][:, n, k * P:(k + 1) * P], ident[:])
                    mm.then_inc(x1_turned[s], 1)
                for s in S:
                    pe.wait_ge(x1T_ready[s], i + 1)
                    for m in range(KD):
                        for k in range(KD):
                            mm = pe.matmul(feature_major(s, 1)[:, m, :], Wq[:, k, m * P:(m + 1) * P],
                                           x1T_f[s][:, k, :], start=(k == 0), stop=(k == KD - 1))
                    mm.then_inc(q_done[s], 1)
                for s in S:
                    for m in range(KD):
                        for k in range(KD):
                            mm = pe.matmul(feature_major(s, 0)[:, m, :], Wk[:, k, m * P:(m + 1) * P],
                                           x1T_f[s][:, k, :], start=(k == 0), stop=(k == KD - 1))
                    mm.then_inc(k_done[s], 1)
                for s in S:
                    pe.wait_ge(qT_ready[s], i + 1)
                    for n in range(TILES):
                        for k in range(KD):
                            mm = pe.matmul(token_major(s, 1)[:, n, :], x1T_f[s][:, k, n * P:(n + 1) * P], Wv[:, k, :],
                                           start=(k == 0), stop=(k == KD - 1))
                    mm.then_inc(v_done[s], 1)
                for s in S:
                    pe.wait_ge(kT_ready[s], i + 1)
                    pe.wait_ge(v_ready[s], i + 1)
                    alone(pe, waits_passed)
                    for g in range(2):
                        f = slice(HEAD_DIM * g, HEAD_DIM * (g + 1))
                        for n in range(TILES):
                            for b in range(2):
                                q = slice(n * P + NODES * b, n * P + NODES * (b + 1))
                                for h2 in range(HEADS // 2):
                                    mm = pe.matmul(scores_ps(s)[NODES * b:NODES * (b + 1), g, 2 * n + h2, :],
                                                   qT[s][f, h2, q], kT[s][f, h2, q], start=True, stop=True)
                    mm.then_inc(sc_done[s], 1)
                for s in S:
                    pe.wait_ge(exp_ready[s], i + 1)
                    for j in range(HEADS * TILES):
                        mm = pe.transpose(wide(s)[:, j, :], attn_bd[s][:, j, :], ident[:])
                    mm.then_inc(at_turned[s], 1)
                for s in S:
                    pe.wait_ge(atA_ready[s], i + 1)
                    pe.wait_ge(atB_ready[s], i + 1)
                    o_ps = half(s, 0).rearrange("p (j d) -> p j d", d=HEAD_DIM)
                    for g in range(2):
                        for n in range(TILES):
                            for h2 in range(HEADS // 2):
                                j = g * NJ + 2 * n + h2
                                h = 2 * h2 + g
                                mm = pe.matmul(o_ps[:, j, :], attnT[s][:, j, :],
                                               v_t[s][:, n, HEAD_DIM * h:HEAD_DIM * (h + 1)], start=True, stop=True)
                    mm.then_inc(o_done[s], 1)
                for s in S:
                    pe.wait_ge(o_ready[s], i + 1)
                    for n in range(TILES):
                        for k in range(KD):
                            mm = pe.transpose(feature_major(s, 1)[:, k, n * P:(n + 1) * P],
                                              hb_t[s][:, n, k * P:(k + 1) * P], ident[:])
                    mm.then_inc(o_turned[s], 1)
                for s in S:
                    pe.wait_ge(oT_ready[s], i + 1)
                    for n in range(TILES):
                        for k in range(KD):
                            mm = pe.matmul(token_major(s, 0)[:, n, :], zT_f[s][:, k, n * P:(n + 1) * P], Wo[:, k, :],
                                           start=(k == 0), stop=(k == KD - 1))
                    mm.then_inc(wo_done[s], 1)
                for s in S:
                    pe.wait_ge(x2_ready[s], i + 1)
                    for n in range(TILES):
                        for k in range(KD):
                            mm = pe.transpose(feature_major(s, 1)[:, k, n * P:(n + 1) * P],
                                              hb_t[s][:, n, k * P:(k + 1) * P], ident[:])
                    mm.then_inc(x2_turned[s], 1)
                for s in S:
                    pe.wait_ge(x2T_ready[s], i + 1)
                    for m in range(HID0 // P):
                        for k in range(KD):
                            mm = pe.matmul(wide_up(s)[:, m, :], W1[:, k, m * P:(m + 1) * P], x1T_f[s][:, k, :],
                                           start=(k == 0), stop=(k == KD - 1))
                    mm.then_inc(up_done[s], 1)
                for s in S:
                    pe.wait_ge(gelu_ready[s], i + 1)
                    for n in range(TILES):
                        for k in range(HID0 // P):
                            mm = pe.matmul(token_major(s, 0)[:, n, :], mT[s][:, k, n * P:(n + 1) * P], W2[:, k, :],
                                           start=(k == 0), stop=(k == HID0 // P - 1))
                    mm.then_inc(down_done[s], 1)

    end_phase()

    gb = region(arena[:, 0:W_BASE], W_BASE)
    xg, zg, h1T, ug = ([gb(G2) for _ in S] for _ in range(4))
    xg_t, ug_t = ([v.rearrange("p (t d) -> p t d", t=TILES) for v in b] for b in (xg, ug))
    zg_f, h1T_f = ([v.rearrange("p (k n) -> p k n", k=KD) for v in b] for b in (zg, h1T))
    xg_ready, ga_done, zg_ready, g0_done = sems("xg_ready"), sems("ga_done"), sems("zg_ready"), sems("g0_done")
    g0_biased, h1_ready, g1_done, ug_ready = sems("g0_biased"), sems("h1_ready"), sems("g1_done"), sems("ug_ready")
    gb_done, gcn_ready = sems("gb_done"), sems("gcn_ready")
    g0_half = psem("g0_half")

    with nc.Block() as block:

        @block.gpsimd
        def _(pool):
            with pool.Fori(0, TURNS) as i:
                for s in S:
                    pool.wait_ge(ga_done[s], i + 1)
                    pool.tensor_copy(xg_t[s], X[:, bass.ds((i * STREAMS + s) * TILES, TILES), :])\
                        .then_inc(xg_ready[s], 1)

        @block.scalar
        def _(act):
            ahead(act, gcn_ready)
            with act.Fori(0, TURNS) as i:
                for s in S:
                    act.wait_ge(ga_done[s], i + 2)
                    act.activation(zg_f[s], feature_major(s, 0), ACT.Copy).then_inc(zg_ready[s], 1)
                for s in S:
                    act.wait_ge(g0_biased[s], i + 1)
                    act.activation(h1T[s], h1T[s], ACT.Relu).then_inc(h1_ready[s], 1)
                for s in S:
                    act.wait_ge(gb_done[s], i + 1)
                    act.activation(Hflat[:, :, bass.ds((i * STREAMS + s) * GROUP, GROUP)], feature_major(s, 1),
                                   ACT.Relu).then_inc(gcn_ready[s], 1)

        @block.vector
        def _(dve):
            dve.wait_ge(gcn_loaded, 3 * 16)
            ahead(dve, ug_ready)
            with dve.Fori(0, TURNS) as i:
                for s in S:
                    dve.wait_ge(g0_done[s], i + 1)
                    for k in range(KD):
                        nb = GROUP // NODES
                        ins = dve.tensor_tensor(h1T_f[s][:, k, :].rearrange("p (b n) -> p b n", n=NODES),
                                                feature_major(s, 1)[:, k, :].rearrange("p (b n) -> p b n", n=NODES),
                                                bg0_rows[:, k, :].unsqueeze(1).to_broadcast([P, nb, NODES]), ALU.add)
                        ins.then_inc(g0_half, 1)
                    dve.wait_ge(g0_half, (i * STREAMS + s + 1) * KD)
                    dve.sem_inc(g0_biased[s], 1)
                for s in S:
                    dve.wait_ge(g1_done[s], i + 1)
                    dve.tensor_tensor(ug_t[s], token_major(s, 0), over_tiles(bg1), ALU.add).then_inc(ug_ready[s], 1)

        @block.tensor
        def _(pe):
            pe.wait_ge(gcn_loaded, 3 * 16)
            ahead(pe, ga_done)
            with pe.Fori(0, TURNS) as i:
                for s in S:
                    pe.wait_ge(xg_ready[s], i + 1)
                    pe.wait_ge(ug_ready[s], i + 1)
                    for n in range(TILES):
                        for k in range(KD):
                            mm = pe.matmul(feature_major(s, 0)[:, k, n * P:(n + 1) * P],
                                           xg_t[s][:, n, k * P:(k + 1) * P], adjT[:], start=True, stop=True)
                    mm.then_inc(ga_done[s], 1)
                for s in S:
                    pe.wait_ge(zg_ready[s], i + 1)
                    pe.wait_ge(gcn_ready[s], i + 1)
                    for m in range(KD):
                        for k in range(KD):
                            mm = pe.matmul(feature_major(s, 1)[:, m, :], Wg0[:, k, m * P:(m + 1) * P],
                                           zg_f[s][:, k, :], start=(k == 0), stop=(k == KD - 1))
                    mm.then_inc(g0_done[s], 1)
                for s in S:
                    pe.wait_ge(h1_ready[s], i + 1)
                    for n in range(TILES):
                        for k in range(KD):
                            mm = pe.matmul(token_major(s, 0)[:, n, :], h1T_f[s][:, k, n * P:(n + 1) * P], Wg1[:, k, :],
                                           start=(k == 0), stop=(k == KD - 1))
                    mm.then_inc(g1_done[s], 1)
                for s in S:
                    pe.wait_ge(ug_ready[s], i + 2)
                    for n in range(TILES):
                        for k in range(KD):
                            mm = pe.matmul(feature_major(s, 1)[:, k, n * P:(n + 1) * P],
                                           ug_t[s][:, n, k * P:(k + 1) * P], adjT[:], start=True, stop=True)
                    mm.then_inc(gb_done[s], 1)

    end_phase()

    LS = 2
    COLS = 256
    lb = region(arena[:, 0:SLOT_B], SLOT_B)
    gate = [lb(GATES, KD * COLS) for _ in range(LS)]
    cell = [lb(KD * COLS) for _ in range(LS)]
    newc = [lb(KD * COLS) for _ in range(LS)]
    tanc = [lb(KD * COLS) for _ in range(LS)]
    hid = [lb(KD * COLS) for _ in range(LS)]

    for p in range(1, MAX_SKIP + 1):
        nw = NODES // p
        nb = min(COLS // nw, 4 * p if p != 3 else 8)
        n_cols = nw * nb
        turns = BATCH // nb // LS
        n_steps = LS * p
        gates_done = sems(f"gates_done{p}_", LS)
        act_done = sems(f"act_done{p}_", LS)
        cell_ready = sems(f"cell_ready{p}_", LS)
        tanh_ready = sems(f"tanh_ready{p}_", LS)
        hid_ready = sems(f"hid_ready{p}_", LS)
        lstm_steps = psem(f"lstm_steps{p}_")
        order = (0, 2, 1, 3)

        def gates_of(j):
            return [q for q in order if not (q == 1 and j == 0)]

        per_turn = sum(len(gates_of(j)) for j in range(p))

        def gate_ps(s, q, m):
            b = q * KD + m
            return ps[:, 4 * s + b // 2, (b % 2) * COLS:(b % 2) * COLS + n_cols]

        def live(v):
            return v.rearrange("p (k n) -> p k n", k=KD)[:, :, 0:n_cols]

        def window(i, s, j):
            return H[:, :, bass.ds((i * LS + s) * nb, nb), j:j + p * (nw - 1) + 1:p]

        with nc.Block() as block:

            @block.sync
            def _(sp):
                if p == 1:
                    sp.dma_start(wih[1], t["wih"][1]).then_inc(lstm_loaded[1], 16)
                    sp.dma_start(whh[1], t["whh"][1]).then_inc(lstm_loaded[1], 16)
                if p in (2, 3):
                    sp.dma_start(wih[p], t["wih"][p]).then_inc(lstm_loaded[p], 16)
                    sp.dma_start(whh[p], t["whh"][p]).then_inc(lstm_loaded[p], 16)
                if p == 4:
                    for dst, name in ((L2W2, "L2W2"), (Wq3, "Wq3"), (Wk3, "Wk3"), (Wv3, "Wv3"), (Wo3, "Wo3")):
                        sp.dma_start(dst, t[name]).then_inc(l3_loaded, 16)
                    sp.dma_start(bv3, rows("bv3")).then_inc(l3_loaded, 16)
                    sp.dma_start(bo3, rows("bo3")).then_inc(l3_loaded, 16)

            @block.scalar
            def _(act):
                with act.Fori(0, turns) as i:
                    for j in range(p):
                        for s in range(LS):
                            done = sum(len(gates_of(jj)) for jj in range(j))
                            if j == 0:
                                act.wait_ge(hid_ready[s], i * p + 1)
                            for n, q in enumerate(gates_of(j)):
                                act.wait_ge(gates_done[s], i * per_turn + done + n + 1)
                                for m in range(KD):
                                    ins = act.activation(gate[s][:, q, :].rearrange("p (k n) -> p k n", k=KD)
                                                         [:, m, 0:n_cols], gate_ps(s, q, m),
                                                         ACT.Tanh if q == 2 else ACT.Sigmoid,
                                                         bias=lstm_bias[:, p - 1, 2 * q + m:2 * q + m + 1])
                                ins.then_inc(act_done[s], 1)
                            act.wait_ge(cell_ready[s], i * p + j + 1)
                            act.activation(live(tanc[s]), live(cell[s]), ACT.Tanh).then_inc(tanh_ready[s], 1)

            @block.vector
            def _(dve):
                ahead(dve, hid_ready)
                c = Chain(dve, lstm_steps, LS * (2 * (p - 1)))
                with dve.Fori(0, turns) as i:
                    c.turn(i)
                    for j in range(p):
                        for s in range(LS):
                            done = sum(len(gates_of(jj)) for jj in range(j))
                            gi, gf, gg, go = (live(gate[s][:, q, :]) for q in range(GATES))
                            dve.wait_ge(act_done[s], i * per_turn + done + 2)
                            if j == 0:
                                dve.tensor_tensor(live(cell[s]), gi, gg, ALU.mult).then_inc(cell_ready[s], 1)
                            else:
                                c.step(dve.tensor_tensor(live(newc[s]), gi, gg, ALU.mult))
                                dve.wait_ge(act_done[s], i * per_turn + done + 3)
                                c.step(dve.tensor_tensor(live(cell[s]), live(cell[s]), gf, ALU.mult))
                                c.settle()
                                dve.tensor_tensor(live(cell[s]), live(cell[s]), live(newc[s]), ALU.add)\
                                   .then_inc(cell_ready[s], 1)
                            dve.wait_ge(act_done[s], i * per_turn + done + len(gates_of(j)))
                            dve.wait_ge(tanh_ready[s], i * p + j + 1)
                            if j < p - 1:
                                dve.tensor_tensor(live(hid[s]), go, live(tanc[s]), ALU.mult)\
                                   .then_inc(hid_ready[s], 1)
                            else:
                                halves = [x.rearrange("p k (b w) -> p k b w", b=nb) for x in (go, live(tanc[s]))]
                                dve.tensor_tensor(window(i, s, j), *halves, ALU.mult).then_inc(hid_ready[s], 1)
                c.end()

            @block.tensor
            def _(pe):
                pe.wait_ge(lstm_loaded[p - 1], 16 if p == 1 else 32)
                with pe.Fori(0, turns) as i:
                    for j in range(p):
                        for s in range(LS):
                            pe.wait_ge(hid_ready[s], i * p + j + 1)
                            for q in gates_of(j):
                                for m in range(KD):
                                    f = slice((q * KD + m) * P, (q * KD + m + 1) * P)
                                    o = gate_ps(s, q, m).rearrange("p (b w) -> p b w", b=nb)
                                    for k in range(KD):
                                        mm = pe.matmul(o, wih[p - 1][:, k, f], window(i, s, j)[:, k],
                                                       start=(k == 0), stop=(j == 0 and k == KD - 1))
                                    if j > 0:
                                        for k in range(KD):
                                            mm = pe.matmul(gate_ps(s, q, m), whh[p - 1][:, k, f],
                                                           live(hid[s])[:, k, :], start=False, stop=(k == KD - 1))
                                mm.then_inc(gates_done[s], 1)

        end_phase()

    cb = region(arena[:, 0:SLOT_A], SLOT_A)
    hs, ys = ([cb(G2) for _ in S] for _ in range(2))
    hs_f = [v.rearrange("p (k n) -> p k n", k=KD) for v in hs]
    ys_t = [v.rearrange("p (t d) -> p t d", t=TILES) for v in ys]
    MB = HID2 // P
    bn_stats1 = cb(MB, STREAMS * TURNS * 6)
    bn_stats2 = cb(KD, STREAMS * TURNS * 6)
    hs_ready, h_turned, l1_ready, l1_var, l1_rstd = (sems(n) for n in
                                                     ("hs_ready", "h_turned", "l1_ready", "l1_var", "l1_rstd"))
    g2_done, g2_ready, up2_done, up2_taken = (sems(n) for n in ("g2_done", "g2_ready", "up2_done", "up2_taken"))
    p7_steps = psem("p7_steps")
    pool7 = psem("pool7")

    def fold_batch_norm(dve, c, stats, cols, ss, blocks, ready, made, biased):
        for m in range(blocks):
            c.step(dve.bn_aggr(bn_mv[:, m, :], stats[:, m, :]))
        c.settle()
        mv = bn_mv[:, 0:blocks, :]
        if biased:
            c.step(dve.tensor_scalar(bn_tmp[:, 0, 0:blocks], mv[:, :, 0], -1.0, None, ALU.mult))
        else:
            c.step(dve.tensor_tensor(bn_tmp[:, 0, 0:blocks], mv[:, :, 0], cols[:, 0, :], ALU.add))
        c.step(dve.tensor_scalar(bn_tmp[:, 1, 0:blocks], mv[:, :, 1], EPS, None, ALU.add))
        c.settle()
        dve.sem_inc(ready, 1)
        if not biased:
            c.step(dve.tensor_tensor(bn_tmp[:, 0, 0:blocks], cols[:, 0, :], bn_tmp[:, 0, 0:blocks], ALU.subtract))
            c.settle()
        dve.wait_ge(made, 1)
        c.step(dve.tensor_tensor(ss[:, 0, :], bn_tmp[:, 2, 0:blocks], cols[:, 1, :], ALU.mult))
        c.settle()
        c.step(dve.tensor_tensor(bn_tmp[:, 0, 0:blocks], bn_tmp[:, 0, 0:blocks], ss[:, 0, :], ALU.mult))
        c.settle()
        c.step(dve.tensor_tensor(ss[:, 1, :], bn_tmp[:, 0, 0:blocks], cols[:, 2, :], ALU.add))
        c.settle()

    bn1_var, bn1_pow = psem("bn1_var"), psem("bn1_pow")
    x_kept = sems("x_kept")
    bn_steps = psem("bn_steps")

    with nc.Block() as block:

        @block.gpsimd
        def _(pool):
            with pool.Fori(0, TURNS) as i:
                pool_base[0], pool_count[0] = i * STREAMS, 0
                for s in S:
                    pool.wait_ge(h_turned[s], i + 1)
                    pool.tensor_copy(hs_f[s], Hflat[:, :, bass.ds((i * STREAMS + s) * GROUP, GROUP)])\
                        .then_inc(hs_ready[s], 1)
                for s in S:
                    pool.wait_ge(l1_var[s], i + 1)
                    pool.tensor_tensor(ln_veps[:, s, :], ln_mv[:, s, :, 1], eps_tile[:, 0:TILES], ALU.add)\
                        .then_inc(pool7, 1)
                    pool.wait_ge(pool7, i * STREAMS + s + 1)
                    pool.tensor_tensor(ln_rstd[:, s, :], ln_veps[:, s, :], minus_half[:, 0:TILES], ALU.pow)\
                        .then_inc(l1_rstd[s], 1)
            pool.wait_ge(bn1_var, 1)
            pool.tensor_tensor(bn_tmp[:, 2, 0:MB], bn_tmp[:, 1, 0:MB], minus_half[:, 0:MB], ALU.pow)\
                .then_inc(bn1_pow, 1)

        @block.scalar
        def _(act):
            with act.Fori(0, TURNS) as i:
                for s in S:
                    act.wait_ge(g2_done[s], i + 1)
                    act.activation(Hflat[:, :, bass.ds((i * STREAMS + s) * GROUP, GROUP)], feature_major(s, 1),
                                   ACT.Copy).then_inc(g2_ready[s], 1)

        @block.vector
        def _(dve):
            ahead(dve, up2_taken, by=4)
            c = Chain(dve, p7_steps, STREAMS * (1 + 2 * TILES - 1 + (TILES - 1)))
            with dve.Fori(0, TURNS) as i:
                c.turn(i)
                for s in S:
                    dve.wait_ge(h_turned[s], i + 2)
                    c.step(dve.tensor_tensor(ys_t[s], token_major(s, 0),
                                             X[:, bass.ds((i * STREAMS + s) * TILES, TILES), :], ALU.add))
                    c.settle()
                    ln_statistics(dve, c, ys_t[s], s, l1_var[s])
                for s in S:
                    dve.wait_ge(l1_rstd[s], i + 1)
                    for n in range(TILES):
                        ins = dve.tensor_scalar(ys_t[s][:, n, :], ys_t[s][:, n, :], ln_mv[:, s, n, 0:1],
                                                ln_rstd[:, s, n:n + 1], ALU.subtract, ALU.mult)
                        if n < TILES - 1:
                            c.step(ins)
                    ins.then_inc(l1_ready[s], 1)
                for s in S:
                    dve.wait_ge(l1_ready[s], i + 1)
                    c.settle()
                    alone(dve, waits_passed)
                    dve.tensor_copy(X[:, bass.ds((i * STREAMS + s) * TILES, TILES), :], ys_t[s])\
                       .then_inc(x_kept[s], 1)
                for h in range(2):
                    for s in S:
                        dve.wait_ge(up2_done[s], 2 * i + h + 1)
                        for m in range(2):
                            ins = dve.bn_stats(bn_stats1[:, 2 * h + m, bass.ds((i * STREAMS + s) * 6, 6)],
                                               feature_major(s, h)[:, m, :])
                            ins.then_inc(up2_taken[s], 1)
            c.end()
            for s in S:
                dve.wait_ge(up2_taken[s], 4 * TURNS + 4)
            e = Chain(dve, bn_steps)
            fold_batch_norm(dve, e, bn_stats1, bn1_col, bn1_ss, MB, bn1_var, bn1_pow, False)

        @block.tensor
        def _(pe):
            pe.wait_ge(l2_loaded, 16)
            ahead(pe, h_turned)
            with pe.Fori(0, TURNS) as i:
                for s in S:
                    pe.wait_ge(hs_ready[s], i + 1)
                    pe.wait_ge(up2_taken[s], 4 * i + 4)
                    for n in range(TILES):
                        for k in range(KD):
                            mm = pe.transpose(token_major(s, 0)[:, n, k * P:(k + 1) * P],
                                              hs_f[s][:, k, n * P:(n + 1) * P], ident[:])
                    mm.then_inc(h_turned[s], 1)
                for s in S:
                    pe.wait_ge(l1_ready[s], i + 1)
                    for n in range(TILES):
                        for k in range(KD):
                            mm = pe.matmul(feature_major(s, 1)[:, k, n * P:(n + 1) * P],
                                           ys_t[s][:, n, k * P:(k + 1) * P], ahatT[:], start=True, stop=True)
                    mm.then_inc(g2_done[s], 1)
                for h in range(2):
                    for s in S:
                        pe.wait_ge(g2_ready[s], i + 1)
                        for m in range(2):
                            for k in range(KD):
                                mm = pe.matmul(feature_major(s, h)[:, m, :],
                                               L2W1[:, k, (2 * h + m) * P:(2 * h + m + 1) * P],
                                               Hflat[:, k, bass.ds((i * STREAMS + s) * GROUP, GROUP)],
                                               start=(k == 0), stop=(k == KD - 1))
                        mm.then_inc(up2_done[s], 1)

    end_phase()

    rT = [cb(MB, GROUP) for _ in S]
    up3_done, r_ready, dn2_done, out2_ready, st2_taken = (sems(n) for n in
                                                          ("up3_done", "r_ready", "dn2_done", "out2_ready",
                                                           "st2_taken"))
    bn_steps2 = psem("bn_steps2")
    bn2_var, bn2_pow = psem("bn2_var"), psem("bn2_pow")

    with nc.Block() as block:

        @block.gpsimd
        def _(pool):
            pool.wait_ge(bn2_var, 1)
            pool.tensor_tensor(bn_tmp[:, 2, 0:KD], bn_tmp[:, 1, 0:KD], minus_half[:, 0:KD], ALU.pow)\
                .then_inc(bn2_pow, 1)

        @block.scalar
        def _(act):
            ahead(act, out2_ready)
            with act.Fori(0, TURNS) as i:
                for h in range(2):
                    for s in S:
                        act.wait_ge(up3_done[s], 2 * i + h + 1)
                        for m in range(2):
                            b = 2 * h + m
                            ins = act.activation(rT[s][:, b, :], feature_major(s, h)[:, m, :], ACT.Relu,
                                                 bias=bn1_ss[:, 1, b:b + 1], scale=bn1_ss[:, 0, b:b + 1])
                        ins.then_inc(r_ready[s], 1)
                for s in S:
                    act.wait_ge(dn2_done[s], i + 1)
                    for m in range(KD):
                        ins = act.activation(Hflat[:, m, bass.ds((i * STREAMS + s) * GROUP, GROUP)],
                                             feature_major(s, 0)[:, m, :], ACT.Identity, bias=bn2_col[:, 0, m:m + 1])
                    ins.then_inc(out2_ready[s], 1)

        @block.vector
        def _(dve):
            with dve.Fori(0, TURNS) as i:
                for s in S:
                    dve.wait_ge(out2_ready[s], i + 2)
                    for m in range(KD):
                        ins = dve.bn_stats(bn_stats2[:, m, bass.ds((i * STREAMS + s) * 6, 6)],
                                           Hflat[:, m, bass.ds((i * STREAMS + s) * GROUP, GROUP)])
                        ins.then_inc(st2_taken[s], 1)
            for s in S:
                dve.wait_ge(st2_taken[s], KD * TURNS)
            e = Chain(dve, bn_steps2)
            fold_batch_norm(dve, e, bn_stats2, bn2_col, bn2_ss, KD, bn2_var, bn2_pow, True)

        @block.tensor
        def _(pe):
            pe.wait_ge(l3_loaded, 7 * 16)
            with pe.Fori(0, TURNS) as i:
                for h in range(2):
                    for s in S:
                        if h == 0:
                            pe.wait_ge(out2_ready[s], i + 1)
                        for m in range(2):
                            for k in range(KD):
                                mm = pe.matmul(feature_major(s, h)[:, m, :],
                                               L2W1[:, k, (2 * h + m) * P:(2 * h + m + 1) * P],
                                               Hflat[:, k, bass.ds((i * STREAMS + s) * GROUP, GROUP)],
                                               start=(k == 0), stop=(k == KD - 1))
                        mm.then_inc(up3_done[s], 1)
                for s in S:
                    pe.wait_ge(r_ready[s], 2 * i + 2)
                    for m in range(KD):
                        for k in range(MB):
                            mm = pe.matmul(feature_major(s, 0)[:, m, :], L2W2[:, k, m * P:(m + 1) * P],
                                           rT[s][:, k, :], start=(k == 0), stop=(k == MB - 1))
                    mm.then_inc(dn2_done[s], 1)

    end_phase()

    db = region(arena[:, 0:SLOT_A], SLOT_A)
    x3, xT3 = ([db(G2) for _ in S] for _ in range(2))
    qk3 = [db(2, GROUP) for _ in S]
    v3 = [db(TILES, ATT3) for _ in S]
    at3 = [db(TILES, NODES) for _ in S]
    bd3 = [db(TILES, P) for _ in S]
    atT3 = [db(TILES, P) for _ in S]
    o3 = [db(TILES, ATT3) for _ in S]
    hs3 = qk3
    x3_t = [v.rearrange("p (t d) -> p t d", t=TILES) for v in x3]
    xT3_f = [v.rearrange("p (k n) -> p k n", k=KD) for v in xT3]
    rf_t = [qk3[s].rearrange("p a n -> p (a n)").rearrange("p (t d) -> p t d", t=TILES) for s in S]
    y3_t = [v.rearrange("p (t d) -> p t d", t=TILES) for v in xT3]
    names9 = ("hn", "ht", "var9", "rstd9", "x3r", "xt", "xTr", "qkd", "qkr", "vd", "vr", "scd", "scr", "exr",
              "att", "atr", "od", "orr", "ott", "otr", "wod", "rfr", "chd", "y3r", "stored")
    (hn_ready, h9_turned, var9, rstd9, x3_ready, x3_turned, xT3_ready, qk_done, qk_ready, v3_done, v3_ready,
     sc3_done, sc3_ready, exp3_ready, at3_turned, at3_ready, o3_done, o3_ready, o3_turned, o3T_ready, wo3_done,
     rf_ready, child_done, y3_ready, stored) = (sems("l3_" + n) for n in names9)
    p9_steps = psem("p9_steps")
    pool9 = psem("pool9")
    bd3_zero = psem("bd3_zero")
    out_t = out_rows.rearrange("(g t p) d -> g p t d", p=P, t=TILES)

    def bankB(s):
        return half(s, 1)

    with nc.Block() as block:

        @block.sync
        def _(sp):
            ahead(sp, stored, by=16)
            with sp.Fori(0, TURNS) as i:
                for s in S:
                    sp.wait_ge(y3_ready[s], i + 2)
                    sp.dma_start(out_t[bass.ds(i * STREAMS + s, 1)].rearrange("g p t d -> (g p) t d"), y3_t[s])\
                      .then_inc(stored[s], 16)
            for s in S:
                sp.wait_ge(stored[s], 16 * TURNS + 16)

        @block.gpsimd
        def _(pool):
            for s in S:
                pool.memset(bd3[s], 0.0).then_inc(bd3_zero, 1)
            with pool.Fori(0, TURNS) as i:
                for ln in range(2):
                    for s in S:
                        pool.wait_ge(var9[s], 2 * i + ln + 1)
                        pool.tensor_tensor(ln_veps[:, s, :], ln_mv[:, s, :, 1], eps_tile[:, 0:TILES], ALU.add)\
                            .then_inc(pool9, 1)
                        pool.wait_ge(pool9, i * (2 * STREAMS) + ln * STREAMS + s + 1)
                        pool.tensor_tensor(ln_rstd[:, s, :], ln_veps[:, s, :], minus_half[:, 0:TILES], ALU.pow)\
                            .then_inc(rstd9[s], 1)

        @block.scalar
        def _(act):
            act.wait_ge(bd3_zero, STREAMS)
            with act.Fori(0, TURNS) as i:
                for s in S:
                    act.wait_ge(rf_ready[s], i + 1)
                    act.wait_ge(y3_ready[s], i + 1)
                    for m in range(KD):
                        ins = act.activation(hs3[s][:, m, :], Hflat[:, m, bass.ds((i * STREAMS + s) * GROUP, GROUP)],
                                             ACT.Identity, bias=bn2_ss[:, 1, m:m + 1], scale=bn2_ss[:, 0, m:m + 1])
                    ins.then_inc(hn_ready[s], 1)
                for s in S:
                    act.wait_ge(x3_turned[s], i + 1)
                    act.wait_ge(stored[s], 16 * i + 16)
                    act.activation(xT3_f[s], feature_major(s, 1), ACT.Copy).then_inc(xT3_ready[s], 1)
                for s in S:
                    act.wait_ge(qk_done[s], i + 1)
                    for m in range(2):
                        ins = act.activation(qk3[s][:, m, :], feature_major(s, 0)[:, m, :], ACT.Identity,
                                             bias=qk3_bias[:, m:m + 1])
                    ins.then_inc(qk_ready[s], 1)
                for s in S:
                    act.wait_ge(sc3_ready[s], i + 1)
                    for b in range(2):
                        r = slice(NODES * b, NODES * (b + 1))
                        ins = act.activation(bd3[s][r, :, r], at3[s][r], ACT.Exp)
                    ins.then_inc(exp3_ready[s], 1)
                for s in S:
                    act.wait_ge(at3_turned[s], i + 1)
                    act.activation(atT3[s], token_major(s, 0, P), ACT.Copy).then_inc(at3_ready[s], 1)
                for s in S:
                    act.wait_ge(o3_turned[s], i + 1)
                    act.activation(atT3[s], token_major(s, 0, P), ACT.Copy).then_inc(o3T_ready[s], 1)

        @block.vector
        def _(dve):
            ahead(dve, rf_ready, y3_ready)
            c = Chain(dve, p9_steps, STREAMS * (1 + (2 * TILES - 1) + 4 + 2 + 1 + 3 + (2 * TILES - 1)))
            with dve.Fori(0, TURNS) as i:
                c.turn(i)
                for s in S:
                    dve.wait_ge(h9_turned[s], i + 1)
                    c.step(dve.tensor_tensor(x3_t[s], token_major(s, 0),
                                             X[:, bass.ds((i * STREAMS + s) * TILES, TILES), :], ALU.add))
                    c.settle()
                    ln_statistics(dve, c, x3_t[s], s, var9[s])
                for s in S:
                    dve.wait_ge(rstd9[s], 2 * i + 1)
                    for n in range(TILES):
                        ins = dve.tensor_scalar(x3_t[s][:, n, :], x3_t[s][:, n, :], ln_mv[:, s, n, 0:1],
                                                ln_rstd[:, s, n:n + 1], ALU.subtract, ALU.mult)
                    ins.then_inc(x3_ready[s], 1)
                for s in S:
                    dve.wait_ge(v3_done[s], i + 1)
                    dve.tensor_tensor(v3[s], token_major(s, 1, ATT3), over_tiles(bv3, ATT3), ALU.add)\
                       .then_inc(v3_ready[s], 1)
                for s in S:
                    dve.wait_ge(sc3_done[s], i + 1)
                    full = [P, TILES, NODES]

                    def spread(v):
                        return v.unsqueeze(1).to_broadcast(full)

                    c.step(dve.scalar_tensor_tensor(out=at3[s], in0=token_major(s, 0, NODES), scalar=float(ATT3) ** -0.5,
                                                    in1=spread(alpha_adj[:]), op0=ALU.mult, op1=ALU.add))
                    c.settle()
                    c.step(dve.tensor_tensor(at3[s], at3[s], spread(nz_mask[:]), ALU.mult))
                    c.settle()
                    c.step(dve.tensor_tensor(at3[s], at3[s], spread(nz_neg[:]), ALU.add))
                    c.settle()
                    c.step(dve.tensor_reduce(sm_max[:, s, 0:TILES], at3[s], AX_X, ALU.max))
                    c.settle()
                    dve.tensor_tensor(at3[s], at3[s], sm_max[:, s, 0:TILES].unsqueeze(2).to_broadcast(full),
                                      ALU.subtract).then_inc(sc3_ready[s], 1)
                for s in S:
                    dve.wait_ge(exp3_ready[s], i + 1)
                    c.step(dve.tensor_reduce(sm_sum[:, s, 0:TILES], bd3[s], AX_X, ALU.add))
                    c.settle()
                    c.step(dve.reciprocal(sm_inv[:, s, 0:TILES], sm_sum[:, s, 0:TILES]))
                for s in S:
                    dve.wait_ge(o3_done[s], i + 1)
                    c.settle()
                    dve.tensor_tensor(o3[s], token_major(s, 1, ATT3),
                                      sm_inv[:, s, 0:TILES].unsqueeze(2).to_broadcast([P, TILES, ATT3]), ALU.mult)\
                       .then_inc(o3_ready[s], 1)
                for s in S:
                    dve.wait_ge(wo3_done[s], i + 1)
                    c.step(dve.tensor_tensor(rf_t[s], token_major(s, 1), over_tiles(bo3), ALU.add))
                    c.settle()
                    dve.tensor_tensor(rf_t[s], rf_t[s], x3_t[s], ALU.add).then_inc(rf_ready[s], 1)
                for s in S:
                    dve.wait_ge(child_done[s], i + 1)
                    c.step(dve.tensor_tensor(y3_t[s], token_major(s, 0), rf_t[s], ALU.subtract))
                    c.settle()
                    c.step(dve.scalar_tensor_tensor(out=y3_t[s], in0=y3_t[s], scalar=parent_gamma[:, 0:1],
                                                    in1=rf_t[s], op0=ALU.mult, op1=ALU.add))
                    c.settle()
                    c.step(dve.tensor_tensor(y3_t[s], y3_t[s], x3_t[s], ALU.add))
                    c.settle()
                    ln_statistics(dve, c, y3_t[s], s, var9[s])
                for s in S:
                    dve.wait_ge(rstd9[s], 2 * i + 2)
                    for n in range(TILES):
                        ins = dve.tensor_scalar(y3_t[s][:, n, :], y3_t[s][:, n, :], ln_mv[:, s, n, 0:1],
                                                ln_rstd[:, s, n:n + 1], ALU.subtract, ALU.mult)
                    ins.then_inc(y3_ready[s], 1)
            c.end()

        @block.tensor
        def _(pe):
            with pe.Fori(0, TURNS) as i:
                for s in S:
                    pe.wait_ge(hn_ready[s], i + 1)
                    pe.wait_ge(y3_ready[s], i + 1)
                    for n in range(TILES):
                        for k in range(KD):
                            mm = pe.transpose(token_major(s, 0)[:, n, k * P:(k + 1) * P],
                                              hs3[s][:, k, n * P:(n + 1) * P], ident[:])
                    mm.then_inc(h9_turned[s], 1)
                for s in S:
                    pe.wait_ge(x3_ready[s], i + 1)
                    for n in range(TILES):
                        for k in range(KD):
                            mm = pe.transpose(feature_major(s, 1)[:, k, n * P:(n + 1) * P],
                                              x3_t[s][:, n, k * P:(k + 1) * P], ident[:])
                    mm.then_inc(x3_turned[s], 1)
                for s in S:
                    pe.wait_ge(xT3_ready[s], i + 1)
                    for m, w in enumerate((Wq3, Wk3)):
                        for k in range(KD):
                            mm = pe.matmul(feature_major(s, 0)[:, m, :], w[:, k, :], xT3_f[s][:, k, :],
                                           start=(k == 0), stop=(k == KD - 1))
                    mm.then_inc(qk_done[s], 1)
                for s in S:
                    for n in range(TILES):
                        for k in range(KD):
                            mm = pe.matmul(token_major(s, 1, ATT3)[:, n, :], xT3_f[s][:, k, n * P:(n + 1) * P],
                                           Wv3[:, k, :], start=(k == 0), stop=(k == KD - 1))
                    mm.then_inc(v3_done[s], 1)
                for s in S:
                    pe.wait_ge(qk_ready[s], i + 1)
                    alone(pe, waits_passed)
                    for n in range(TILES):
                        for b in range(2):
                            q = slice(n * P + NODES * b, n * P + NODES * (b + 1))
                            mm = pe.matmul(token_major(s, 0, NODES)[NODES * b:NODES * (b + 1), n, :],
                                           qk3[s][:, 0, q], qk3[s][:, 1, q], start=True, stop=True)
                    mm.then_inc(sc3_done[s], 1)
                for s in S:
                    pe.wait_ge(exp3_ready[s], i + 1)
                    for n in range(TILES):
                        mm = pe.transpose(token_major(s, 0, P)[:, n, :], bd3[s][:, n, :], ident[:])
                    mm.then_inc(at3_turned[s], 1)
                for s in S:
                    pe.wait_ge(at3_ready[s], i + 1)
                    pe.wait_ge(v3_ready[s], i + 1)
                    for n in range(TILES):
                        mm = pe.matmul(token_major(s, 1, ATT3)[:, n, :], atT3[s][:, n, :], v3[s][:, n, :],
                                       start=True, stop=True)
                    mm.then_inc(o3_done[s], 1)
                for s in S:
                    pe.wait_ge(o3_ready[s], i + 1)
                    for n in range(TILES):
                        mm = pe.transpose(token_major(s, 0, P)[:, n, :], o3[s][:, n, :], ident[:])
                    mm.then_inc(o3_turned[s], 1)
                for s in S:
                    pe.wait_ge(o3T_ready[s], i + 1)
                    for n in range(TILES):
                        mm = pe.matmul(token_major(s, 1)[:, n, :], atT3[s][:, n, :], Wo3[:], start=True, stop=True)
                    mm.then_inc(wo3_done[s], 1)
                for s in S:
                    pe.wait_ge(rf_ready[s], i + 2)
                    for n in range(TILES):
                        mm = pe.matmul(token_major(s, 0)[:, n, :], adjT[:], rf_t[s][:, n, :], start=True, stop=True)
                    mm.then_inc(child_done[s], 1)


def kernel(**inputs):
    import numpy as np
    import concourse.bacc as bacc
    from concourse.bass_utils import run_bass_kernel_spmd

    a = {k: np.asarray(v) for k, v in inputs.items()}

    def split_rows(w):
        return w.reshape(-1, 128, w.shape[-1]).transpose(1, 0, 2)

    def columns(v):
        return v.reshape(-1, 128).T

    lay = {"x": a["x"].reshape(-1, a["x"].shape[-1]), "adj": a["adj"], "adjT": a["adj"].T}
    for n in ("Wc", "Wq", "Wk", "Wv", "Wo", "W1", "W2"):
        lay[n] = split_rows(a["L0_gnn_" + n])
    for n in ("bc", "g1", "be1", "bo", "g2", "be2", "b2", "g3", "be3"):
        lay[n] = a["L0_gnn_" + n]
    lay["b1"] = columns(a["L0_gnn_b1"])
    lay["Wg0"], lay["Wg1"] = split_rows(a["L1_gnn_Wg0"]), split_rows(a["L1_gnn_Wg1"])
    lay["bg0"], lay["bg1"] = columns(a["L1_gnn_bg0"]), a["L1_gnn_bg1"]
    lay["wih"] = np.stack([split_rows(w.T) for w in a["L1_gnn_Wih"]])
    lay["whh"] = np.stack([split_rows(w.T) for w in a["L1_gnn_Whh"]])
    lay["lstm_bih"] = a["L1_gnn_bih"].reshape(4, 8, 128).transpose(2, 0, 1)
    lay["lstm_bhh"] = a["L1_gnn_bhh"].reshape(4, 8, 128).transpose(2, 0, 1)
    lay["L2W1"], lay["L2W2"] = split_rows(a["L2_gnn_W1"].T), split_rows(a["L2_gnn_W2"].T)
    lay["bn1"] = np.stack([columns(a["L2_gnn_" + n]) for n in ("b1", "g1", "be1")], 1)
    lay["bn2"] = np.stack([columns(a["L2_gnn_" + n]) for n in ("b2", "g2", "be2")], 1)
    for n in ("Wq", "Wk", "Wv"):
        lay[n + "3"] = split_rows(a["L3_gnn_" + n])
    lay["Wo3"] = a["L3_gnn_Wo"]
    lay["qk3b"] = np.stack([a["L3_gnn_bq"], a["L3_gnn_bk"]], 1)
    lay["bv3"], lay["bo3"] = a["L3_gnn_bv"], a["L3_gnn_bo"]
    lay["alpha"], lay["gamma"] = a["L3_gnn_alpha"].reshape(1), a["L3_gnn_gamma"].reshape(1)

    nc = bacc.Bacc("TRN2", target_bir_lowering=False, num_devices=1)
    arrays, dram = {}, {}
    for n, v in lay.items():
        v = np.ascontiguousarray(v)
        arrays["in_" + n] = v
        dram[n] = nc.dram_tensor("in_" + n, v.shape, mybir.dt.from_np(v.dtype), kind="ExternalInput").ap()
    out = nc.dram_tensor("out_0", a["x"].shape, F32, kind="ExternalOutput").ap()
    build_stack(nc, dram, out)
    return run_bass_kernel_spmd(nc, [arrays], core_ids=[0]).results[0]["out_0"]
```

```python
from contextlib import ExitStack

import concourse.bass as bass
from concourse import mybir

ALU = mybir.AluOpType
ACT = mybir.ActivationFunctionType
F32 = mybir.dt.float32
F32R = mybir.dt.float32r
AX_X = mybir.AxisListType.X

P = 128
BATCH, NODES, D = 128, 64, 256
TOKENS = BATCH * NODES
KD = D // P
HEADS = 4
HEAD_DIM = D // HEADS
HID0 = 2 * D
HID2 = 2 * D
ATT3 = 128
MAX_SKIP = 4
GATES = 4
EPS = 1e-5
NEG = 1e9
SQUARINGS = 24
RUN = 4

GROUP = 256
STREAMS = 4
TILES = GROUP // P
TURNS = TOKENS // GROUP // STREAMS
BANKS = 8 // STREAMS
HALF = BANKS // 2


def alone(eng, waits_passed):
    eng.sem_inc(waits_passed, 1)


def ahead(eng, *lists, by=1):
    for group in lists:
        for s in group:
            eng.sem_inc(s, by)


class Chain:

    def __init__(self, eng, sem, per_turn=0):
        self.eng, self.sem, self.per_turn = eng, sem, per_turn
        self.base, self.n = 0, 0

    def turn(self, i):
        assert self.n in (0, self.per_turn), (self.n, self.per_turn)
        self.base, self.n = i * self.per_turn, 0

    def at(self, i, n):
        self.base, self.n = i * self.per_turn, n

    def step(self, ins):
        ins.then_inc(self.sem, 1)
        self.n += 1

    def settle(self):
        self.eng.wait_ge(self.sem, self.base + self.n)

    def end(self):
        assert self.n == self.per_turn, (self.n, self.per_turn)


def weave(eng, turns, plan, part, stage):
    period, lead = plan["period"], plan["lead"]
    slots_at = [[slot for slot, tick in plan[part].items() if tick == at] for at in range(period)]

    def visit(first, last, turn_of):
        for at in range(first, last):
            for s in range(STREAMS):
                turn = turn_of((at + lead[s]) // period)
                for slot in slots_at[(at + lead[s]) % period] if turn is not None else ():
                    stage(s, slot, turn)

    visit(-lead[-1], 0, lambda n: 0 if n == 0 else None)
    with eng.Fori(0, turns - 1) as i:
        visit(0, period, lambda n: i + n)
    visit(0, period, lambda n: turns - 1 if n == 0 else None)


def build_stack(nc, t, out):
    with ExitStack() as ctx:
        build_program(nc, ctx, t, out.rearrange("b n d -> (b n) d"))


def build_program(nc, ctx, t, out_rows):
    def sb(name, shape):
        return ctx.enter_context(nc.sbuf_tensor(name, shape, F32))

    def sem(name):
        return ctx.enter_context(nc.semaphore(name))

    phase_sems = []

    def psem(name):
        phase_sems.append(nc.alloc_semaphore(name))
        return phase_sems[-1]

    def sems(name, n=STREAMS):
        return [psem(f"{name}{s}") for s in range(n)]

    def end_phase():
        nc.clear_and_free_semaphores(list(phase_sems))
        phase_sems.clear()
        nc.all_engine_barrier()

    H = sb("H", [P, KD, BATCH, NODES])
    H2 = sb("H2", [P, KD, BATCH, NODES])
    Hflat = H[:].rearrange("p k b n -> p k (b n)")
    H2flat = H2[:].rearrange("p k b n -> p k (b n)")
    R_WORDS, ARENA = 12288, 6400
    R = ctx.enter_context(nc.sbuf_tensor("R", [P, R_WORDS], F32R))
    arena = sb("arena", [P, ARENA])
    ps = ctx.enter_context(nc.psum_tensor("ps", [P, 8, 512], F32))
    state_rows = [nc.dram_tensor(f"residual{n}", (TOKENS, D), F32).ap() for n in range(2)]

    ident = sb("ident", [P, P])
    ones = sb("ones", [P, P])
    adjT = sb("adjT", [P, P])
    lnormT = sb("lnormT", [P, P])
    ahatT = sb("ahatT", [P, P])
    pos_mask = sb("pos_mask", [P, NODES])
    pos_neg = sb("pos_neg", [P, NODES])
    nz_mask = sb("nz_mask", [P, NODES])
    nz_neg = sb("nz_neg", [P, NODES])
    alpha_adj = sb("alpha_adj", [P, NODES])
    parent_gamma = sb("parent_gamma", [P, 1])
    bg0_rows = sb("bg0_rows", [P, KD, NODES])
    lstm_bias = sb("lstm_bias", [P, MAX_SKIP, 2 * GATES])
    b1_col = sb("b1_col", [P, HID0 // P])
    MB = HID2 // P
    bn1_col = sb("bn1_col", [P, 3, MB])
    bn2_col = sb("bn2_col", [P, 3, KD])
    qk3_bias = sb("qk3_bias", [P, 2])
    bv3_col = sb("bv3_col", [P, 1])
    rest_gamma = sb("rest_gamma", [P, 1])
    scal = sb("scal", [P, 2])
    bn1_ss = sb("bn1_ss", [P, 2, MB])
    bn2_ss = sb("bn2_ss", [P, 2, KD])
    minus_half = sb("minus_half", [P, 16])
    eps_tile = sb("eps_tile", [P, TILES])
    bn_mv = sb("bn_mv", [P, MB, 2])
    bn_tmp = sb("bn_tmp", [P, 3, MB])
    ln_stats = sb("ln_stats", [P, STREAMS, TILES, 6])
    ln_mv = sb("ln_mv", [P, STREAMS, TILES, 2])
    ln_veps = sb("ln_veps", [P, STREAMS, TILES])
    ln_rstd = sb("ln_rstd", [P, STREAMS, TILES])
    NJ = 2 * TILES
    sm_max = sb("sm_max", [P, STREAMS, 2 * NJ])
    sm_sum = sb("sm_sum", [P, STREAMS, 2 * NJ])
    sm_inv = sb("sm_inv", [P, STREAMS, 2 * NJ])

    def region(*pieces):
        at = [0] * len(pieces)

        def take(*dims):
            n = 1
            for x in dims:
                n *= x
            for q, base in enumerate(pieces):
                if at[q] + n <= base.shape[1]:
                    v = base[:, at[q]:at[q] + n]
                    at[q] += n
                    if len(dims) == 2:
                        v = v.rearrange("p (a b) -> p a b", a=dims[0])
                    if len(dims) == 3:
                        v = v.rearrange("p (a b c) -> p a b c", a=dims[0], b=dims[1])
                    if len(dims) == 4:
                        v = v.rearrange("p (a b c d) -> p a b c d", a=dims[0], b=dims[1], c=dims[2])
                    return v
            raise AssertionError((dims, at))

        return take

    H_words = H[:].rearrange("p k b n -> p (k b n)")
    H2_words = H2[:].rearrange("p k b n -> p (k b n)")
    G2 = KD * GROUP

    W0_WORDS = KD * D * 5 + KD * HID0 + (HID0 // P) * D + 9 * D
    w0 = region(H2_words[:, KD * TOKENS - W0_WORDS:])
    Wc, Wq, Wk, Wv, Wo = (w0(KD, D) for _ in range(5))
    W1 = w0(KD, HID0)
    W2 = w0(HID0 // P, D)
    vec0 = w0(9, D)
    bc, g1, be1, bo, g2, be2, b2, g3, be3 = (vec0[:, n, :] for n in range(9))
    wg = region(arena[:])
    gcn_raw = wg(2, KD, D)
    bg1 = wg(D)

    st = region(H2_words[:, 2 * 4096:])
    lstm_stage = [[st(KD, GATES * D), st(KD, GATES * D)] for _ in range(2)]
    l2r = region(H2_words[:, 2 * 4096:])
    l2_raw = [l2r(KD, HID2), l2r(MB, D)]
    w3 = region(arena[:])
    Wq3, Wk3, Wv3 = w3(KD, ATT3), w3(KD, ATT3), w3(KD, ATT3)
    Wo3 = w3(D)
    bo3 = w3(D)
    W3_WORDS = 3 * KD * ATT3 + 2 * D

    def tiles_of(v):
        return v.rearrange("p (t d) -> p t d", t=TILES)

    def blocks_of(v):
        return v.rearrange("p (k n) -> p k n", k=KD)

    def half(s, h):
        b = BANKS * s + HALF * h
        return ps[:, b:b + HALF, :].rearrange("p b w -> p (b w)")

    def token_major(s, h, width=D):
        return half(s, h)[:, 0:TILES * width].rearrange("p (t d) -> p t d", t=TILES)

    def feature_major(s, h):
        return blocks_of(half(s, h))

    def squares(s):
        return ps[:, BANKS * s:BANKS * (s + 1), :].rearrange("p b (c n) -> p (b c) n", n=P)

    def over_tiles(v, width=D):
        return v.unsqueeze(1).to_broadcast([P, TILES, width])

    def group_rows(dram):
        return dram.rearrange("(g t p) d -> g p t d", p=P, t=TILES)

    def rows_of_group(view, s, turn):
        return view[bass.ds(turn * STREAMS + s, 1)].rearrange("g p t d -> (g p) t d")

    def columns_of(state, s, turn):
        return state[:, :, bass.ds((turn * STREAMS + s) * GROUP, GROUP)]

    x_rows, out_view = group_rows(t["x"]), group_rows(out_rows)
    state0, state1 = (group_rows(v) for v in state_rows)
    S = range(STREAMS)

    def raw(v):
        return v.bitcast(F32)

    PASSES = ((0, 0), (1, 0), (0, 1))

    def exact_mm(pe, out, lhsT, rhs, start, stop):
        for n, (a, b) in enumerate(PASSES):
            mm = pe.matmul(out, lhsT(a), rhs(b), start=start and n == 0, stop=stop and n == len(PASSES) - 1)
        return mm

    waits_passed = sem("waits_passed")
    small_loaded = sem("small_loaded")
    w0_loaded = sem("w0_loaded")
    gcn_loaded = sem("gcn_loaded")
    lstm_loaded = [sem(f"lstm_loaded{p}") for p in range(MAX_SKIP)]
    l2_loaded = sem("l2_loaded")
    l3_loaded = sem("l3_loaded")

    def rows(name):
        return t[name].partition_broadcast(P)

    LN_STATS = 2 * TILES - 1

    def ln_statistics(dve, c, y, s, ready):
        for n in range(TILES):
            c.step(dve.bn_stats(ln_stats[:, s, n, :], y[:, n, :]))
        c.settle()
        alone(dve, waits_passed)
        for n in range(TILES):
            ins = dve.bn_aggr(ln_mv[:, s, n, :], ln_stats[:, s, n, :])
            if n < TILES - 1:
                c.step(ins)
        ins.then_inc(ready, 1)

    def ln_reciprocal(pool, c, s, ready, rstd, count):
        pool.wait_ge(ready, count)
        c.step(pool.tensor_tensor(ln_veps[:, s, :], ln_mv[:, s, :, 1], eps_tile[:, 0:TILES], ALU.add))
        c.settle()
        pool.tensor_tensor(ln_rstd[:, s, :], ln_veps[:, s, :], minus_half[:, 0:TILES], ALU.pow).then_inc(rstd, 1)

    LN_AFFINE = 2 * TILES

    def ln_affine(dve, c, y, s, g, be, ready, rstd, count):
        dve.wait_ge(ready, count)
        for n in range(TILES):
            c.step(dve.scalar_tensor_tensor(out=y[:, n, :], in0=y[:, n, :], scalar=ln_mv[:, s, n, 0:1], in1=g,
                                            op0=ALU.subtract, op1=ALU.mult))
        c.settle()
        dve.wait_ge(rstd, count)
        for n in range(TILES):
            ins = dve.scalar_tensor_tensor(out=y[:, n, :], in0=y[:, n, :], scalar=ln_rstd[:, s, n:n + 1], in1=be,
                                           op0=ALU.mult, op1=ALU.add)
            if n < TILES - 1:
                c.step(ins)
        return ins

    def ln_plain(dve, y, s, rstd, count):
        dve.wait_ge(rstd, count)
        for n in range(TILES):
            ins = dve.tensor_scalar(y[:, n, :], y[:, n, :], ln_mv[:, s, n, 0:1], ln_rstd[:, s, n:n + 1],
                                    ALU.subtract, ALU.mult)
        return ins

    class Steps:

        def __init__(self, eng, name, per_slot):
            self.per_slot = per_slot
            total = sum(per_slot.values())
            self.chains = [Chain(eng, x, total) for x in sems(name)]

        def enter(self, s, slot, turn):
            c = self.chains[s]
            c.at(turn, sum(n for k, n in self.per_slot.items() if k < slot))
            return c

        def leave(self, s, slot):
            c = self.chains[s]
            want = sum(n for k, n in self.per_slot.items() if k <= slot)
            assert c.n == want, (slot, c.n, want)

    sq = region(H_words)
    adj_bd = sq(P)
    adj2 = sq(NODES)
    lstm_b2 = sq(2, MAX_SKIP, 2 * GATES)
    col = sq(16)
    S64, P64, M64, eye_s = (sq(NODES) for _ in range(4))
    abd, abdT, diag, ddinv = sq(P), sq(P), sq(P), sq(P)
    big = sq(P)

    def ps0(b):
        return ps[:, b, :]

    zeroed = psem("zeroed")
    small_steps = psem("small_steps")
    small_mm = psem("small_mm")
    pool_made = psem("pool_made")
    adj_loaded = psem("adj_loaded")
    deg_ready = psem("deg_ready")
    sq_ready = psem("sq_ready")
    tr_ready = psem("tr_ready")
    sq_steps = psem("sq_steps")
    p_ready = psem("p_ready")
    squared = psem("squared")
    q_ready = psem("q_ready")

    with nc.Block() as block:

        @block.sync
        def _(sp):
            sp.wait_ge(zeroed, 2)
            for g in range(2):
                r = slice(NODES * g, NODES * (g + 1))
                sp.dma_start(adjT[r, r], t["adjT"]).then_inc(adj_loaded, 16)
                sp.dma_start(adj_bd[r, r], t["adj"]).then_inc(adj_loaded, 16)
                sp.dma_start(adj2[r, :], t["adj"]).then_inc(adj_loaded, 16)
            for dst, name in ((lstm_b2[:, 0], "lstm_bih"), (lstm_b2[:, 1], "lstm_bhh"), (b1_col[:], "b1"),
                              (bn1_col[:], "bn1"), (bn2_col[:], "bn2"), (qk3_bias[:], "qk3b"), (col[:, 8:10], "bg0")):
                sp.dma_start(dst, t[name]).then_inc(small_loaded, 16)
            sp.dma_start(bv3_col[:], t["bv3"]).then_inc(small_loaded, 16)
            sp.dma_start(scal[:, 0:1], rows("alpha")).then_inc(small_loaded, 16)
            sp.dma_start(scal[:, 1:2], rows("gamma")).then_inc(small_loaded, 16)
            for dst, name in ((Wc, "Wc"), (Wq, "Wq"), (Wk, "Wk"), (Wv, "Wv"), (Wo, "Wo"), (W1, "W1"), (W2, "W2")):
                sp.dma_start(dst, t[name]).then_inc(w0_loaded, 16)
            for dst, name in ((bc, "bc"), (g1, "g1"), (be1, "be1"), (bo, "bo"), (g2, "g2"), (be2, "be2"),
                              (b2, "b2"), (g3, "g3"), (be3, "be3")):
                sp.dma_start(dst, rows(name)).then_inc(w0_loaded, 16)
            for dst, name in ((gcn_raw[:, 0], "Wg0"), (gcn_raw[:, 1], "Wg1")):
                sp.dma_start(dst, t[name]).then_inc(gcn_loaded, 16)
            sp.dma_start(bg1, rows("bg1")).then_inc(gcn_loaded, 16)

        @block.gpsimd
        def _(pool):
            pool.memset(adjT[:], 0.0).then_inc(zeroed, 1)
            pool.memset(adj_bd, 0.0).then_inc(zeroed, 1)
            pool.memset(ident[:], 0.0).then_inc(pool_made, 1)
            pool.memset(minus_half[:], -0.5).then_inc(pool_made, 1)
            pool.memset(eps_tile[:], EPS).then_inc(pool_made, 1)
            pool.wait_ge(pool_made, 3)
            pool.affine_select(out=ident[:], in_=ident[:], compare_op=ALU.not_equal, fill=1.0, base=0,
                               pattern=[[-1, P]], channel_multiplier=1).then_inc(pool_made, 1)
            pool.memset(ones[:], 1.0).then_inc(pool_made, 1)
            pool.wait_ge(deg_ready, 1)
            pool.tensor_tensor(col[:, 5:6], col[:, 4:5], minus_half[:, 0:1], ALU.pow).then_inc(pool_made, 1)

        @block.vector
        def _(dve):
            c = Chain(dve, small_steps)

            def link(ins):
                c.step(ins)
                c.settle()

            dve.wait_ge(adj_loaded, 96)
            dve.wait_ge(small_loaded, 10 * 16)
            dve.wait_ge(pool_made, 5)
            link(dve.tensor_scalar(pos_mask[:], adj2, 0.0, None, ALU.is_gt))
            link(dve.tensor_scalar(nz_mask[:], adj2, 0.0, None, ALU.not_equal))
            link(dve.tensor_scalar(pos_neg[:], pos_mask[:], NEG, -NEG, ALU.mult, ALU.add))
            link(dve.tensor_scalar(nz_neg[:], nz_mask[:], NEG, -NEG, ALU.mult, ALU.add))
            link(dve.tensor_scalar(alpha_adj[:], adj2, scal[:, 0:1], None, ALU.mult))
            link(dve.tensor_reduce(col[:, 0:1], adj2, AX_X, ALU.add))
            link(dve.tensor_scalar(parent_gamma[:], col[:, 0:1], 0.0, scal[:, 1:2], ALU.is_gt, ALU.mult))
            link(dve.tensor_scalar(rest_gamma[:], parent_gamma[:], -1.0, 1.0, ALU.mult, ALU.add))
            link(dve.tensor_tensor(lstm_bias[:], lstm_b2[:, 0], lstm_b2[:, 1], ALU.add))
            link(dve.tensor_tensor(abd, adj_bd, ident[:], ALU.add))
            link(dve.tensor_tensor(abdT, adjT[:], ident[:], ALU.add))
            link(dve.tensor_tensor(diag, abd, ident[:], ALU.mult))
            link(dve.tensor_reduce(col[:, 1:2], abd, AX_X, ALU.add))
            link(dve.tensor_reduce(col[:, 2:3], abdT, AX_X, ALU.add))
            link(dve.tensor_reduce(col[:, 3:4], diag, AX_X, ALU.add))
            link(dve.tensor_tensor(col[:, 4:5], col[:, 1:2], col[:, 2:3], ALU.add))
            dve.tensor_tensor(col[:, 4:5], col[:, 4:5], col[:, 3:4], ALU.subtract).then_inc(deg_ready, 1)
            dve.wait_ge(pool_made, 6)
            link(dve.tensor_scalar(abdT, abdT, col[:, 5:6], None, ALU.mult))
            link(dve.tensor_scalar(ddinv, ident[:], col[:, 5:6], None, ALU.mult))
            link(dve.tensor_scalar(big, ident[:], col[:, 0:1], None, ALU.mult))
            link(dve.tensor_tensor(S64[0:NODES], adj_bd[0:NODES, 0:NODES], adjT[0:NODES, 0:NODES], ALU.add))
            link(dve.tensor_scalar(S64[0:NODES], S64[0:NODES], 0.5, None, ALU.mult))
            dve.tensor_reduce(col[0:NODES, 6:7], S64[0:NODES], AX_X, ALU.add,
                              apply_absolute_value=True).then_inc(sq_ready, 1)
            dve.wait_ge(small_mm, 1)
            link(dve.tensor_tensor(ahatT[:], abdT, ps0(0)[:, 0:P], ALU.mult))
            for k in range(KD):
                link(dve.tensor_scalar(bg0_rows[:, k, :], ps0(0)[:, P:P + NODES], col[:, 8 + k:9 + k], None,
                                       ALU.mult))
            dve.wait_ge(small_mm, 2)
            dve.tensor_reduce(col[0:1, 7:8], ps0(1)[0:1, 0:NODES], AX_X, ALU.max).then_inc(sq_ready, 1)
            dve.wait_ge(small_mm, 3)
            link(dve.tensor_scalar(col[0:NODES, 10:11], ps0(2)[0:NODES, 0:1], 1e-30, None, ALU.max))
            link(dve.tensor_scalar(eye_s[0:NODES], ident[0:NODES, 0:NODES], col[0:NODES, 10:11], None, ALU.mult))
            link(dve.tensor_tensor(P64[0:NODES], S64[0:NODES], eye_s[0:NODES], ALU.add))
            link(dve.reciprocal(col[0:NODES, 11:12], col[0:NODES, 10:11]))
            dve.tensor_scalar(P64[0:NODES], P64[0:NODES], col[0:NODES, 11:12], None, ALU.mult).then_inc(p_ready, 1)
            ch = Chain(dve, sq_steps, 2)
            with dve.Fori(0, SQUARINGS // RUN) as i:
                ch.turn(i)
                for r in range(RUN):
                    if r == RUN - 1:
                        dve.wait_ge(p_ready, RUN * i + RUN)
                        ch.step(dve.tensor_tensor(M64[0:NODES], P64[0:NODES], P64[0:NODES], ALU.mult))
                        ch.settle()
                        dve.tensor_reduce(col[0:NODES, 12:13], M64[0:NODES], AX_X, ALU.add).then_inc(q_ready, 1)
                        dve.wait_ge(tr_ready, i + 1)
                        ch.step(dve.reciprocal(col[0:NODES, 13:14], ps0(4)[0:NODES, 0:1]))
                        ch.settle()
                    dve.wait_ge(squared, RUN * i + r + 1)
                    if r < RUN - 1:
                        dve.tensor_copy(P64[0:NODES], ps0(3)[0:NODES, 0:NODES]).then_inc(p_ready, 1)
                    else:
                        dve.tensor_scalar(P64[0:NODES], ps0(3)[0:NODES, 0:NODES], col[0:NODES, 13:14], None,
                                          ALU.mult).then_inc(p_ready, 1)
            ch.end()
            dve.wait_ge(p_ready, SQUARINGS + 1)
            link(dve.tensor_tensor(M64[0:NODES], P64[0:NODES], P64[0:NODES], ALU.mult))
            link(dve.tensor_reduce(col[0:NODES, 15:16], M64[0:NODES], AX_X, ALU.add))
            dve.wait_ge(small_mm, 4)
            link(dve.tensor_tensor(M64[0:NODES], P64[0:NODES], ps0(3)[0:NODES, 0:NODES], ALU.mult))
            dve.tensor_reduce(col[0:NODES, 14:15], M64[0:NODES], AX_X, ALU.add).then_inc(sq_ready, 1)
            dve.wait_ge(small_mm, 5)
            link(dve.reciprocal(col[:, 12:13], ps0(2)[:, 1:2]))
            link(dve.tensor_scalar(col[:, 13:14], ps0(2)[:, 0:1], col[:, 12:13], 1e-8, ALU.mult, ALU.add))
            link(dve.reciprocal(col[:, 12:13], col[:, 13:14]))
            link(dve.tensor_scalar(big, adjT[:], 2.0, col[:, 12:13], ALU.mult, ALU.mult))
            link(dve.tensor_tensor(lnormT[:], big, ident[:], ALU.subtract))

        @block.tensor
        def _(pe):
            pe.wait_ge(sq_ready, 1)
            pe.matmul(ps0(0)[:, 0:P], ones[:], ddinv, start=True, stop=True)
            pe.matmul(ps0(0)[:, P:2 * P], ones[:], big, start=True, stop=True).then_inc(small_mm, 1)
            pe.transpose(ps0(1)[0:1, 0:NODES], col[0:NODES, 6:7], ident[0:NODES, 0:NODES]).then_inc(small_mm, 1)
            pe.wait_ge(sq_ready, 2)
            pe.matmul(ps0(2)[0:NODES, 0:1], ones[0:1, 0:NODES], col[0:1, 7:8], start=True, stop=True)\
              .then_inc(small_mm, 1)
            with pe.Fori(0, SQUARINGS // RUN) as i:
                for r in range(RUN):
                    pe.wait_ge(p_ready, RUN * i + r + 1)
                    alone(pe, waits_passed)
                    pe.matmul(ps0(3)[0:NODES, 0:NODES], P64[0:NODES], P64[0:NODES], start=True, stop=True)\
                      .then_inc(squared, 1)
                pe.wait_ge(q_ready, i + 1)
                pe.matmul(ps0(4)[:, 0:1], ones[0:NODES, :], col[0:NODES, 12:13],
                          start=True, stop=True).then_inc(tr_ready, 1)
            pe.wait_ge(p_ready, SQUARINGS + 1)
            pe.matmul(ps0(3)[0:NODES, 0:NODES], S64[0:NODES], P64[0:NODES], start=True, stop=True)\
              .then_inc(small_mm, 1)
            pe.wait_ge(sq_ready, 3)
            pe.matmul(ps0(2)[:, 0:2], ones[0:NODES, :], col[0:NODES, 14:16], start=True, stop=True)\
              .then_inc(small_mm, 1)

    end_phase()

    buf = region(H_words, H2_words[:, 0:KD * TOKENS - W0_WORDS])
    xs, sc_words, hbuf, x1, vt, x1b, x2b = ([buf(G2) for _ in S] for _ in range(7))
    attn_bd = [buf(HEADS * TILES, P) for _ in S]
    attnT = [buf(HEADS * TILES, P) for _ in S]
    xs_t, hb_t, x1_t, v_t, x1b_t, x2b_t = ([tiles_of(v) for v in b] for b in (xs, hbuf, x1, vt, x1b, x2b))
    sc = [v.rearrange("p (j m) -> p j m", m=NODES) for v in sc_words]
    w0r = region(R[:])
    Wc_r, Wq_r, Wk_r, Wv_r, Wo_r = (w0r(2, KD, D) for _ in range(5))
    W1_r = w0r(2, KD, HID0)
    fm = [w0r(2, KD, GROUP) for _ in S]
    flat_at = [v.rearrange("p a b -> p (a b)") for v in attnT]
    qkT = [v.rearrange("p (q k n) -> p q k n", q=2, k=KD) for v in flat_at]
    mT = [v.rearrange("p (m n) -> p m n", m=HID0 // P) for v in flat_at]

    def up_ps(s):
        return ps[:, BANKS * s:BANKS * (s + 1), :].rearrange("p b w -> p (b w)").rearrange(
            "p (m n) -> p m n", m=HID0 // P)

    (xs_loaded, agg_done, h_done, var_ready, rstd_ready, x1_ready, x1b_ready, x1_turned, qk_done, qkT_ready,
     v_done, v_ready, sc_done, sc_ready, exp_ready, at_ready, at_turned, atT_ready, o_done, wo_done, x2_ready,
     x2b_ready, x2_turned, up_done, gelu_ready, down_done, y_made, yx_ready, y_ready, y_stored, fm_hi, fm_ready) = (sems(n) for n in
                  ("xs_loaded", "agg_done", "h_done", "var_ready", "rstd_ready", "x1_ready", "x1b_ready", "x1_turned",
                   "qk_done", "qkT_ready", "v_done", "v_ready", "sc_done", "sc_ready", "exp_ready", "at_ready",
                   "at_turned", "atT_ready", "o_done", "wo_done", "x2_ready", "x2b_ready", "x2_turned", "up_done",
                   "gelu_ready", "down_done", "y_made", "yx_ready", "y_ready", "y_stored", "fm_hi", "fm_ready"))
    w0_hi, w0_ready = psem("w0_hi"), psem("w0_ready")
    splits0 = ((Wc_r, Wc), (Wq_r, Wq), (Wk_r, Wk), (Wv_r, Wv), (Wo_r, Wo), (W1_r, W1))
    bd_zero = psem("bd_zero")
    FM = 4
    LN0 = 4
    plan0 = dict(
        period=96, lead=(0, 17, 45, 61),
        pe={0: 0, 1: 3, 3: 11, 4: 19, 5: 24, 6: 26, 9: 41, 10: 48, 11: 54, 13: 65, 14: 75, 15: 80},
        act={0: 3, 3: 12, 4: 21, 5: 24, 7: 36, 9: 46, 10: 51, 13: 69, 14: 77},
        dve={0: 3, 1: 6, 2: 10, 3: 16, 6: 30, 8: 38, 10: 51, 11: 61, 12: 65, 13: 71, 15: 85, 16: 88, 17: 91, 18: 93},
        pool={1: 7, 3: 23, 11: 65, 13: 70, 15: 85, 16: 90, 17: 93},
        sp={17: 93, 18: 93})

    with nc.Block() as block:

        @block.sync
        def _(sp):
            ahead(sp, y_stored, by=16)
            for s in S:
                sp.dma_start(xs_t[s], rows_of_group(x_rows, s, 0)).then_inc(xs_loaded[s], 16)

            def stage(s, slot, turn):
                if slot == 17:
                    if not (isinstance(turn, int) and turn == TURNS - 1):
                        sp.wait_ge(yx_ready[s], turn + 1)
                        sp.dma_start(xs_t[s], rows_of_group(x_rows, s, turn + 1)).then_inc(xs_loaded[s], 16)
                if slot == 18:
                    sp.wait_ge(y_ready[s], turn + 2)
                    sp.dma_start(rows_of_group(state0, s, turn), x1_t[s]).then_inc(y_stored[s], 16)

            weave(sp, TURNS, plan0, "sp", stage)
            for s in S:
                sp.wait_ge(y_stored[s], 16 * TURNS + 16)
            for s in S:
                sp.wait_ge(down_done[s], TURNS)
            sp.dma_start(lstm_stage[0][0], t["wih"][0]).then_inc(lstm_loaded[0], 16)

        @block.gpsimd
        def _(pool):
            for s in S:
                pool.memset(attn_bd[s], 0.0).then_inc(bd_zero, 1)
            steps = Steps(pool, "l0_pool", {1: 1, 11: 1, 15: 1, 17: 1})

            def stage(s, slot, turn):
                for n, at in enumerate((1, 11, 15, 17)):
                    if slot == at:
                        ln_reciprocal(pool, steps.enter(s, slot, turn), s, var_ready[s], rstd_ready[s],
                                      LN0 * turn + n + 1)
                if slot == 3:
                    pool.wait_ge(x1_ready[s], turn + 1)
                    pool.tensor_tensor(x1b_t[s], x1_t[s], over_tiles(bo), ALU.add).then_inc(x1b_ready[s], 1)
                if slot == 13:
                    pool.wait_ge(x2_ready[s], turn + 1)
                    pool.tensor_tensor(x2b_t[s], hb_t[s], over_tiles(b2), ALU.add).then_inc(x2b_ready[s], 1)
                if slot == 16:
                    pool.wait_ge(y_made[s], turn + 1)
                    pool.tensor_tensor(x1_t[s], x1_t[s], xs_t[s], ALU.add).then_inc(yx_ready[s], 1)

            weave(pool, TURNS, plan0, "pool", stage)

        @block.scalar
        def _(act):
            act.wait_ge(w0_loaded, 16 * 16)
            for split, w in splits0:
                act.activation(split[:, 0], w, ACT.Copy).then_inc(w0_hi, 1)

            def stage(s, slot, turn):
                if slot == 0:
                    act.wait_ge(agg_done[s], turn + 1)
                    act.activation(fm[s][:, 0], feature_major(s, 0), ACT.Copy).then_inc(fm_hi[s], 1)
                if slot == 3:
                    act.wait_ge(x1_turned[s], turn + 1)
                    act.activation(fm[s][:, 0], feature_major(s, 0), ACT.Copy).then_inc(fm_hi[s], 1)
                if slot == 4:
                    act.wait_ge(qk_done[s], turn + 1)
                    act.activation(qkT[s][:, 0], feature_major(s, 0), ACT.Copy, scale=float(HEAD_DIM) ** -0.5)
                    act.activation(qkT[s][:, 1], feature_major(s, 1), ACT.Copy).then_inc(qkT_ready[s], 1)
                if slot == 5:
                    act.wait_ge(v_done[s], turn + 1)
                    act.activation(v_t[s], token_major(s, 0), ACT.Copy).then_inc(v_ready[s], 1)
                if slot == 7:
                    act.wait_ge(sc_ready[s], turn + 1)
                    act.activation(sc[s], sc[s], ACT.Exp).then_inc(exp_ready[s], 1)
                if slot == 9:
                    act.wait_ge(at_turned[s], turn + 1)
                    act.activation(attnT[s], squares(s), ACT.Copy).then_inc(atT_ready[s], 1)
                if slot == 10:
                    act.wait_ge(o_done[s], turn + 1)
                    act.activation(fm[s][:, 0], feature_major(s, 1), ACT.Copy).then_inc(fm_hi[s], 1)
                if slot == 13:
                    act.wait_ge(x2_turned[s], turn + 1)
                    act.activation(fm[s][:, 0], feature_major(s, 1), ACT.Copy).then_inc(fm_hi[s], 1)
                if slot == 14:
                    act.wait_ge(up_done[s], turn + 1)
                    for m in range(HID0 // P):
                        ins = act.activation(mT[s][:, m, :], up_ps(s)[:, m, :], ACT.Gelu, bias=b1_col[:, m:m + 1])
                    ins.then_inc(gelu_ready[s], 1)

            weave(act, TURNS, plan0, "act", stage)

        @block.vector
        def _(dve):
            steps = Steps(dve, "l0_dve", {1: 1 + LN_STATS, 2: LN_AFFINE, 6: 5, 8: 2, 11: 1 + LN_STATS,
                                          12: LN_AFFINE - 1, 15: 1 + LN_STATS, 16: LN_AFFINE - 1,
                                          17: LN_STATS})
            for n, (split, w) in enumerate(splits0):
                dve.wait_ge(w0_hi, n + 1)
                dve.tensor_tensor(split[:, 1], w, raw(split[:, 0]), ALU.subtract).then_inc(w0_ready, 1)
            ahead(dve, y_ready)
            dve.wait_ge(w0_loaded, 16 * 16)
            dve.wait_ge(bd_zero, STREAMS)
            rows_b = [slice(NODES * b, NODES * (b + 1)) for b in range(2)]

            def split_lo(s, count, half):
                dve.wait_ge(fm_hi[s], count)
                dve.tensor_tensor(fm[s][:, 1], feature_major(s, half), raw(fm[s][:, 0]), ALU.subtract)\
                   .then_inc(fm_ready[s], 1)

            def stage(s, slot, turn):
                c = steps.enter(s, slot, turn)
                for n, (at, h) in enumerate(((0, 0), (3, 0), (10, 1), (13, 1))):
                    if slot == at:
                        split_lo(s, FM * turn + n + 1, h)
                if slot == 1:
                    dve.wait_ge(h_done[s], turn + 1)
                    c.step(dve.tensor_tensor(hb_t[s], token_major(s, 1), over_tiles(bc), ALU.add))
                    c.settle()
                    ln_statistics(dve, c, hb_t[s], s, var_ready[s])
                if slot == 2:
                    c.step(ln_affine(dve, c, hb_t[s], s, g1, be1, var_ready[s], rstd_ready[s], LN0 * turn + 1))
                    c.settle()
                    dve.wait_ge(y_stored[s], 16 * turn + 16)
                    dve.wait_ge(xs_loaded[s], 16 * turn + 16)
                    dve.scalar_tensor_tensor(out=x1_t[s], in0=hb_t[s], scalar=0.0, in1=xs_t[s],
                                             op0=ALU.max, op1=ALU.add).then_inc(x1_ready[s], 1)
                if slot == 6:
                    dve.wait_ge(sc_done[s], turn + 1)
                    full = [P, 2 * NJ, NODES]
                    for r in rows_b:
                        c.step(dve.tensor_tensor(sc[s][r], squares(s)[r, :, r],
                                                 pos_mask[r].unsqueeze(1).to_broadcast([NODES, 2 * NJ, NODES]),
                                                 ALU.mult))
                    c.settle()
                    c.step(dve.tensor_tensor(sc[s], sc[s], pos_neg[:].unsqueeze(1).to_broadcast(full), ALU.add))
                    c.settle()
                    c.step(dve.tensor_reduce(sm_max[:, s, :], sc[s], AX_X, ALU.max))
                    c.settle()
                    c.step(dve.tensor_tensor(sc[s], sc[s], sm_max[:, s, :].unsqueeze(2).to_broadcast(full),
                                             ALU.subtract))
                    c.settle()
                    dve.sem_inc(sc_ready[s], 1)
                if slot == 8:
                    dve.wait_ge(exp_ready[s], turn + 1)
                    c.step(dve.tensor_reduce(sm_sum[:, s, :], sc[s], AX_X, ALU.add))
                    c.settle()
                    c.step(dve.reciprocal(sm_inv[:, s, :], sm_sum[:, s, :]))
                    c.settle()
                    for r in rows_b:
                        dve.tensor_tensor(attn_bd[s][r, :, r], sc[s][r],
                                          sm_inv[r, s, :].unsqueeze(2).to_broadcast([NODES, 2 * NJ, NODES]),
                                          ALU.mult).then_inc(at_ready[s], 1)
                if slot == 11:
                    dve.wait_ge(wo_done[s], turn + 1)
                    dve.wait_ge(x1b_ready[s], turn + 1)
                    c.step(dve.tensor_tensor(hb_t[s], token_major(s, 0), x1b_t[s], ALU.add))
                    c.settle()
                    ln_statistics(dve, c, hb_t[s], s, var_ready[s])
                if slot == 12:
                    ln_affine(dve, c, hb_t[s], s, g2, be2, var_ready[s], rstd_ready[s], LN0 * turn + 2)\
                        .then_inc(x2_ready[s], 1)
                if slot == 15:
                    dve.wait_ge(down_done[s], turn + 1)
                    dve.wait_ge(x2b_ready[s], turn + 1)
                    c.step(dve.tensor_tensor(x1_t[s], token_major(s, 0), x2b_t[s], ALU.add))
                    c.settle()
                    ln_statistics(dve, c, x1_t[s], s, var_ready[s])
                if slot == 16:
                    ln_affine(dve, c, x1_t[s], s, g3, be3, var_ready[s], rstd_ready[s], LN0 * turn + 3)\
                        .then_inc(y_made[s], 1)
                if slot == 17:
                    dve.wait_ge(yx_ready[s], turn + 1)
                    ln_statistics(dve, c, x1_t[s], s, var_ready[s])
                if slot == 18:
                    ln_plain(dve, x1_t[s], s, rstd_ready[s], LN0 * turn + 4).then_inc(y_ready[s], 1)
                steps.leave(s, slot)

            weave(dve, TURNS, plan0, "dve", stage)

        @block.tensor
        def _(pe):
            pe.wait_ge(w0_ready, len(splits0))
            pe.wait_ge(w0_loaded, 16 * 16)

            def product(out, src, w):
                for n in range(TILES):
                    for k in range(KD):
                        mm = exact_mm(pe, out[:, n, :], lambda q: src[:, q, k, n * P:(n + 1) * P],
                                      lambda q: w[:, q, k, :], k == 0, k == KD - 1)
                return mm

            def product_T(out, w, src, blocks):
                for m in range(blocks):
                    for k in range(KD):
                        mm = exact_mm(pe, out[:, m, :], lambda q: w[:, q, k, m * P:(m + 1) * P],
                                      lambda q: src[:, q, k, :], k == 0, k == KD - 1)
                return mm

            def turn_over(out, src):
                for n in range(TILES):
                    for k in range(KD):
                        mm = pe.transpose(out[:, k, n * P:(n + 1) * P], src[:, n, k * P:(k + 1) * P], ident[:])
                return mm

            def stage(s, slot, turn):
                if slot == 0:
                    pe.wait_ge(xs_loaded[s], 16 * turn + 16)
                    pe.wait_ge(y_ready[s], turn + 1)
                    for n in range(TILES):
                        for k in range(KD):
                            mm = pe.matmul(feature_major(s, 0)[:, k, n * P:(n + 1) * P],
                                           xs_t[s][:, n, k * P:(k + 1) * P], lnormT[:], start=True, stop=True)
                    mm.then_inc(agg_done[s], 1)
                if slot == 1:
                    pe.wait_ge(fm_ready[s], FM * turn + 1)
                    product(token_major(s, 1), fm[s], Wc_r).then_inc(h_done[s], 1)
                if slot == 3:
                    pe.wait_ge(x1_ready[s], turn + 1)
                    turn_over(feature_major(s, 0), x1_t[s]).then_inc(x1_turned[s], 1)
                if slot == 4:
                    pe.wait_ge(fm_ready[s], FM * turn + 2)
                    product_T(feature_major(s, 0), Wq_r, fm[s], KD)
                    product_T(feature_major(s, 1), Wk_r, fm[s], KD).then_inc(qk_done[s], 1)
                if slot == 5:
                    pe.wait_ge(qkT_ready[s], turn + 1)
                    product(token_major(s, 0), fm[s], Wv_r).then_inc(v_done[s], 1)
                if slot == 6:
                    pe.wait_ge(v_ready[s], turn + 1)
                    for g in range(2):
                        f = slice(HEAD_DIM * g, HEAD_DIM * (g + 1))
                        for n in range(TILES):
                            for h2 in range(HEADS // 2):
                                q = slice(n * P, (n + 1) * P)
                                mm = pe.matmul(squares(s)[:, g * NJ + 2 * n + h2, :], qkT[s][f, 0, h2, q],
                                               qkT[s][f, 1, h2, q], start=True, stop=True)
                    mm.then_inc(sc_done[s], 1)
                if slot == 9:
                    pe.wait_ge(at_ready[s], 2 * turn + 2)
                    for j in range(HEADS * TILES):
                        mm = pe.transpose(squares(s)[:, j, :], attn_bd[s][:, j, :], ident[:])
                    mm.then_inc(at_turned[s], 1)
                if slot == 10:
                    pe.wait_ge(atT_ready[s], turn + 1)
                    for n in range(TILES):
                        for h in range(HEADS):
                            g, h2 = h % 2, h // 2
                            mm = pe.matmul(feature_major(s, 1)[HEAD_DIM * g:HEAD_DIM * (g + 1), h2,
                                                               n * P:(n + 1) * P],
                                           v_t[s][:, n, HEAD_DIM * h:HEAD_DIM * (h + 1)],
                                           attnT[s][:, g * NJ + 2 * n + h2, :], start=True, stop=True)
                    mm.then_inc(o_done[s], 1)
                if slot == 11:
                    pe.wait_ge(fm_ready[s], FM * turn + 3)
                    product(token_major(s, 0), fm[s], Wo_r).then_inc(wo_done[s], 1)
                if slot == 13:
                    pe.wait_ge(x2_ready[s], turn + 1)
                    turn_over(feature_major(s, 1), hb_t[s]).then_inc(x2_turned[s], 1)
                if slot == 14:
                    pe.wait_ge(fm_ready[s], FM * turn + 4)
                    product_T(up_ps(s), W1_r, fm[s], HID0 // P).then_inc(up_done[s], 1)
                if slot == 15:
                    pe.wait_ge(gelu_ready[s], turn + 1)
                    for n in range(TILES):
                        for k in range(HID0 // P):
                            mm = pe.matmul(token_major(s, 0)[:, n, :], mT[s][:, k, n * P:(n + 1) * P], W2[:, k, :],
                                           start=(k == 0), stop=(k == HID0 // P - 1))
                    mm.then_inc(down_done[s], 1)

            weave(pe, TURNS, plan0, "pe", stage)

    end_phase()

    gb = region(H2_words[:, 0:2 * 4096])
    xg, tg, ug = ([gb(G2) for _ in S] for _ in range(3))
    xg_t, ug_t = ([tiles_of(v) for v in b] for b in (xg, ug))
    tg_f = [blocks_of(v) for v in tg]
    gr = region(R[:])
    wg_r = gr(2, 2, KD, D)
    zg = [gr(2, KD, GROUP) for _ in S]
    h1 = [gr(2, KD, GROUP) for _ in S]
    (xg_loaded, ga_done, zg_hi, zg_ready, g0_done, tg_ready, h1_hi, h1_ready, g1_done, ug_ready, gb_done,
     gcn_ready) = (sems(n) for n in ("xg_loaded", "ga_done", "zg_hi", "zg_ready", "g0_done", "tg_ready", "h1_hi",
                                     "h1_ready", "g1_done", "ug_ready", "gb_done", "gcn_ready"))
    wg_hi, wg_ready = psem("wg_hi"), psem("wg_ready")
    plan1 = dict(
        period=32, lead=(0, 8, 10, 17),
        pe={0: 2, 1: 11, 3: 21, 4: 31},
        act={0: 3, 2: 13, 4: 31},
        dve={0: 4, 1: 12, 2: 16, 3: 25},
        sp={3: 24})

    with nc.Block() as block:

        @block.sync
        def _(sp):
            for s in S:
                sp.dma_start(xg_t[s], rows_of_group(state0, s, 0)).then_inc(xg_loaded[s], 16)
            sp.dma_start(lstm_stage[1][0], t["wih"][1]).then_inc(lstm_loaded[1], 16)
            sp.dma_start(lstm_stage[1][1], t["whh"][1]).then_inc(lstm_loaded[1], 16)

            def stage(s, slot, turn):
                if slot == 3 and not (isinstance(turn, int) and turn == TURNS - 1):
                    sp.wait_ge(ga_done[s], turn + 1)
                    sp.dma_start(xg_t[s], rows_of_group(state0, s, turn + 1)).then_inc(xg_loaded[s], 16)

            weave(sp, TURNS, plan1, "sp", stage)

        @block.scalar
        def _(act):
            act.wait_ge(gcn_loaded, 3 * 16)
            act.activation(wg_r[:, 0], gcn_raw, ACT.Copy).then_inc(wg_hi, 1)
            ahead(act, gcn_ready)

            def stage(s, slot, turn):
                if slot == 0:
                    act.wait_ge(ga_done[s], turn + 1)
                    act.activation(zg[s][:, 0], feature_major(s, 0), ACT.Copy).then_inc(zg_hi[s], 1)
                if slot == 2:
                    act.wait_ge(tg_ready[s], KD * turn + KD)
                    act.activation(h1[s][:, 0], tg_f[s], ACT.Relu).then_inc(h1_hi[s], 1)
                if slot == 4:
                    act.wait_ge(gb_done[s], turn + 1)
                    act.activation(columns_of(Hflat, s, turn), feature_major(s, 1), ACT.Relu)\
                       .then_inc(gcn_ready[s], 1)

            weave(act, TURNS, plan1, "act", stage)

        @block.vector
        def _(dve):
            dve.wait_ge(wg_hi, 1)
            dve.tensor_tensor(wg_r[:, 1], gcn_raw, raw(wg_r[:, 0]), ALU.subtract).then_inc(wg_ready, 1)
            ahead(dve, ug_ready)

            def stage(s, slot, turn):
                if slot == 0:
                    dve.wait_ge(zg_hi[s], turn + 1)
                    dve.tensor_tensor(zg[s][:, 1], feature_major(s, 0), raw(zg[s][:, 0]), ALU.subtract)\
                       .then_inc(zg_ready[s], 1)
                if slot == 1:
                    dve.wait_ge(g0_done[s], turn + 1)
                    for k in range(KD):
                        nb = GROUP // NODES
                        by_graph = (tg_f[s][:, k, :], feature_major(s, 1)[:, k, :])
                        o, i = (v.rearrange("p (b n) -> p b n", n=NODES) for v in by_graph)
                        dve.tensor_tensor(o, i, bg0_rows[:, k, :].unsqueeze(1).to_broadcast([P, nb, NODES]),
                                          ALU.add).then_inc(tg_ready[s], 1)
                if slot == 2:
                    dve.wait_ge(h1_hi[s], turn + 1)
                    dve.scalar_tensor_tensor(out=h1[s][:, 1], in0=tg_f[s], scalar=0.0, in1=raw(h1[s][:, 0]),
                                             op0=ALU.max, op1=ALU.subtract).then_inc(h1_ready[s], 1)
                if slot == 3:
                    dve.wait_ge(g1_done[s], turn + 1)
                    dve.tensor_tensor(ug_t[s], token_major(s, 0), over_tiles(bg1), ALU.add).then_inc(ug_ready[s], 1)

            weave(dve, TURNS, plan1, "dve", stage)

        @block.tensor
        def _(pe):
            pe.wait_ge(wg_ready, 1)

            def mix(out, src):
                for n in range(TILES):
                    for k in range(KD):
                        mm = pe.matmul(out[:, k, n * P:(n + 1) * P], src[:, n, k * P:(k + 1) * P], adjT[:],
                                       start=True, stop=True)
                return mm

            def stage(s, slot, turn):
                if slot == 0:
                    pe.wait_ge(xg_loaded[s], 16 * turn + 16)
                    pe.wait_ge(ug_ready[s], turn + 1)
                    mix(feature_major(s, 0), xg_t[s]).then_inc(ga_done[s], 1)
                if slot == 1:
                    pe.wait_ge(zg_ready[s], turn + 1)
                    pe.wait_ge(gcn_ready[s], turn + 1)
                    for m in range(KD):
                        for k in range(KD):
                            mm = exact_mm(pe, feature_major(s, 1)[:, m, :],
                                          lambda q: wg_r[:, q, 0, k, m * P:(m + 1) * P],
                                          lambda q: zg[s][:, q, k, :], k == 0, k == KD - 1)
                    mm.then_inc(g0_done[s], 1)
                if slot == 3:
                    pe.wait_ge(h1_ready[s], turn + 1)
                    for n in range(TILES):
                        for k in range(KD):
                            mm = exact_mm(pe, token_major(s, 0)[:, n, :],
                                          lambda q: h1[s][:, q, k, n * P:(n + 1) * P],
                                          lambda q: wg_r[:, q, 1, k, :], k == 0, k == KD - 1)
                    mm.then_inc(g1_done[s], 1)
                if slot == 4:
                    pe.wait_ge(ug_ready[s], turn + 2)
                    mix(feature_major(s, 1), ug_t[s]).then_inc(gb_done[s], 1)

            weave(pe, TURNS, plan1, "pe", stage)

    end_phase()

    LS = 2
    COLS = 256
    lb = region(H2_words[:, 0:2 * 4096])
    gate = [lb(GATES, KD * COLS) for _ in range(LS)]
    cell = [lb(KD * COLS) for _ in range(LS)]
    hid = [lb(KD * COLS) for _ in range(LS)]
    lr = region(R[:])
    w_r = lr(2, 2, KD, GATES * D)
    xin = [lr(2, KD, COLS) for _ in range(LS)]
    hin = [lr(2, KD, COLS) for _ in range(LS)]
    order = (0, 2, 1, 3)

    def gates_of(j):
        return [q for q in order if not (q == 1 and j == 0)]

    for p in range(1, MAX_SKIP + 1):
        nw = NODES // p
        nb = COLS // nw
        turns = -(-BATCH // (nb * LS))
        nb_last = (BATCH - nb * LS * (turns - 1)) // LS
        per_turn = sum(len(gates_of(j)) for j in range(p))
        stg = lstm_stage[(p - 1) % 2]
        gates_done, act_done = sems(f"gates_done{p}_", LS), sems(f"act_done{p}_", LS)
        x_hi, x_ready = sems(f"x_hi{p}_", LS), sems(f"x_ready{p}_", LS)
        cell_ready, tanh_ready = sems(f"cell_ready{p}_", LS), sems(f"tanh_ready{p}_", LS)
        hid_ready = sems(f"hid_ready{p}_", LS)
        lstm_steps = sems(f"lstm_steps{p}_", LS)
        w_hi, w_ready = psem(f"w_hi{p}"), psem(f"w_ready{p}")
        parts = [(w, k) for w in range(1 if p == 1 else 2) for k in range(KD)]

        def graphs(turn):
            return nb_last if isinstance(turn, int) and turn == turns - 1 else nb

        def blocks_at(q, s):
            return blocks_of(gate[s][:, q, :])

        def gate_ps(s, q, m):
            b = q * KD + m
            return ps[:, 4 * s + b // 2, (b % 2) * COLS:(b % 2 + 1) * COLS]

        def window(turn, s, j):
            n = graphs(turn)
            first = (turns - 1) * LS * nb + s * n if isinstance(turn, int) and turn == turns - 1 \
                else (turn * LS + s) * nb
            return H[:, :, bass.ds(first, n), j:j + p * (nw - 1) + 1:p]

        def as_window(v, turn):
            n = graphs(turn)
            return v[:, :, 0:n * nw].rearrange("p k (b w) -> p k b w", b=n)

        def run(eng, step):
            looped = turns - 1 if nb_last == nb else turns - 2
            with eng.Fori(0, looped) as i:
                for j in range(p):
                    for s in range(LS):
                        step(i, j, s, (i, j + 1) if j < p - 1 else (i + 1, 0))
            for turn in range(looped, turns):
                for j in range(p):
                    for s in range(LS):
                        after = (turn + 1, 0) if turn < turns - 1 else None
                        step(turn, j, s, (turn, j + 1) if j < p - 1 else after)

        with nc.Block() as block:

            @block.sync
            def _(sp):
                if p in (1, 2):
                    sp.wait_ge(w_ready, len(parts))
                    sp.dma_start(lstm_stage[(p + 1) % 2][0], t["wih"][p + 1]).then_inc(lstm_loaded[p + 1], 16)
                    sp.dma_start(lstm_stage[(p + 1) % 2][1], t["whh"][p + 1]).then_inc(lstm_loaded[p + 1], 16)
                if p == 3:
                    sp.wait_ge(w_ready, len(parts))
                    sp.dma_start(l2_raw[0], t["L2W1"]).then_inc(l2_loaded, 16)
                    sp.dma_start(l2_raw[1], t["L2W2"]).then_inc(l2_loaded, 16)
                    for dst, name in ((Wq3, "Wq3"), (Wk3, "Wk3"), (Wv3, "Wv3"), (Wo3, "Wo3")):
                        sp.dma_start(dst, t[name]).then_inc(l3_loaded, 16)
                    sp.dma_start(bo3, rows("bo3")).then_inc(l3_loaded, 16)

            @block.scalar
            def _(act):
                act.wait_ge(lstm_loaded[p - 1], 16 if p == 1 else 32)
                for w, k in parts:
                    act.activation(w_r[:, 0, w, k, :], stg[w][:, k, :], ACT.Copy).then_inc(w_hi, 1)

                def split_x(s, turn, j):
                    act.activation(as_window(xin[s][:, 0], turn), window(turn, s, j), ACT.Copy).then_inc(x_hi[s], 1)

                def step(turn, j, s, nxt):
                    done = sum(len(gates_of(jj)) for jj in range(j))
                    act.wait_ge(hid_ready[s], turn * p + j + 1)
                    for n, q in enumerate(gates_of(j)):
                        act.wait_ge(gates_done[s], turn * per_turn + done + n + 1)
                        for m in range(KD):
                            ins = act.activation(blocks_at(q, s)[:, m, :], gate_ps(s, q, m),
                                                 ACT.Tanh if q == 2 else ACT.Sigmoid,
                                                 bias=lstm_bias[:, p - 1, 2 * q + m:2 * q + m + 1])
                        ins.then_inc(act_done[s], 1)
                    act.wait_ge(cell_ready[s], turn * p + j + 1)
                    act.activation(blocks_at(2, s), blocks_of(cell[s]), ACT.Tanh).then_inc(tanh_ready[s], 1)
                    if nxt:
                        split_x(s, *nxt)

                for s in range(LS):
                    split_x(s, 0, 0)
                run(act, step)

            @block.vector
            def _(dve):
                for n, (w, k) in enumerate(parts):
                    dve.wait_ge(w_hi, n + 1)
                    dve.tensor_tensor(w_r[:, 1, w, k, :], stg[w][:, k, :], raw(w_r[:, 0, w, k, :]), ALU.subtract)\
                       .then_inc(w_ready, 1)
                ahead(dve, hid_ready)
                per_step = [2 if j < p - 1 else 0 for j in range(p)]
                per_step = [n + (2 if j else 0) for j, n in enumerate(per_step)]

                def split_x(s, turn, j):
                    dve.wait_ge(x_hi[s], turn * p + j + 1)
                    dve.tensor_tensor(as_window(xin[s][:, 1], turn), window(turn, s, j),
                                      as_window(raw(xin[s][:, 0]), turn), ALU.subtract).then_inc(x_ready[s], 1)

                def step(turn, j, s, nxt):
                    c = Chain(dve, lstm_steps[s], sum(per_step))
                    c.at(turn, sum(per_step[:j]))
                    done = sum(len(gates_of(jj)) for jj in range(j))
                    gi, gf, gg, go = (blocks_at(q, s) for q in range(GATES))
                    cl = blocks_of(cell[s])
                    dve.wait_ge(act_done[s], turn * per_turn + done + 2)
                    if j == 0:
                        dve.tensor_tensor(cl, gi, gg, ALU.mult).then_inc(cell_ready[s], 1)
                    else:
                        c.step(dve.tensor_tensor(gi, gi, gg, ALU.mult))
                        dve.wait_ge(act_done[s], turn * per_turn + done + 3)
                        c.step(dve.tensor_tensor(cl, cl, gf, ALU.mult))
                        c.settle()
                        dve.tensor_tensor(cl, cl, gi, ALU.add).then_inc(cell_ready[s], 1)
                    dve.wait_ge(act_done[s], turn * per_turn + done + len(gates_of(j)))
                    dve.wait_ge(tanh_ready[s], turn * p + j + 1)
                    if j < p - 1:
                        h = blocks_of(hid[s])
                        c.step(dve.tensor_tensor(h, go, gg, ALU.mult))
                        c.settle()
                        c.step(dve.tensor_scalar(hin[s][:, 0], h, 1.0, None, ALU.mult))
                        c.settle()
                        dve.tensor_tensor(hin[s][:, 1], h, raw(hin[s][:, 0]), ALU.subtract)\
                           .then_inc(hid_ready[s], 1)
                    else:
                        dve.tensor_tensor(window(turn, s, j), as_window(go, turn), as_window(gg, turn), ALU.mult)\
                           .then_inc(hid_ready[s], 1)
                    if nxt:
                        split_x(s, *nxt)

                for s in range(LS):
                    split_x(s, 0, 0)
                run(dve, step)

            @block.tensor
            def _(pe):
                pe.wait_ge(w_ready, len(parts))

                def step(turn, j, s, nxt):
                    pe.wait_ge(x_ready[s], turn * p + j + 1)
                    pe.wait_ge(hid_ready[s], turn * p + j + 1)
                    for q in gates_of(j):
                        for m in range(KD):
                            f = slice((q * KD + m) * P, (q * KD + m + 1) * P)
                            operands = [(0, xin, k) for k in range(KD)] + [(1, hin, k) for k in range(KD) if j]
                            for n, (w, src, k) in enumerate(operands):
                                mm = exact_mm(pe, gate_ps(s, q, m), lambda a: w_r[:, a, w, k, f],
                                              lambda a: src[s][:, a, k, :], n == 0, n == len(operands) - 1)
                        mm.then_inc(gates_done[s], 1)

                run(pe, step)

        end_phase()

    cb = region(arena[:, W3_WORDS:])
    hs, ys = ([cb(G2) for _ in S] for _ in range(2))
    hs_f = [blocks_of(v) for v in hs]
    ys_t = [tiles_of(v) for v in ys]
    bn_stats1 = cb(MB, STREAMS * TURNS * 6)
    cr = region(R[:])
    l2w1_r = cr(2, KD, HID2)
    l2w2_r = cr(2, MB, D)
    ag = [cr(2, KD, GROUP) for _ in S]
    (hs_ready, ys_loaded, h_turned, l1_var, l1_rstd, l1_ready, l1_stored, g2_done, ag_hi, ag_ready, up2_done,
     h2_kept, st_taken) = (sems(n) for n in
                           ("hs_ready", "ys_loaded", "h_turned", "l1_var", "l1_rstd", "l1_ready", "l1_stored",
                            "g2_done", "ag_hi", "ag_ready", "up2_done", "h2_kept", "st_taken"))
    l2_hi, l2_ready, bn1_var, bn1_pow, bn_steps = (psem(n) for n in ("l2_hi", "l2_ready", "bn1_var", "bn1_pow",
                                                                     "bn_steps"))
    plan2 = dict(
        period=48, lead=(0, 7, 24, 32),
        pe={1: 2, 3: 20, 4: 35},
        act={0: 0, 3: 27, 4: 43},
        dve={1: 11, 2: 19, 3: 27, 5: 46},
        pool={1: 15},
        sp={3: 20, 5: 36})

    def fold_batch_norm(dve, c, stats, cols, ss, blocks, ready, made, biased):
        for m in range(blocks):
            c.step(dve.bn_aggr(bn_mv[:, m, :], stats[:, m, :]))
        c.settle()
        mv = bn_mv[:, 0:blocks, :]
        if biased:
            c.step(dve.tensor_scalar(bn_tmp[:, 0, 0:blocks], mv[:, :, 0], -1.0, None, ALU.mult))
        else:
            c.step(dve.tensor_tensor(bn_tmp[:, 0, 0:blocks], mv[:, :, 0], cols[:, 0, :], ALU.add))
        c.step(dve.tensor_scalar(bn_tmp[:, 1, 0:blocks], mv[:, :, 1], EPS, None, ALU.add))
        c.settle()
        dve.sem_inc(ready, 1)
        if not biased:
            c.step(dve.tensor_tensor(bn_tmp[:, 0, 0:blocks], cols[:, 0, :], bn_tmp[:, 0, 0:blocks], ALU.subtract))
            c.settle()
        dve.wait_ge(made, 1)
        c.step(dve.tensor_tensor(ss[:, 0, :], bn_tmp[:, 2, 0:blocks], cols[:, 1, :], ALU.mult))
        c.settle()
        c.step(dve.tensor_tensor(bn_tmp[:, 0, 0:blocks], bn_tmp[:, 0, 0:blocks], ss[:, 0, :], ALU.mult))
        c.settle()
        c.step(dve.tensor_tensor(ss[:, 1, :], bn_tmp[:, 0, 0:blocks], cols[:, 2, :], ALU.add))
        c.settle()

    with nc.Block() as block:

        @block.sync
        def _(sp):
            for s in S:
                sp.dma_start(ys_t[s], rows_of_group(state0, s, 0)).then_inc(ys_loaded[s], 16)

            def stage(s, slot, turn):
                if slot == 3:
                    sp.wait_ge(l1_ready[s], turn + 1)
                    sp.dma_start(rows_of_group(state1, s, turn), ys_t[s]).then_inc(l1_stored[s], 16)
                if slot == 5 and not (isinstance(turn, int) and turn == TURNS - 1):
                    sp.wait_ge(l1_stored[s], 16 * turn + 16)
                    alone(sp, waits_passed)
                    sp.wait_ge(g2_done[s], turn + 1)
                    sp.dma_start(ys_t[s], rows_of_group(state0, s, turn + 1)).then_inc(ys_loaded[s], 16)

            weave(sp, TURNS, plan2, "sp", stage)
            for s in S:
                sp.wait_ge(l1_stored[s], 16 * TURNS)

        @block.gpsimd
        def _(pool):
            steps = Steps(pool, "p7_pool", {1: 1})

            def stage(s, slot, turn):
                if slot == 1:
                    ln_reciprocal(pool, steps.enter(s, slot, turn), s, l1_var[s], l1_rstd[s], turn + 1)

            weave(pool, TURNS, plan2, "pool", stage)
            pool.wait_ge(bn1_var, 1)
            pool.tensor_tensor(bn_tmp[:, 2, 0:MB], bn_tmp[:, 1, 0:MB], minus_half[:, 0:MB], ALU.pow)\
                .then_inc(bn1_pow, 1)

        @block.scalar
        def _(act):
            act.wait_ge(l2_loaded, 32)
            act.activation(l2w1_r[:, 0], l2_raw[0], ACT.Copy).then_inc(l2_hi, 1)
            act.activation(l2w2_r[:, 0], l2_raw[1], ACT.Copy).then_inc(l2_hi, 1)
            act.wait_ge(l2_ready, 2)
            ahead(act, h2_kept, by=2)

            def stage(s, slot, turn):
                if slot == 0:
                    act.wait_ge(h_turned[s], turn + 1)
                    act.activation(hs_f[s], columns_of(Hflat, s, turn), ACT.Copy).then_inc(hs_ready[s], 1)
                if slot == 3:
                    act.wait_ge(g2_done[s], turn + 1)
                    act.activation(ag[s][:, 0], feature_major(s, 1), ACT.Copy).then_inc(ag_hi[s], 1)
                if slot == 4:
                    act.wait_ge(up2_done[s], turn + 1)
                    alone(act, waits_passed)
                    act.activation(columns_of(Hflat, s, turn), feature_major(s, 0), ACT.Copy).then_inc(h2_kept[s], 1)
                    act.activation(columns_of(H2flat, s, turn), feature_major(s, 1), ACT.Copy)\
                       .then_inc(h2_kept[s], 1)

            weave(act, TURNS, plan2, "act", stage)

        @block.vector
        def _(dve):
            for q, w in enumerate((l2w1_r, l2w2_r)):
                dve.wait_ge(l2_hi, q + 1)
                dve.tensor_tensor(w[:, 1], l2_raw[q], raw(w[:, 0]), ALU.subtract).then_inc(l2_ready, 1)
            steps = Steps(dve, "p7_dve", {1: 1 + LN_STATS})

            def stage(s, slot, turn):
                c = steps.enter(s, slot, turn)
                if slot == 1:
                    dve.wait_ge(h_turned[s], turn + 2)
                    dve.wait_ge(ys_loaded[s], 16 * turn + 16)
                    c.step(dve.tensor_tensor(ys_t[s], token_major(s, 0), ys_t[s], ALU.add))
                    c.settle()
                    ln_statistics(dve, c, ys_t[s], s, l1_var[s])
                if slot == 2:
                    ln_plain(dve, ys_t[s], s, l1_rstd[s], turn + 1).then_inc(l1_ready[s], 1)
                if slot == 3:
                    dve.wait_ge(ag_hi[s], turn + 1)
                    dve.tensor_tensor(ag[s][:, 1], feature_major(s, 1), raw(ag[s][:, 0]), ALU.subtract)\
                       .then_inc(ag_ready[s], 1)
                if slot == 5:
                    for h, state in enumerate((Hflat, H2flat)):
                        dve.wait_ge(h2_kept[s], 2 * turn + h + 3)
                        for m in range(KD):
                            dve.bn_stats(bn_stats1[:, KD * h + m, bass.ds((turn * STREAMS + s) * 6, 6)],
                                         columns_of(state, s, turn)[:, m, :]).then_inc(st_taken[s], 1)

            weave(dve, TURNS, plan2, "dve", stage)
            for s in S:
                dve.wait_ge(st_taken[s], MB * TURNS)
            fold_batch_norm(dve, Chain(dve, bn_steps), bn_stats1, bn1_col, bn1_ss, MB, bn1_var, bn1_pow, False)

        @block.tensor
        def _(pe):
            pe.wait_ge(l2_ready, 2)
            ahead(pe, h_turned)

            def stage(s, slot, turn):
                if slot == 1:
                    pe.wait_ge(hs_ready[s], turn + 1)
                    pe.wait_ge(h2_kept[s], 2 * turn + 2)
                    for n in range(TILES):
                        for k in range(KD):
                            mm = pe.transpose(token_major(s, 0)[:, n, k * P:(k + 1) * P],
                                              hs_f[s][:, k, n * P:(n + 1) * P], ident[:])
                    mm.then_inc(h_turned[s], 1)
                if slot == 3:
                    pe.wait_ge(l1_ready[s], turn + 1)
                    for n in range(TILES):
                        for k in range(KD):
                            mm = pe.matmul(feature_major(s, 1)[:, k, n * P:(n + 1) * P],
                                           ys_t[s][:, n, k * P:(k + 1) * P], ahatT[:], start=True, stop=True)
                    mm.then_inc(g2_done[s], 1)
                if slot == 4:
                    pe.wait_ge(ag_ready[s], turn + 1)
                    for m in range(MB):
                        for k in range(KD):
                            mm = exact_mm(pe, feature_major(s, m // KD)[:, m % KD, :],
                                          lambda q: l2w1_r[:, q, k, m * P:(m + 1) * P],
                                          lambda q: ag[s][:, q, k, :], k == 0, k == KD - 1)
                    mm.then_inc(up2_done[s], 1)

            weave(pe, TURNS, plan2, "pe", stage)

    end_phase()

    eb = region(arena[:, W3_WORDS:])
    rf32 = [eb(MB, GROUP) for _ in S]
    bn_stats2 = eb(KD, STREAMS * TURNS * 6)
    er = region(R[:, 2 * KD * HID2 + 2 * MB * D:])
    rr = [er(2, MB, GROUP) for _ in S]
    (r_ready, r_split, dn2_done, out2_ready, st2_taken) = (sems(n) for n in
                                                           ("r_ready", "r_split", "dn2_done", "out2_ready",
                                                            "st2_taken"))
    bn2_var, bn2_pow, bn_steps2 = psem("bn2_var"), psem("bn2_pow"), psem("bn_steps2")
    plan3 = dict(
        period=24, lead=(0, 4, 12, 21),
        pe={2: 17},
        act={0: 1, 2: 22},
        dve={1: 1, 3: 23})

    with nc.Block() as block:

        @block.gpsimd
        def _(pool):
            pool.wait_ge(bn2_var, 1)
            pool.tensor_tensor(bn_tmp[:, 2, 0:KD], bn_tmp[:, 1, 0:KD], minus_half[:, 0:KD], ALU.pow)\
                .then_inc(bn2_pow, 1)

        @block.scalar
        def _(act):
            ahead(act, out2_ready)

            def stage(s, slot, turn):
                if slot == 0:
                    act.wait_ge(r_split[s], turn + 1)
                    for m in range(MB):
                        state = (Hflat, H2flat)[m // KD]
                        ins = act.activation(rf32[s][:, m, :], columns_of(state, s, turn)[:, m % KD, :], ACT.Relu,
                                             bias=bn1_ss[:, 1, m:m + 1], scale=bn1_ss[:, 0, m:m + 1])
                    ins.then_inc(r_ready[s], 1)
                if slot == 2:
                    act.wait_ge(dn2_done[s], turn + 2)
                    alone(act, waits_passed)
                    for m in range(KD):
                        ins = act.activation(columns_of(Hflat, s, turn)[:, m, :], feature_major(s, 0)[:, m, :],
                                             ACT.Identity, bias=bn2_col[:, 0, m:m + 1])
                    ins.then_inc(out2_ready[s], 1)

            weave(act, TURNS, plan3, "act", stage)

        @block.vector
        def _(dve):
            steps = Steps(dve, "p8_dve", {1: 1})
            ahead(dve, r_split)

            def stage(s, slot, turn):
                c = steps.enter(s, slot, turn)
                if slot == 1:
                    dve.wait_ge(r_ready[s], turn + 1)
                    dve.wait_ge(dn2_done[s], turn + 1)
                    c.step(dve.tensor_scalar(rr[s][:, 0], rf32[s], 1.0, None, ALU.mult))
                    c.settle()
                    dve.tensor_tensor(rr[s][:, 1], rf32[s], raw(rr[s][:, 0]), ALU.subtract).then_inc(r_split[s], 1)
                if slot == 3:
                    dve.wait_ge(out2_ready[s], turn + 2)
                    for m in range(KD):
                        dve.bn_stats(bn_stats2[:, m, bass.ds((turn * STREAMS + s) * 6, 6)],
                                     columns_of(Hflat, s, turn)[:, m, :]).then_inc(st2_taken[s], 1)

            weave(dve, TURNS, plan3, "dve", stage)
            for s in S:
                dve.wait_ge(st2_taken[s], KD * TURNS)
            fold_batch_norm(dve, Chain(dve, bn_steps2), bn_stats2, bn2_col, bn2_ss, KD, bn2_var, bn2_pow, True)

        @block.tensor
        def _(pe):
            ahead(pe, dn2_done)

            def stage(s, slot, turn):
                if slot == 2:
                    pe.wait_ge(r_split[s], turn + 2)
                    pe.wait_ge(out2_ready[s], turn + 1)
                    for m in range(KD):
                        for k in range(MB):
                            mm = exact_mm(pe, feature_major(s, 0)[:, m, :],
                                          lambda q: l2w2_r[:, q, k, m * P:(m + 1) * P],
                                          lambda q: rr[s][:, q, k, :], k == 0, k == MB - 1)
                    mm.then_inc(dn2_done[s], 1)

            weave(pe, TURNS, plan3, "pe", stage)

    end_phase()

    db = region(H2_words)
    x3, xT3, x3b, xr = ([db(G2) for _ in S] for _ in range(4))
    qk3 = [db(2, GROUP) for _ in S]
    v3 = [db(TILES, ATT3) for _ in S]
    at3 = [db(TILES, NODES) for _ in S]
    bd3 = [db(TILES, P) for _ in S]
    atT3 = [db(TILES, P) for _ in S]
    hs3 = qk3
    rf_t = [tiles_of(v.rearrange("p a n -> p (a n)")) for v in qk3]
    x3_t, x3b_t, xr_t, y3_t = ([tiles_of(v) for v in b] for b in (x3, x3b, xr, xT3))
    xT3_f = [blocks_of(v) for v in xT3]
    (xr_loaded, hn_ready, h9_turned, var9, rstd9, x3_ready, x3b_ready, x3_turned, xT3_ready, qk3_done, qk3_ready,
     v3_done, v3_ready, sc3_done, sc3_ready, exp3_ready, at3_ready, at3_turned, atT3_ready, o3_done, o3T_ready,
     wo3_done, rf_ready, child_done, y3_ready, stored) = (sems("l3_" + n) for n in
                                                          ("xr", "hn", "ht", "var", "rstd", "x3", "x3b", "xt",
                                                           "xT", "qkd", "qkr", "vd", "vr", "scd", "scr", "exr",
                                                           "atr", "att", "atT", "od", "oT", "wod", "rfr", "chd",
                                                           "y3", "stored"))
    rest_made, rest_ready = sems("l3_rest_made"), sems("l3_rest_ready")
    bd3_zero = psem("bd3_zero")
    plan4 = dict(
        period=64, lead=(0, 11, 37, 49),
        pe={1: 5, 3: 18, 4: 23, 5: 25, 6: 28, 9: 38, 10: 40, 11: 41, 12: 46},
        act={0: 2, 3: 21, 4: 25, 5: 25, 7: 33, 9: 38, 10: 40, 11: 46},
        dve={1: 9, 2: 15, 6: 30, 8: 34, 11: 44, 12: 51, 13: 58},
        pool={1: 13, 3: 32, 11: 49, 12: 56},
        sp={10: 54, 13: 60})

    with nc.Block() as block:

        @block.sync
        def _(sp):
            ahead(sp, stored, by=16)
            for s in S:
                sp.dma_start(xr_t[s], rows_of_group(state1, s, 0)).then_inc(xr_loaded[s], 16)

            def stage(s, slot, turn):
                if slot == 10 and not (isinstance(turn, int) and turn == TURNS - 1):
                    sp.wait_ge(var9[s], 2 * turn + 1)
                    sp.dma_start(xr_t[s], rows_of_group(state1, s, turn + 1)).then_inc(xr_loaded[s], 16)
                if slot == 13:
                    sp.wait_ge(y3_ready[s], turn + 2)
                    sp.dma_start(rows_of_group(out_view, s, turn), y3_t[s]).then_inc(stored[s], 16)

            weave(sp, TURNS, plan4, "sp", stage)
            for s in S:
                sp.wait_ge(stored[s], 16 * TURNS + 16)

        @block.gpsimd
        def _(pool):
            for s in S:
                pool.memset(bd3[s], 0.0).then_inc(bd3_zero, 1)
            steps = Steps(pool, "p9_pool", {1: 1, 12: 1})

            def stage(s, slot, turn):
                for n, at in enumerate((1, 12)):
                    if slot == at:
                        ln_reciprocal(pool, steps.enter(s, slot, turn), s, var9[s], rstd9[s], 2 * turn + n + 1)
                if slot == 3:
                    pool.wait_ge(x3_ready[s], turn + 1)
                    pool.tensor_tensor(x3b_t[s], x3_t[s], over_tiles(bo3), ALU.add).then_inc(x3b_ready[s], 1)
                if slot == 11:
                    pool.wait_ge(rest_made[s], turn + 1)
                    pool.tensor_tensor(x3b_t[s], x3b_t[s], x3_t[s], ALU.add).then_inc(rest_ready[s], 1)

            weave(pool, TURNS, plan4, "pool", stage)

        @block.scalar
        def _(act):
            def stage(s, slot, turn):
                if slot == 0:
                    act.wait_ge(y3_ready[s], turn + 1)
                    for m in range(KD):
                        ins = act.activation(hs3[s][:, m, :], columns_of(Hflat, s, turn)[:, m, :],
                                             ACT.Identity, bias=bn2_ss[:, 1, m:m + 1], scale=bn2_ss[:, 0, m:m + 1])
                    ins.then_inc(hn_ready[s], 1)
                if slot == 3:
                    act.wait_ge(x3_turned[s], turn + 1)
                    act.wait_ge(stored[s], 16 * turn + 16)
                    act.activation(xT3_f[s], feature_major(s, 1), ACT.Copy).then_inc(xT3_ready[s], 1)
                if slot == 4:
                    act.wait_ge(qk3_done[s], turn + 1)
                    for m in range(2):
                        ins = act.activation(qk3[s][:, m, :], feature_major(s, 0)[:, m, :], ACT.Identity,
                                             bias=qk3_bias[:, m:m + 1])
                    ins.then_inc(qk3_ready[s], 1)
                if slot == 5:
                    act.wait_ge(v3_done[s], turn + 1)
                    act.activation(v3[s], token_major(s, 1, ATT3), ACT.Copy).then_inc(v3_ready[s], 1)
                if slot == 7:
                    act.wait_ge(sc3_ready[s], turn + 1)
                    act.activation(at3[s], at3[s], ACT.Exp).then_inc(exp3_ready[s], 1)
                if slot == 9:
                    act.wait_ge(at3_turned[s], turn + 1)
                    act.activation(atT3[s], token_major(s, 0, P), ACT.Copy).then_inc(atT3_ready[s], 1)
                if slot == 10:
                    act.wait_ge(o3_done[s], turn + 1)
                    act.activation(atT3[s], token_major(s, 1, P), ACT.Identity, bias=bv3_col[:, 0:1])\
                       .then_inc(o3T_ready[s], 1)
                if slot == 11:
                    act.wait_ge(rf_ready[s], turn + 1)
                    act.activation(x3b_t[s], rf_t[s], ACT.Copy, scale=rest_gamma[:, 0:1])\
                       .then_inc(rest_made[s], 1)

            weave(act, TURNS, plan4, "act", stage)

        @block.vector
        def _(dve):
            dve.wait_ge(bd3_zero, STREAMS)
            steps = Steps(dve, "p9_dve", {1: 1 + LN_STATS, 6: 6, 8: 2, 12: 1 + LN_STATS})
            ahead(dve, y3_ready)
            rows_b = [slice(NODES * b, NODES * (b + 1)) for b in range(2)]

            def stage(s, slot, turn):
                c = steps.enter(s, slot, turn)
                if slot == 1:
                    dve.wait_ge(h9_turned[s], turn + 1)
                    dve.wait_ge(xr_loaded[s], 16 * turn + 16)
                    c.step(dve.tensor_tensor(x3_t[s], token_major(s, 0), xr_t[s], ALU.add))
                    c.settle()
                    ln_statistics(dve, c, x3_t[s], s, var9[s])
                if slot == 2:
                    ln_plain(dve, x3_t[s], s, rstd9[s], 2 * turn + 1).then_inc(x3_ready[s], 1)
                if slot == 6:
                    dve.wait_ge(sc3_done[s], turn + 1)
                    full = [P, TILES, NODES]

                    def spread(v):
                        return v.unsqueeze(1).to_broadcast(full)

                    for r in rows_b:
                        c.step(dve.scalar_tensor_tensor(out=at3[s][r], in0=token_major(s, 0, P)[r, :, r],
                                                        scalar=float(ATT3) ** -0.5,
                                                        in1=alpha_adj[r].unsqueeze(1).to_broadcast(
                                                            [NODES, TILES, NODES]),
                                                        op0=ALU.mult, op1=ALU.add))
                    c.settle()
                    c.step(dve.tensor_tensor(at3[s], at3[s], spread(nz_mask[:]), ALU.mult))
                    c.settle()
                    c.step(dve.tensor_tensor(at3[s], at3[s], spread(nz_neg[:]), ALU.add))
                    c.settle()
                    c.step(dve.tensor_reduce(sm_max[:, s, 0:TILES], at3[s], AX_X, ALU.max))
                    c.settle()
                    c.step(dve.tensor_tensor(at3[s], at3[s], sm_max[:, s, 0:TILES].unsqueeze(2).to_broadcast(full),
                                             ALU.subtract))
                    c.settle()
                    dve.sem_inc(sc3_ready[s], 1)
                if slot == 8:
                    dve.wait_ge(exp3_ready[s], turn + 1)
                    c.step(dve.tensor_reduce(sm_sum[:, s, 0:TILES], at3[s], AX_X, ALU.add))
                    c.settle()
                    c.step(dve.reciprocal(sm_inv[:, s, 0:TILES], sm_sum[:, s, 0:TILES]))
                    c.settle()
                    for r in rows_b:
                        dve.tensor_tensor(bd3[s][r, :, r], at3[s][r],
                                          sm_inv[r, s, 0:TILES].unsqueeze(2).to_broadcast([NODES, TILES, NODES]),
                                          ALU.mult).then_inc(at3_ready[s], 1)
                if slot == 11:
                    dve.wait_ge(wo3_done[s], turn + 1)
                    dve.wait_ge(x3b_ready[s], turn + 1)
                    dve.tensor_tensor(rf_t[s], token_major(s, 0), x3b_t[s], ALU.add).then_inc(rf_ready[s], 1)
                if slot == 12:
                    dve.wait_ge(child_done[s], turn + 1)
                    dve.wait_ge(rest_ready[s], turn + 1)
                    c.step(dve.scalar_tensor_tensor(out=y3_t[s], in0=token_major(s, 1), scalar=parent_gamma[:, 0:1],
                                                    in1=x3b_t[s], op0=ALU.mult, op1=ALU.add))
                    c.settle()
                    ln_statistics(dve, c, y3_t[s], s, var9[s])
                if slot == 13:
                    ln_plain(dve, y3_t[s], s, rstd9[s], 2 * turn + 2).then_inc(y3_ready[s], 1)
                steps.leave(s, slot)

            weave(dve, TURNS, plan4, "dve", stage)

        @block.tensor
        def _(pe):
            pe.wait_ge(l3_loaded, 5 * 16)

            def stage(s, slot, turn):
                if slot == 1:
                    pe.wait_ge(hn_ready[s], turn + 1)
                    for n in range(TILES):
                        for k in range(KD):
                            mm = pe.transpose(token_major(s, 0)[:, n, k * P:(k + 1) * P],
                                              hs3[s][:, k, n * P:(n + 1) * P], ident[:])
                    mm.then_inc(h9_turned[s], 1)
                if slot == 3:
                    pe.wait_ge(x3_ready[s], turn + 1)
                    for n in range(TILES):
                        for k in range(KD):
                            mm = pe.transpose(feature_major(s, 1)[:, k, n * P:(n + 1) * P],
                                              x3_t[s][:, n, k * P:(k + 1) * P], ident[:])
                    mm.then_inc(x3_turned[s], 1)
                if slot == 4:
                    pe.wait_ge(xT3_ready[s], turn + 1)
                    for m, w in enumerate((Wq3, Wk3)):
                        for k in range(KD):
                            mm = pe.matmul(feature_major(s, 0)[:, m, :], w[:, k, :], xT3_f[s][:, k, :],
                                           start=(k == 0), stop=(k == KD - 1))
                    mm.then_inc(qk3_done[s], 1)
                if slot == 5:
                    for n in range(TILES):
                        for k in range(KD):
                            mm = pe.matmul(token_major(s, 1, ATT3)[:, n, :], xT3_f[s][:, k, n * P:(n + 1) * P],
                                           Wv3[:, k, :], start=(k == 0), stop=(k == KD - 1))
                    mm.then_inc(v3_done[s], 1)
                if slot == 6:
                    pe.wait_ge(qk3_ready[s], turn + 1)
                    for n in range(TILES):
                        q = slice(n * P, (n + 1) * P)
                        mm = pe.matmul(token_major(s, 0, P)[:, n, :], qk3[s][:, 0, q], qk3[s][:, 1, q],
                                       start=True, stop=True)
                    mm.then_inc(sc3_done[s], 1)
                if slot == 9:
                    pe.wait_ge(at3_ready[s], 2 * turn + 2)
                    for n in range(TILES):
                        mm = pe.transpose(token_major(s, 0, P)[:, n, :], bd3[s][:, n, :], ident[:])
                    mm.then_inc(at3_turned[s], 1)
                if slot == 10:
                    pe.wait_ge(atT3_ready[s], turn + 1)
                    pe.wait_ge(v3_ready[s], turn + 1)
                    for n in range(TILES):
                        mm = pe.matmul(token_major(s, 1, P)[:, n, :], v3[s][:, n, :], atT3[s][:, n, :],
                                       start=True, stop=True)
                    mm.then_inc(o3_done[s], 1)
                if slot == 11:
                    pe.wait_ge(o3T_ready[s], turn + 1)
                    for n in range(TILES):
                        mm = pe.matmul(token_major(s, 0)[:, n, :], atT3[s][:, n, :], Wo3[:], start=True, stop=True)
                    mm.then_inc(wo3_done[s], 1)
                if slot == 12:
                    pe.wait_ge(rf_ready[s], turn + 1)
                    for n in range(TILES):
                        mm = pe.matmul(token_major(s, 1)[:, n, :], adjT[:], rf_t[s][:, n, :], start=True, stop=True)
                    mm.then_inc(child_done[s], 1)

            weave(pe, TURNS, plan4, "pe", stage)


def kernel(**inputs):
    import numpy as np
    import concourse.bacc as bacc
    from concourse.bass_utils import run_bass_kernel_spmd

    a = {k: np.asarray(v) for k, v in inputs.items()}

    def split_rows(w):
        return w.reshape(-1, 128, w.shape[-1]).transpose(1, 0, 2)

    def columns(v):
        return v.reshape(-1, 128).T

    lay = {"x": a["x"].reshape(-1, a["x"].shape[-1]), "adj": a["adj"], "adjT": a["adj"].T}
    for n in ("Wc", "Wq", "Wk", "Wv", "Wo", "W1", "W2"):
        lay[n] = split_rows(a["L0_gnn_" + n])
    for n in ("bc", "g1", "be1", "bo", "g2", "be2", "b2", "g3", "be3"):
        lay[n] = a["L0_gnn_" + n]
    lay["b1"] = columns(a["L0_gnn_b1"])
    lay["Wg0"], lay["Wg1"] = split_rows(a["L1_gnn_Wg0"]), split_rows(a["L1_gnn_Wg1"])
    lay["bg0"], lay["bg1"] = columns(a["L1_gnn_bg0"]), a["L1_gnn_bg1"]
    lay["wih"] = np.stack([split_rows(w.T) for w in a["L1_gnn_Wih"]])
    lay["whh"] = np.stack([split_rows(w.T) for w in a["L1_gnn_Whh"]])
    lay["lstm_bih"] = a["L1_gnn_bih"].reshape(4, 8, 128).transpose(2, 0, 1)
    lay["lstm_bhh"] = a["L1_gnn_bhh"].reshape(4, 8, 128).transpose(2, 0, 1)
    lay["L2W1"], lay["L2W2"] = split_rows(a["L2_gnn_W1"].T), split_rows(a["L2_gnn_W2"].T)
    lay["bn1"] = np.stack([columns(a["L2_gnn_" + n]) for n in ("b1", "g1", "be1")], 1)
    lay["bn2"] = np.stack([columns(a["L2_gnn_" + n]) for n in ("b2", "g2", "be2")], 1)
    for n in ("Wq", "Wk", "Wv"):
        lay[n + "3"] = split_rows(a["L3_gnn_" + n])
    lay["Wo3"] = a["L3_gnn_Wo"]
    lay["qk3b"] = np.stack([a["L3_gnn_bq"], a["L3_gnn_bk"]], 1)
    lay["bv3"], lay["bo3"] = columns(a["L3_gnn_bv"]), a["L3_gnn_bo"]
    lay["alpha"], lay["gamma"] = a["L3_gnn_alpha"].reshape(1), a["L3_gnn_gamma"].reshape(1)

    nc = bacc.Bacc("TRN2", target_bir_lowering=False, num_devices=1)
    arrays, dram = {}, {}
    for n, v in lay.items():
        v = np.ascontiguousarray(v)
        arrays["in_" + n] = v
        dram[n] = nc.dram_tensor("in_" + n, v.shape, mybir.dt.from_np(v.dtype), kind="ExternalInput").ap()
    out = nc.dram_tensor("out_0", a["x"].shape, F32, kind="ExternalOutput").ap()
    build_stack(nc, dram, out)
    return run_bass_kernel_spmd(nc, [arrays], core_ids=[0]).results[0]["out_0"]
```

```python
from contextlib import ExitStack

import concourse.bass as bass
from concourse import mybir

ALU = mybir.AluOpType
ACT = mybir.ActivationFunctionType
F32 = mybir.dt.float32
F32R = mybir.dt.float32r
AX_X = mybir.AxisListType.X

P = 128
BATCH, NODES, D = 128, 64, 256
TOKENS = BATCH * NODES
KD = D // P
HEADS = 4
HEAD_DIM = D // HEADS
HID0 = 2 * D
HID2 = 2 * D
ATT3 = 128
MAX_SKIP = 4
GATES = 4
EPS = 1e-5
NEG = 1e9
SQUARINGS = 24
RUN = 4

GROUP = 256
STREAMS = 4
TILES = GROUP // P
TURNS = TOKENS // GROUP // STREAMS
BANKS = 8 // STREAMS
HALF = BANKS // 2


def alone(eng, waits_passed):
    eng.sem_inc(waits_passed, 1)


def ahead(eng, *lists, by=1):
    for group in lists:
        for s in group:
            eng.sem_inc(s, by)


class Chain:

    def __init__(self, eng, sem, per_turn=0):
        self.eng, self.sem, self.per_turn = eng, sem, per_turn
        self.base, self.n = 0, 0

    def turn(self, i):
        assert self.n in (0, self.per_turn), (self.n, self.per_turn)
        self.base, self.n = i * self.per_turn, 0

    def at(self, i, n):
        self.base, self.n = i * self.per_turn, n

    def step(self, ins):
        ins.then_inc(self.sem, 1)
        self.n += 1

    def settle(self):
        self.eng.wait_ge(self.sem, self.base + self.n)

    def end(self):
        assert self.n == self.per_turn, (self.n, self.per_turn)


def weave(eng, turns, plan, part, stage):
    period, lead = plan["period"], plan["lead"]
    late = max(tick for p in ("pe", "act", "dve", "pool", "sp") for tick in plan.get(p, {}).values()) // period

    def round_of(i):
        for at in range(period):
            for s in range(STREAMS):
                for slot, tick in plan[part].items():
                    if tick % period == (at + lead[s]) % period:
                        turn = i + ((at + lead[s]) // period - tick // period)
                        if not isinstance(turn, int) or 0 <= turn < turns:
                            stage(s, slot, turn)

    for i in range(-1, late):
        round_of(i)
    with eng.Fori(late, turns - 1) as i:
        round_of(i)
    for i in range(turns - 1, turns + late):
        round_of(i)


def build_stack(nc, t, out):
    with ExitStack() as ctx:
        build_program(nc, ctx, t, out.rearrange("b n d -> (b n) d"))


def build_program(nc, ctx, t, out_rows):
    def sb(name, shape):
        return ctx.enter_context(nc.sbuf_tensor(name, shape, F32))

    def sem(name):
        return ctx.enter_context(nc.semaphore(name))

    phase_sems = []

    def psem(name):
        phase_sems.append(nc.alloc_semaphore(name))
        return phase_sems[-1]

    def sems(name, n=STREAMS):
        return [psem(f"{name}{s}") for s in range(n)]

    def end_phase():
        nc.clear_and_free_semaphores(list(phase_sems))
        phase_sems.clear()
        nc.all_engine_barrier()

    H = sb("H", [P, KD, BATCH, NODES])
    H2 = sb("H2", [P, KD, BATCH, NODES])
    Hflat = H[:].rearrange("p k b n -> p k (b n)")
    H2flat = H2[:].rearrange("p k b n -> p k (b n)")
    R_WORDS, ARENA = 12288, 6400
    R = ctx.enter_context(nc.sbuf_tensor("R", [P, R_WORDS], F32R))
    arena = sb("arena", [P, ARENA])
    ps = ctx.enter_context(nc.psum_tensor("ps", [P, 8, 512], F32))
    state_rows = [nc.dram_tensor(f"residual{n}", (TOKENS, D), F32).ap() for n in range(2)]

    ident = sb("ident", [P, P])
    ones = sb("ones", [P, P])
    adjT = sb("adjT", [P, P])
    lnormT = sb("lnormT", [P, P])
    ahatT = sb("ahatT", [P, P])
    pos_mask = sb("pos_mask", [P, NODES])
    nz_mask = sb("nz_mask", [P, NODES])
    nz_neg = sb("nz_neg", [P, NODES])
    alpha_adj = sb("alpha_adj", [P, NODES])
    parent_gamma = sb("parent_gamma", [P, 1])
    bg0_rows = sb("bg0_rows", [P, KD, NODES])
    lstm_bias = sb("lstm_bias", [P, MAX_SKIP, 2 * GATES])
    b1_col = sb("b1_col", [P, HID0 // P])
    MB = HID2 // P
    bn1_col = sb("bn1_col", [P, 3, MB])
    bn2_col = sb("bn2_col", [P, 3, KD])
    qk3_bias = sb("qk3_bias", [P, 2])
    bv3_col = sb("bv3_col", [P, 1])
    rest_gamma = sb("rest_gamma", [P, 1])
    scal = sb("scal", [P, 2])
    bn1_ss = sb("bn1_ss", [P, 2, MB])
    bn2_ss = sb("bn2_ss", [P, 2, KD])
    minus_half = sb("minus_half", [P, 16])
    eps_tile = sb("eps_tile", [P, TILES])
    bn_mv = sb("bn_mv", [P, MB, 2])
    bn_tmp = sb("bn_tmp", [P, 3, MB])
    SETS = 2 * STREAMS
    ln_stats = sb("ln_stats", [P, SETS, TILES, 6])
    ln_mv = sb("ln_mv", [P, SETS, TILES, 2])
    ln_veps = sb("ln_veps", [P, SETS, TILES])
    ln_rstd = sb("ln_rstd", [P, SETS, TILES])
    ln_shift = sb("ln_shift", [P, SETS, TILES])
    zeros = sb("zeros", [P, TILES])
    NJ = 2 * TILES
    sm_max = sb("sm_max", [P, STREAMS, 2 * NJ])
    sm_sum = sb("sm_sum", [P, STREAMS, 2 * NJ])
    sm_inv = sb("sm_inv", [P, STREAMS, 2 * NJ])

    def region(*pieces):
        at = [0] * len(pieces)

        def take(*dims):
            n = 1
            for x in dims:
                n *= x
            for q, base in enumerate(pieces):
                if at[q] + n <= base.shape[1]:
                    v = base[:, at[q]:at[q] + n]
                    at[q] += n
                    if len(dims) == 2:
                        v = v.rearrange("p (a b) -> p a b", a=dims[0])
                    if len(dims) == 3:
                        v = v.rearrange("p (a b c) -> p a b c", a=dims[0], b=dims[1])
                    if len(dims) == 4:
                        v = v.rearrange("p (a b c d) -> p a b c d", a=dims[0], b=dims[1], c=dims[2])
                    return v
            raise AssertionError((dims, at))

        return take

    H_words = H[:].rearrange("p k b n -> p (k b n)")
    H2_words = H2[:].rearrange("p k b n -> p (k b n)")
    G2 = KD * GROUP

    W0_WORDS = KD * D * 5 + KD * HID0 + (HID0 // P) * D + 9 * D
    w0 = region(H2_words[:, KD * TOKENS - W0_WORDS:])
    Wc, Wq, Wk, Wv, Wo = (w0(KD, D) for _ in range(5))
    W1 = w0(KD, HID0)
    W2 = w0(HID0 // P, D)
    vec0 = w0(9, D)
    bc, g1, be1, bo, g2, be2, b2, g3, be3 = (vec0[:, n, :] for n in range(9))
    w0r = region(R[:])
    Wq_r, Wk_r, Wv_r = (w0r(2, KD, D) for _ in range(3))
    W1_r = w0r(2, KD, HID0)
    buf = region(H_words, H2_words[:, 0:KD * TOKENS - W0_WORDS])
    xs = [buf(G2) for _ in range(STREAMS)]
    splits0 = ((Wq_r, Wq), (Wk_r, Wk), (Wv_r, Wv), (W1_r, W1))
    wg = region(arena[:])
    gcn_raw = wg(2, KD, D)
    bg1 = wg(D)

    st = region(H2_words[:, 2 * 4096:])
    lstm_stage = [[st(KD, GATES * D), st(KD, GATES * D)] for _ in range(2)]
    l2r = region(H2_words[:, 2 * 4096:])
    l2_raw = [l2r(KD, HID2), l2r(MB, D)]
    w3 = region(arena[:])
    Wq3, Wk3, Wv3 = w3(KD, ATT3), w3(KD, ATT3), w3(KD, ATT3)
    Wo3 = w3(D)
    bo3 = w3(D)
    W3_WORDS = 3 * KD * ATT3 + 2 * D

    def tiles_of(v):
        return v.rearrange("p (t d) -> p t d", t=TILES)

    def blocks_of(v):
        return v.rearrange("p (k n) -> p k n", k=KD)

    def half(s, h):
        b = BANKS * s + HALF * h
        return ps[:, b:b + HALF, :].rearrange("p b w -> p (b w)")

    def token_major(s, h, width=D):
        return half(s, h)[:, 0:TILES * width].rearrange("p (t d) -> p t d", t=TILES)

    def feature_major(s, h):
        return blocks_of(half(s, h))

    def squares(s):
        return ps[:, BANKS * s:BANKS * (s + 1), :].rearrange("p b (c n) -> p (b c) n", n=P)

    def over_tiles(v, width=D):
        return v.unsqueeze(1).to_broadcast([P, TILES, width])

    def group_rows(dram):
        return dram.rearrange("(g t p) d -> g p t d", p=P, t=TILES)

    def rows_of_group(view, s, turn):
        return view[bass.ds(turn * STREAMS + s, 1)].rearrange("g p t d -> (g p) t d")

    def columns_of(state, s, turn):
        return state[:, :, bass.ds((turn * STREAMS + s) * GROUP, GROUP)]

    x_rows, out_view = group_rows(t["x"]), group_rows(out_rows)
    state0, state1 = (group_rows(v) for v in state_rows)
    S = range(STREAMS)

    def raw(v):
        return v.bitcast(F32)

    PASSES = ((0, 0), (1, 0), (0, 1))

    def exact_mm(pe, out, lhsT, rhs, start, stop):
        for n, (a, b) in enumerate(PASSES):
            mm = pe.matmul(out, lhsT(a), rhs(b), start=start and n == 0, stop=stop and n == len(PASSES) - 1)
        return mm

    waits_passed = sem("waits_passed")
    small_loaded = sem("small_loaded")
    w0_loaded = sem("w0_loaded")
    gcn_loaded = sem("gcn_loaded")
    xs_loaded = [sem(f"xs_loaded{s}") for s in range(STREAMS)]
    lstm_loaded = [sem(f"lstm_loaded{p}") for p in range(MAX_SKIP)]
    l2_loaded = sem("l2_loaded")
    l3_loaded = sem("l3_loaded")

    def rows(name):
        return t[name].partition_broadcast(P)

    LN_STATS = 2 * TILES - 1

    def ln_statistics(dve, c, y, s, ready):
        for n in range(TILES):
            c.step(dve.bn_stats(ln_stats[:, s, n, :], y[:, n, :]))
        c.settle()
        alone(dve, waits_passed)
        for n in range(TILES):
            ins = dve.bn_aggr(ln_mv[:, s, n, :], ln_stats[:, s, n, :])
            if n < TILES - 1:
                c.step(ins)
        ins.then_inc(ready, 1)

    def ln_reciprocal(pool, c, s, ready, rstd, count):
        pool.wait_ge(ready, count)
        c.step(pool.tensor_tensor(ln_veps[:, s, :], ln_mv[:, s, :, 1], eps_tile[:, 0:TILES], ALU.add))
        c.settle()
        pool.tensor_tensor(ln_rstd[:, s, :], ln_veps[:, s, :], minus_half[:, 0:TILES], ALU.pow).then_inc(rstd, 1)

    LN_SHIFT = 3

    def ln_reciprocal_and_shift(pool, c, s, ready, rstd, count):
        pool.wait_ge(ready, count)
        c.step(pool.tensor_tensor(ln_veps[:, s, :], ln_mv[:, s, :, 1], eps_tile[:, 0:TILES], ALU.add))
        c.step(pool.tensor_tensor(ln_shift[:, s, :], zeros[:], ln_mv[:, s, :, 0], ALU.subtract))
        c.settle()
        c.step(pool.tensor_tensor(ln_rstd[:, s, :], ln_veps[:, s, :], minus_half[:, 0:TILES], ALU.pow))
        c.settle()
        pool.tensor_tensor(ln_shift[:, s, :], ln_shift[:, s, :], ln_rstd[:, s, :], ALU.mult).then_inc(rstd, 1)

    def ln_apply(act, y, s, rstd, count):
        act.wait_ge(rstd, count)
        for n in range(TILES):
            ins = act.activation(y[:, n, :], y[:, n, :], ACT.Identity, bias=ln_shift[:, s, n:n + 1],
                                 scale=ln_rstd[:, s, n:n + 1])
        return ins

    LN_AFFINE = 2 * TILES

    def ln_affine(dve, c, y, s, g, be, ready, rstd, count, ready_count=None):
        dve.wait_ge(ready, count if ready_count is None else ready_count)
        for n in range(TILES):
            c.step(dve.scalar_tensor_tensor(out=y[:, n, :], in0=y[:, n, :], scalar=ln_mv[:, s, n, 0:1], in1=g,
                                            op0=ALU.subtract, op1=ALU.mult))
        c.settle()
        dve.wait_ge(rstd, count)
        for n in range(TILES):
            ins = dve.scalar_tensor_tensor(out=y[:, n, :], in0=y[:, n, :], scalar=ln_rstd[:, s, n:n + 1], in1=be,
                                           op0=ALU.mult, op1=ALU.add)
            if n < TILES - 1:
                c.step(ins)
        return ins

    class Steps:

        def __init__(self, eng, name, per_slot):
            self.per_slot = per_slot
            total = sum(per_slot.values())
            self.chains = [Chain(eng, x, total) for x in sems(name)]

        def enter(self, s, slot, turn):
            c = self.chains[s]
            c.at(turn, sum(n for k, n in self.per_slot.items() if k < slot))
            return c

        def leave(self, s, slot):
            c = self.chains[s]
            want = sum(n for k, n in self.per_slot.items() if k <= slot)
            assert c.n == want, (slot, c.n, want)

    sq = region(arena[:, 2048:])
    adj_bd = sq(P)
    adj2 = sq(NODES)
    lstm_b2 = sq(2, MAX_SKIP, 2 * GATES)
    col = sq(16)
    S64, P64, M64, eye_s = (sq(NODES) for _ in range(4))
    abd, abdT, diag, ddinv = sq(P), sq(P), sq(P), sq(P)
    big = sq(P)

    def ps0(b):
        return ps[:, b, :]

    zeroed = psem("zeroed")
    small_steps = psem("small_steps")
    small_mm = psem("small_mm")
    pool_made = psem("pool_made")
    adj_loaded = psem("adj_loaded")
    deg_ready = psem("deg_ready")
    sq_ready = psem("sq_ready")
    tr_ready = psem("tr_ready")
    sq_steps = psem("sq_steps")
    p_ready = psem("p_ready")
    squared = psem("squared")
    q_ready = psem("q_ready")
    w0_hi = psem("w0_hi")
    pool_steps, sums_asked, spread_asked = psem("pool_steps"), psem("sums_asked"), psem("spread_asked")
    spread_done = psem("spread_done")

    with nc.Block() as block:

        @block.sync
        def _(sp):
            sp.wait_ge(zeroed, 2)
            for g in range(2):
                r = slice(NODES * g, NODES * (g + 1))
                sp.dma_start(adjT[r, r], t["adjT"]).then_inc(adj_loaded, 16)
                sp.dma_start(adj_bd[r, r], t["adj"]).then_inc(adj_loaded, 16)
                sp.dma_start(adj2[r, :], t["adj"]).then_inc(adj_loaded, 16)
            for dst, name in ((lstm_b2[:, 0], "lstm_bih"), (lstm_b2[:, 1], "lstm_bhh"), (b1_col[:], "b1"),
                              (bn1_col[:], "bn1"), (bn2_col[:], "bn2"), (qk3_bias[:], "qk3b"), (col[:, 8:10], "bg0")):
                sp.dma_start(dst, t[name]).then_inc(small_loaded, 16)
            sp.dma_start(bv3_col[:], t["bv3"]).then_inc(small_loaded, 16)
            sp.dma_start(scal[:, 0:1], rows("alpha")).then_inc(small_loaded, 16)
            sp.dma_start(scal[:, 1:2], rows("gamma")).then_inc(small_loaded, 16)
            for dst, name in ((Wc, "Wc"), (Wq, "Wq"), (Wk, "Wk"), (Wv, "Wv"), (Wo, "Wo"), (W1, "W1"), (W2, "W2")):
                sp.dma_start(dst, t[name]).then_inc(w0_loaded, 16)
            for dst, name in ((bc, "bc"), (g1, "g1"), (be1, "be1"), (bo, "bo"), (g2, "g2"), (be2, "be2"),
                              (b2, "b2"), (g3, "g3"), (be3, "be3")):
                sp.dma_start(dst, rows(name)).then_inc(w0_loaded, 16)
            for s in S:
                sp.dma_start(tiles_of(xs[s]), rows_of_group(x_rows, s, 0)).then_inc(xs_loaded[s], 16)
            for dst, name in ((gcn_raw[:, 0], "Wg0"), (gcn_raw[:, 1], "Wg1")):
                sp.dma_start(dst, t[name]).then_inc(gcn_loaded, 16)
            sp.dma_start(bg1, rows("bg1")).then_inc(gcn_loaded, 16)

        @block.gpsimd
        def _(pool):
            pool.memset(adjT[:], 0.0).then_inc(zeroed, 1)
            pool.memset(adj_bd, 0.0).then_inc(zeroed, 1)
            pool.memset(ident[:], 0.0).then_inc(pool_made, 1)
            pool.memset(minus_half[:], -0.5).then_inc(pool_made, 1)
            pool.memset(eps_tile[:], EPS).then_inc(pool_made, 1)
            pool.memset(zeros[:], 0.0).then_inc(pool_made, 1)
            pool.wait_ge(pool_made, 4)
            pool.affine_select(out=ident[:], in_=ident[:], compare_op=ALU.not_equal, fill=1.0, base=0,
                               pattern=[[-1, P]], channel_multiplier=1).then_inc(pool_made, 1)
            pool.memset(ones[:], 1.0).then_inc(pool_made, 1)
            c = Chain(pool, pool_steps)

            def link(ins):
                c.step(ins)
                c.settle()

            pool.wait_ge(adj_loaded, 96)
            pool.wait_ge(pool_made, 6)
            link(pool.tensor_tensor(abd, adj_bd, ident[:], ALU.add))
            link(pool.tensor_tensor(abdT, adjT[:], ident[:], ALU.add))
            link(pool.tensor_tensor(diag, abd, ident[:], ALU.mult))
            pool.sem_inc(sums_asked, 1)
            pool.wait_ge(deg_ready, 1)
            link(pool.tensor_tensor(col[:, 5:6], col[:, 4:5], minus_half[:, 0:1], ALU.pow))
            link(pool.tensor_scalar(abdT, abdT, col[:, 5:6], None, ALU.mult))
            link(pool.tensor_scalar(ddinv, ident[:], col[:, 5:6], None, ALU.mult))
            pool.tensor_scalar(big, ident[:], col[:, 0:1], None, ALU.mult).then_inc(spread_asked, 1)
            pool.wait_ge(small_loaded, 10 * 16)
            link(pool.tensor_scalar(pos_mask[:], adj2, 0.0, None, ALU.is_gt))
            link(pool.tensor_scalar(nz_mask[:], adj2, 0.0, None, ALU.is_equal))
            link(pool.tensor_scalar(nz_neg[:], nz_mask[:], -NEG, None, ALU.mult))
            link(pool.tensor_scalar(nz_mask[:], nz_mask[:], -1.0, 1.0, ALU.mult, ALU.add))
            link(pool.tensor_scalar(alpha_adj[:], adj2, scal[:, 0:1], None, ALU.mult))
            link(pool.tensor_scalar(parent_gamma[:], col[:, 0:1], 0.0, scal[:, 1:2], ALU.is_gt, ALU.mult))
            link(pool.tensor_scalar(rest_gamma[:], parent_gamma[:], -1.0, 1.0, ALU.mult, ALU.add))
            link(pool.tensor_tensor(lstm_bias[:], lstm_b2[:, 0], lstm_b2[:, 1], ALU.add))
            for n, (split, w) in enumerate(splits0):
                pool.wait_ge(w0_hi, n + 1)
                pool.tensor_tensor(split[:, 1], w, raw(split[:, 0]), ALU.subtract)

        @block.scalar
        def _(act):
            act.wait_ge(w0_loaded, 16 * 16)
            for split, w in splits0:
                act.activation(split[:, 0], w, ACT.Copy).then_inc(w0_hi, 1)

        @block.vector
        def _(dve):
            c = Chain(dve, small_steps)

            def link(ins):
                c.step(ins)
                c.settle()

            dve.wait_ge(adj_loaded, 96)
            link(dve.tensor_tensor(S64[0:NODES], adj_bd[0:NODES, 0:NODES], adjT[0:NODES, 0:NODES], ALU.add))
            link(dve.tensor_scalar(S64[0:NODES], S64[0:NODES], 0.5, None, ALU.mult))
            dve.tensor_reduce(col[0:NODES, 6:7], S64[0:NODES], AX_X, ALU.add,
                              apply_absolute_value=True).then_inc(sq_ready, 1)
            dve.wait_ge(pool_made, 6)
            dve.wait_ge(small_mm, 1)
            dve.tensor_reduce(col[0:1, 7:8], ps0(1)[0:1, 0:NODES], AX_X, ALU.max).then_inc(sq_ready, 1)
            dve.wait_ge(small_mm, 2)
            link(dve.tensor_scalar(col[0:NODES, 10:11], ps0(2)[0:NODES, 0:1], 1e-30, None, ALU.max))
            link(dve.tensor_scalar(eye_s[0:NODES], ident[0:NODES, 0:NODES], col[0:NODES, 10:11], None, ALU.mult))
            link(dve.tensor_tensor(P64[0:NODES], S64[0:NODES], eye_s[0:NODES], ALU.add))
            link(dve.reciprocal(col[0:NODES, 11:12], col[0:NODES, 10:11]))
            dve.tensor_scalar(P64[0:NODES], P64[0:NODES], col[0:NODES, 11:12], None, ALU.mult).then_inc(p_ready, 1)
            dve.wait_ge(sums_asked, 1)
            link(dve.tensor_reduce(col[:, 1:2], abd, AX_X, ALU.add))
            link(dve.tensor_reduce(col[:, 2:3], abdT, AX_X, ALU.add))
            link(dve.tensor_reduce(col[:, 3:4], diag, AX_X, ALU.add))
            link(dve.tensor_reduce(col[:, 0:1], adj2, AX_X, ALU.add))
            link(dve.tensor_tensor(col[:, 4:5], col[:, 1:2], col[:, 2:3], ALU.add))
            dve.tensor_tensor(col[:, 4:5], col[:, 4:5], col[:, 3:4], ALU.subtract).then_inc(deg_ready, 1)
            ch = Chain(dve, sq_steps, 2)
            with dve.Fori(0, SQUARINGS // RUN) as i:
                ch.turn(i)
                for r in range(RUN):
                    if r == RUN - 1:
                        dve.wait_ge(p_ready, RUN * i + RUN)
                        ch.step(dve.tensor_tensor(M64[0:NODES], P64[0:NODES], P64[0:NODES], ALU.mult))
                        ch.settle()
                        dve.tensor_reduce(col[0:NODES, 12:13], M64[0:NODES], AX_X, ALU.add).then_inc(q_ready, 1)
                        dve.wait_ge(tr_ready, i + 1)
                        ch.step(dve.reciprocal(col[0:NODES, 13:14], ps0(4)[0:NODES, 0:1]))
                        ch.settle()
                    dve.wait_ge(squared, RUN * i + r + 1)
                    if r < RUN - 1:
                        dve.tensor_copy(P64[0:NODES], ps0(3)[0:NODES, 0:NODES]).then_inc(p_ready, 1)
                    else:
                        dve.tensor_scalar(P64[0:NODES], ps0(3)[0:NODES, 0:NODES], col[0:NODES, 13:14], None,
                                          ALU.mult).then_inc(p_ready, 1)
            ch.end()
            dve.wait_ge(p_ready, SQUARINGS + 1)
            link(dve.tensor_tensor(M64[0:NODES], P64[0:NODES], P64[0:NODES], ALU.mult))
            link(dve.tensor_reduce(col[0:NODES, 15:16], M64[0:NODES], AX_X, ALU.add))
            dve.wait_ge(small_mm, 3)
            link(dve.tensor_tensor(M64[0:NODES], P64[0:NODES], ps0(3)[0:NODES, 0:NODES], ALU.mult))
            dve.tensor_reduce(col[0:NODES, 14:15], M64[0:NODES], AX_X, ALU.add).then_inc(sq_ready, 1)
            dve.wait_ge(small_mm, 4)
            link(dve.reciprocal(col[:, 12:13], ps0(2)[:, 1:2]))
            link(dve.tensor_scalar(col[:, 13:14], ps0(2)[:, 0:1], col[:, 12:13], 1e-8, ALU.mult, ALU.add))
            link(dve.reciprocal(col[:, 12:13], col[:, 13:14]))
            link(dve.tensor_scalar(lnormT[:], adjT[:], 2.0, col[:, 12:13], ALU.mult, ALU.mult))
            link(dve.tensor_tensor(lnormT[:], lnormT[:], ident[:], ALU.subtract))
            dve.wait_ge(small_loaded, 10 * 16)
            dve.wait_ge(spread_done, 1)
            link(dve.tensor_tensor(ahatT[:], abdT, ps0(0)[:, 0:P], ALU.mult))
            for k in range(KD):
                link(dve.tensor_scalar(bg0_rows[:, k, :], ps0(0)[:, P:P + NODES], col[:, 8 + k:9 + k], None,
                                       ALU.mult))

        @block.tensor
        def _(pe):
            pe.wait_ge(sq_ready, 1)
            pe.wait_ge(pool_made, 6)
            pe.transpose(ps0(1)[0:1, 0:NODES], col[0:NODES, 6:7], ident[0:NODES, 0:NODES]).then_inc(small_mm, 1)
            pe.wait_ge(sq_ready, 2)
            pe.matmul(ps0(2)[0:NODES, 0:1], ones[0:1, 0:NODES], col[0:1, 7:8], start=True, stop=True)\
              .then_inc(small_mm, 1)
            with pe.Fori(0, SQUARINGS // RUN) as i:
                for r in range(RUN):
                    pe.wait_ge(p_ready, RUN * i + r + 1)
                    alone(pe, waits_passed)
                    pe.matmul(ps0(3)[0:NODES, 0:NODES], P64[0:NODES], P64[0:NODES], start=True, stop=True)\
                      .then_inc(squared, 1)
                pe.wait_ge(q_ready, i + 1)
                pe.matmul(ps0(4)[:, 0:1], ones[0:NODES, :], col[0:NODES, 12:13],
                          start=True, stop=True).then_inc(tr_ready, 1)
            pe.wait_ge(spread_asked, 1)
            pe.matmul(ps0(0)[:, 0:P], ones[:], ddinv, start=True, stop=True)
            pe.matmul(ps0(0)[:, P:2 * P], ones[:], big, start=True, stop=True).then_inc(spread_done, 1)
            pe.wait_ge(p_ready, SQUARINGS + 1)
            pe.matmul(ps0(3)[0:NODES, 0:NODES], S64[0:NODES], P64[0:NODES], start=True, stop=True)\
              .then_inc(small_mm, 1)
            pe.wait_ge(sq_ready, 3)
            pe.matmul(ps0(2)[:, 0:2], ones[0:NODES, :], col[0:NODES, 14:16], start=True, stop=True)\
              .then_inc(small_mm, 1)

    end_phase()

    xr0, sc_words, hbuf, x1, vt, x1b, x2b = ([buf(G2) for _ in S] for _ in range(7))
    attn_bd = [buf(HEADS * TILES, P) for _ in S]
    attnT = [buf(HEADS * TILES, P) for _ in S]
    xs_t, xr0_t, hb_t, x1_t, v_t, x1b_t, x2b_t = ([tiles_of(v) for v in b]
                                                  for b in (xs, xr0, hbuf, x1, vt, x1b, x2b))
    y_t = x2b_t
    sc = [v.rearrange("p (j m) -> p j m", m=NODES) for v in sc_words]
    zT_f = [blocks_of(v) for v in sc_words]
    pos_bits = pos_mask[:].bitcast(mybir.dt.int32)
    fm = [w0r(2, KD, GROUP) for _ in S]
    flat_at = [v.rearrange("p a b -> p (a b)") for v in attnT]
    qkT = [v.rearrange("p (q k n) -> p q k n", q=2, k=KD) for v in flat_at]
    mT = [v.rearrange("p (m n) -> p m n", m=HID0 // P) for v in flat_at]

    def up_ps(s):
        return ps[:, BANKS * s:BANKS * (s + 1), :].rearrange("p b w -> p (b w)").rearrange(
            "p (m n) -> p m n", m=HID0 // P)

    (xr0_loaded, mixed, mixed_ready, product_done, turned, blank_ready, fm_hi, fm_ready,
     var_ready, rstd_ready, x_ready, biased_ready, qkv_done, qkv_ready, sc_done, sc_ready, exp_ready, at_ready,
     atT_ready, up_done, gelu_ready, var2_ready, rstd2_ready, y_made, yx_ready, y_ready, y_stored) = (sems(n) for n in
                  ("xr0_loaded", "mixed", "mixed_ready", "product_done", "turned", "blank_ready",
                   "fm_hi", "fm_ready", "var_ready", "rstd_ready", "x_ready", "biased_ready",
                   "qkv_done", "qkv_ready", "sc_done", "sc_ready", "exp_ready", "at_ready", "atT_ready",
                   "up_done", "gelu_ready", "var2_ready", "rstd2_ready", "y_made", "yx_ready", "y_ready",
                   "y_stored"))
    bd_zero = psem("bd_zero")
    rows_b = [slice(NODES * b, NODES * (b + 1)) for b in range(2)]
    FM = 2
    plan0 = dict(
        period=88, lead=(0, 13, 19, 31),
        pe={0: 15, 1: 19, 3: 31, 4: 36, 5: 41, 6: 46, 9: 60, 10: 65, 11: 70, 13: 80, 14: 86, 15: 93},
        act={0: 18, 3: 34, 4: 39, 5: 44, 7: 54, 9: 64, 10: 67, 13: 81, 14: 89, 18: 122},
        dve={1: 26, 2: 31, 3: 35, 6: 51, 8: 60, 11: 77, 12: 80, 13: 85, 15: 100, 16: 104, 17: 111},
        pool={1: 29, 3: 45, 5: 47, 11: 78, 13: 80, 15: 104, 16: 108, 17: 119},
        sp={2: 56, 4: 68, 18: 122})

    with nc.Block() as block:

        @block.sync
        def _(sp):
            ahead(sp, y_stored, by=16)

            def stage(s, slot, turn):
                if slot == 2 and not (isinstance(turn, int) and turn == TURNS - 1):
                    sp.wait_ge(x_ready[s], 2 * turn + 1)
                    sp.dma_start(xs_t[s], rows_of_group(x_rows, s, turn + 1)).then_inc(xs_loaded[s], 16)
                if slot == 4:
                    sp.wait_ge(yx_ready[s], turn + 1)
                    sp.dma_start(xr0_t[s], rows_of_group(x_rows, s, turn)).then_inc(xr0_loaded[s], 16)
                if slot == 18:
                    sp.wait_ge(y_ready[s], turn + 1)
                    sp.dma_start(rows_of_group(state0, s, turn), y_t[s]).then_inc(y_stored[s], 16)

            weave(sp, TURNS, plan0, "sp", stage)
            for s in S:
                sp.wait_ge(y_stored[s], 16 * TURNS + 16)
            for s in S:
                sp.wait_ge(product_done[s], 3 * TURNS)
            sp.dma_start(lstm_stage[0][0], t["wih"][0]).then_inc(lstm_loaded[0], 16)

        @block.gpsimd
        def _(pool):
            for s in S:
                pool.memset(attn_bd[s], 0.0).then_inc(bd_zero, 1)
            steps = Steps(pool, "l0_pool", {1: 1, 11: 1})
            tail = Steps(pool, "l0_pool_tail", {15: 1, 17: LN_SHIFT})
            ahead(pool, yx_ready)

            def stage(s, slot, turn):
                for n, at in enumerate((1, 11)):
                    if slot == at:
                        ln_reciprocal(pool, steps.enter(s, slot, turn), s, var_ready[s], rstd_ready[s],
                                      2 * turn + n + 1)
                if slot == 15:
                    ln_reciprocal(pool, tail.enter(s, slot, turn), STREAMS + s, var2_ready[s], rstd2_ready[s],
                                  2 * turn + 3)
                if slot == 17:
                    ln_reciprocal_and_shift(pool, tail.enter(s, slot, turn), STREAMS + s, var2_ready[s],
                                            rstd2_ready[s], 2 * turn + 4)
                if slot == 3:
                    pool.wait_ge(x_ready[s], 2 * turn + 1)
                    pool.tensor_tensor(x1b_t[s], x1_t[s], over_tiles(bo), ALU.add).then_inc(biased_ready[s], 1)
                if slot == 5:
                    pool.memset(sc[s], -NEG).then_inc(blank_ready[s], 1)
                if slot == 13:
                    pool.wait_ge(x_ready[s], 2 * turn + 2)
                    pool.wait_ge(y_stored[s], 16 * turn + 16)
                    pool.tensor_tensor(x2b_t[s], hb_t[s], over_tiles(b2), ALU.add).then_inc(biased_ready[s], 1)
                if slot == 16:
                    pool.wait_ge(y_made[s], turn + 1)
                    pool.wait_ge(xr0_loaded[s], 16 * turn + 16)
                    pool.tensor_tensor(y_t[s], y_t[s], xr0_t[s], ALU.add).then_inc(yx_ready[s], 1)

            weave(pool, TURNS, plan0, "pool", stage)

        @block.scalar
        def _(act):
            def stage(s, slot, turn):
                if slot == 0:
                    act.wait_ge(mixed[s], 2 * turn + 1)
                    act.activation(zT_f[s], feature_major(s, 0), ACT.Copy).then_inc(mixed_ready[s], 1)
                if slot == 3:
                    act.wait_ge(turned[s], 3 * turn + 1)
                    act.activation(fm[s][:, 0], feature_major(s, 0), ACT.Copy).then_inc(fm_hi[s], 1)
                if slot == 4:
                    act.wait_ge(qkv_done[s], 2 * turn + 1)
                    act.activation(qkT[s][:, 0], feature_major(s, 0), ACT.Copy, scale=float(HEAD_DIM) ** -0.5)
                    act.activation(qkT[s][:, 1], feature_major(s, 1), ACT.Copy).then_inc(qkv_ready[s], 1)
                if slot == 5:
                    act.wait_ge(qkv_done[s], 2 * turn + 2)
                    act.activation(v_t[s], token_major(s, 0), ACT.Copy).then_inc(qkv_ready[s], 1)
                if slot == 7:
                    act.wait_ge(sc_ready[s], turn + 1)
                    act.activation(sc[s], sc[s], ACT.Exp).then_inc(exp_ready[s], 1)
                if slot == 9:
                    act.wait_ge(turned[s], 3 * turn + 2)
                    act.activation(attnT[s], squares(s), ACT.Copy).then_inc(atT_ready[s], 1)
                if slot == 10:
                    act.wait_ge(mixed[s], 2 * turn + 2)
                    act.activation(zT_f[s], feature_major(s, 1), ACT.Copy).then_inc(mixed_ready[s], 1)
                if slot == 13:
                    act.wait_ge(turned[s], 3 * turn + 3)
                    act.activation(fm[s][:, 0], feature_major(s, 1), ACT.Copy).then_inc(fm_hi[s], 1)
                if slot == 14:
                    act.wait_ge(up_done[s], turn + 1)
                    for m in range(HID0 // P):
                        ins = act.activation(mT[s][:, m, :], up_ps(s)[:, m, :], ACT.Gelu, bias=b1_col[:, m:m + 1])
                    ins.then_inc(gelu_ready[s], 1)
                if slot == 18:
                    ln_apply(act, y_t[s], STREAMS + s, rstd2_ready[s], 2 * turn + 2).then_inc(y_ready[s], 1)

            weave(act, TURNS, plan0, "act", stage)

        @block.vector
        def _(dve):
            steps = Steps(dve, "l0_dve", {1: 1 + LN_STATS, 2: LN_AFFINE, 6: 4, 8: 2, 11: 1 + LN_STATS,
                                          12: LN_AFFINE - 1})
            tail = Steps(dve, "l0_dve_tail", {15: 1 + LN_STATS, 16: LN_AFFINE - 1, 17: LN_STATS})
            ahead(dve, var2_ready, by=2)
            dve.wait_ge(bd_zero, STREAMS)

            def split_lo(s, count, half):
                dve.wait_ge(fm_hi[s], count)
                dve.tensor_tensor(fm[s][:, 1], feature_major(s, half), raw(fm[s][:, 0]), ALU.subtract)\
                   .then_inc(fm_ready[s], 1)

            def stage(s, slot, turn):
                c = (steps if slot < 15 else tail).enter(s, slot, turn)
                for n, (at, h) in enumerate(((3, 0), (13, 1))):
                    if slot == at:
                        split_lo(s, FM * turn + n + 1, h)
                if slot == 1:
                    dve.wait_ge(product_done[s], 3 * turn + 1)
                    c.step(dve.tensor_tensor(hb_t[s], token_major(s, 1), over_tiles(bc), ALU.add))
                    c.settle()
                    ln_statistics(dve, c, hb_t[s], s, var_ready[s])
                if slot == 2:
                    c.step(ln_affine(dve, c, hb_t[s], s, g1, be1, var_ready[s], rstd_ready[s], 2 * turn + 1))
                    c.settle()
                    dve.wait_ge(xs_loaded[s], 16 * turn + 16)
                    dve.scalar_tensor_tensor(out=x1_t[s], in0=hb_t[s], scalar=0.0, in1=xs_t[s],
                                             op0=ALU.max, op1=ALU.add).then_inc(x_ready[s], 1)
                if slot == 6:
                    dve.wait_ge(blank_ready[s], turn + 1)
                    dve.wait_ge(sc_done[s], turn + 1)
                    alone(dve, waits_passed)
                    full = [P, 2 * NJ, NODES]
                    for r in rows_b:
                        c.step(dve.copy_predicated(sc[s][r], pos_bits[r].unsqueeze(1).to_broadcast(
                            [NODES, 2 * NJ, NODES]), squares(s)[r, :, r]))
                    c.settle()
                    c.step(dve.tensor_reduce(sm_max[:, s, :], sc[s], AX_X, ALU.max))
                    c.settle()
                    c.step(dve.tensor_tensor(sc[s], sc[s], sm_max[:, s, :].unsqueeze(2).to_broadcast(full),
                                             ALU.subtract))
                    c.settle()
                    dve.sem_inc(sc_ready[s], 1)
                if slot == 8:
                    dve.wait_ge(exp_ready[s], turn + 1)
                    c.step(dve.tensor_reduce(sm_sum[:, s, :], sc[s], AX_X, ALU.add))
                    c.settle()
                    c.step(dve.reciprocal(sm_inv[:, s, :], sm_sum[:, s, :]))
                    c.settle()
                    for r in rows_b:
                        dve.tensor_tensor(attn_bd[s][r, :, r], sc[s][r],
                                          sm_inv[r, s, :].unsqueeze(2).to_broadcast([NODES, 2 * NJ, NODES]),
                                          ALU.mult).then_inc(at_ready[s], 1)
                if slot == 11:
                    dve.wait_ge(product_done[s], 3 * turn + 2)
                    dve.wait_ge(biased_ready[s], 2 * turn + 1)
                    c.step(dve.tensor_tensor(hb_t[s], token_major(s, 0), x1b_t[s], ALU.add))
                    c.settle()
                    ln_statistics(dve, c, hb_t[s], s, var_ready[s])
                if slot == 12:
                    ln_affine(dve, c, hb_t[s], s, g2, be2, var_ready[s], rstd_ready[s], 2 * turn + 2)\
                        .then_inc(x_ready[s], 1)
                if slot == 15:
                    dve.wait_ge(product_done[s], 3 * turn + 3)
                    dve.wait_ge(biased_ready[s], 2 * turn + 2)
                    c.step(dve.tensor_tensor(y_t[s], token_major(s, 0), x2b_t[s], ALU.add))
                    c.settle()
                    ln_statistics(dve, c, y_t[s], STREAMS + s, var2_ready[s])
                if slot == 16:
                    ln_affine(dve, c, y_t[s], STREAMS + s, g3, be3, var2_ready[s], rstd2_ready[s],
                              2 * turn + 1, 2 * turn + 3).then_inc(y_made[s], 1)
                if slot == 17:
                    dve.wait_ge(yx_ready[s], turn + 2)
                    ln_statistics(dve, c, y_t[s], STREAMS + s, var2_ready[s])
                (steps if slot < 15 else tail).leave(s, slot)

            weave(dve, TURNS, plan0, "dve", stage)

        @block.tensor
        def _(pe):
            def product(out, src, w, blocks=KD):
                for n in range(TILES):
                    for k in range(blocks):
                        mm = pe.matmul(out[:, n, :], src[:, k, n * P:(n + 1) * P], w[:, k, :],
                                       start=(k == 0), stop=(k == blocks - 1))
                return mm

            def exact_product(out, src, w):
                for n in range(TILES):
                    for k in range(KD):
                        mm = exact_mm(pe, out[:, n, :], lambda q: src[:, q, k, n * P:(n + 1) * P],
                                      lambda q: w[:, q, k, :], k == 0, k == KD - 1)
                return mm

            def product_T(out, w, src, blocks):
                for m in range(blocks):
                    for k in range(KD):
                        mm = exact_mm(pe, out[:, m, :], lambda q: w[:, q, k, m * P:(m + 1) * P],
                                      lambda q: src[:, q, k, :], k == 0, k == KD - 1)
                return mm

            def turn_over(out, src):
                for n in range(TILES):
                    for k in range(KD):
                        mm = pe.transpose(out[:, k, n * P:(n + 1) * P], src[:, n, k * P:(k + 1) * P], ident[:])
                return mm

            def stage(s, slot, turn):
                if slot == 0:
                    pe.wait_ge(xs_loaded[s], 16 * turn + 16)
                    pe.wait_ge(var2_ready[s], 2 * turn + 1)
                    for n in range(TILES):
                        for k in range(KD):
                            mm = pe.matmul(feature_major(s, 0)[:, k, n * P:(n + 1) * P],
                                           xs_t[s][:, n, k * P:(k + 1) * P], lnormT[:], start=True, stop=True)
                    mm.then_inc(mixed[s], 1)
                if slot == 1:
                    pe.wait_ge(mixed_ready[s], 2 * turn + 1)
                    product(token_major(s, 1), zT_f[s], Wc).then_inc(product_done[s], 1)
                if slot == 3:
                    pe.wait_ge(x_ready[s], 2 * turn + 1)
                    turn_over(feature_major(s, 0), x1_t[s]).then_inc(turned[s], 1)
                if slot == 4:
                    pe.wait_ge(fm_ready[s], FM * turn + 1)
                    product_T(feature_major(s, 0), Wq_r, fm[s], KD)
                    product_T(feature_major(s, 1), Wk_r, fm[s], KD).then_inc(qkv_done[s], 1)
                if slot == 5:
                    pe.wait_ge(qkv_ready[s], 2 * turn + 1)
                    exact_product(token_major(s, 0), fm[s], Wv_r).then_inc(qkv_done[s], 1)
                if slot == 6:
                    pe.wait_ge(qkv_ready[s], 2 * turn + 2)
                    for n in range(TILES):
                        q = slice(n * P, (n + 1) * P)
                        for h2 in range(HEADS // 2):
                            for g in range(2):
                                f = slice(HEAD_DIM * g, HEAD_DIM * (g + 1))
                                mm = pe.matmul(squares(s)[:, g * NJ + 2 * n + h2, :], qkT[s][f, 0, h2, q],
                                               qkT[s][f, 1, h2, q], start=True, stop=True)
                    mm.then_inc(sc_done[s], 1)
                if slot == 9:
                    pe.wait_ge(at_ready[s], 2 * turn + 2)
                    for j in range(HEADS * TILES):
                        mm = pe.transpose(squares(s)[:, j, :], attn_bd[s][:, j, :], ident[:])
                    mm.then_inc(turned[s], 1)
                if slot == 10:
                    pe.wait_ge(atT_ready[s], turn + 1)
                    for n in range(TILES):
                        for h in range(HEADS):
                            g, h2 = h % 2, h // 2
                            mm = pe.matmul(feature_major(s, 1)[HEAD_DIM * g:HEAD_DIM * (g + 1), h2,
                                                               n * P:(n + 1) * P],
                                           v_t[s][:, n, HEAD_DIM * h:HEAD_DIM * (h + 1)],
                                           attnT[s][:, g * NJ + 2 * n + h2, :], start=True, stop=True)
                    mm.then_inc(mixed[s], 1)
                if slot == 11:
                    pe.wait_ge(mixed_ready[s], 2 * turn + 2)
                    product(token_major(s, 0), zT_f[s], Wo).then_inc(product_done[s], 1)
                if slot == 13:
                    pe.wait_ge(x_ready[s], 2 * turn + 2)
                    turn_over(feature_major(s, 1), hb_t[s]).then_inc(turned[s], 1)
                if slot == 14:
                    pe.wait_ge(fm_ready[s], FM * turn + 2)
                    product_T(up_ps(s), W1_r, fm[s], HID0 // P).then_inc(up_done[s], 1)
                if slot == 15:
                    pe.wait_ge(gelu_ready[s], turn + 1)
                    product(token_major(s, 0), mT[s], W2, HID0 // P).then_inc(product_done[s], 1)

            weave(pe, TURNS, plan0, "pe", stage)

    end_phase()

    gb = region(H2_words[:, 0:2 * 4096])
    xg, tg, ug = ([gb(G2) for _ in S] for _ in range(3))
    xg_t, ug_t = ([tiles_of(v) for v in b] for b in (xg, ug))
    tg_f = [blocks_of(v) for v in tg]
    gr = region(R[:])
    wg_r = gr(2, 2, KD, D)
    zg = [gr(2, KD, GROUP) for _ in S]
    h1 = [gr(2, KD, GROUP) for _ in S]
    (xg_loaded, ga_done, zg_hi, zg_ready, g0_done, tg_ready, h1_hi, h1_ready, g1_done, ug_ready, gb_done,
     gcn_ready) = (sems(n) for n in ("xg_loaded", "ga_done", "zg_hi", "zg_ready", "g0_done", "tg_ready", "h1_hi",
                                     "h1_ready", "g1_done", "ug_ready", "gb_done", "gcn_ready"))
    wg_hi, wg_ready = psem("wg_hi"), psem("wg_ready")
    plan1 = dict(
        period=32, lead=(0, 2, 7, 8),
        pe={0: 0, 1: 8, 3: 20, 4: 30},
        act={0: 0, 2: 9, 4: 31},
        dve={0: 1, 1: 9, 2: 13, 3: 22},
        sp={3: 22})

    with nc.Block() as block:

        @block.sync
        def _(sp):
            for s in S:
                sp.dma_start(xg_t[s], rows_of_group(state0, s, 0)).then_inc(xg_loaded[s], 16)
            sp.dma_start(lstm_stage[1][0], t["wih"][1]).then_inc(lstm_loaded[1], 16)
            sp.dma_start(lstm_stage[1][1], t["whh"][1]).then_inc(lstm_loaded[1], 16)

            def stage(s, slot, turn):
                if slot == 3 and not (isinstance(turn, int) and turn == TURNS - 1):
                    sp.wait_ge(ga_done[s], turn + 1)
                    sp.dma_start(xg_t[s], rows_of_group(state0, s, turn + 1)).then_inc(xg_loaded[s], 16)

            weave(sp, TURNS, plan1, "sp", stage)

        @block.scalar
        def _(act):
            act.wait_ge(gcn_loaded, 3 * 16)
            act.activation(wg_r[:, 0], gcn_raw, ACT.Copy).then_inc(wg_hi, 1)
            ahead(act, gcn_ready)

            def stage(s, slot, turn):
                if slot == 0:
                    act.wait_ge(ga_done[s], turn + 1)
                    act.activation(zg[s][:, 0], feature_major(s, 0), ACT.Copy).then_inc(zg_hi[s], 1)
                if slot == 2:
                    act.wait_ge(tg_ready[s], KD * turn + KD)
                    act.activation(h1[s][:, 0], tg_f[s], ACT.Relu).then_inc(h1_hi[s], 1)
                if slot == 4:
                    act.wait_ge(gb_done[s], turn + 1)
                    act.activation(columns_of(Hflat, s, turn), feature_major(s, 1), ACT.Relu)\
                       .then_inc(gcn_ready[s], 1)

            weave(act, TURNS, plan1, "act", stage)

        @block.vector
        def _(dve):
            dve.wait_ge(wg_hi, 1)
            dve.tensor_tensor(wg_r[:, 1], gcn_raw, raw(wg_r[:, 0]), ALU.subtract).then_inc(wg_ready, 1)
            ahead(dve, ug_ready)

            def stage(s, slot, turn):
                if slot == 0:
                    dve.wait_ge(zg_hi[s], turn + 1)
                    dve.tensor_tensor(zg[s][:, 1], feature_major(s, 0), raw(zg[s][:, 0]), ALU.subtract)\
                       .then_inc(zg_ready[s], 1)
                if slot == 1:
                    dve.wait_ge(g0_done[s], turn + 1)
                    for k in range(KD):
                        nb = GROUP // NODES
                        by_graph = (tg_f[s][:, k, :], feature_major(s, 1)[:, k, :])
                        o, i = (v.rearrange("p (b n) -> p b n", n=NODES) for v in by_graph)
                        dve.tensor_tensor(o, i, bg0_rows[:, k, :].unsqueeze(1).to_broadcast([P, nb, NODES]),
                                          ALU.add).then_inc(tg_ready[s], 1)
                if slot == 2:
                    dve.wait_ge(h1_hi[s], turn + 1)
                    dve.scalar_tensor_tensor(out=h1[s][:, 1], in0=tg_f[s], scalar=0.0, in1=raw(h1[s][:, 0]),
                                             op0=ALU.max, op1=ALU.subtract).then_inc(h1_ready[s], 1)
                if slot == 3:
                    dve.wait_ge(g1_done[s], turn + 1)
                    dve.tensor_tensor(ug_t[s], token_major(s, 0), over_tiles(bg1), ALU.add).then_inc(ug_ready[s], 1)

            weave(dve, TURNS, plan1, "dve", stage)

        @block.tensor
        def _(pe):
            pe.wait_ge(wg_ready, 1)

            def mix(out, src):
                for n in range(TILES):
                    for k in range(KD):
                        mm = pe.matmul(out[:, k, n * P:(n + 1) * P], src[:, n, k * P:(k + 1) * P], adjT[:],
                                       start=True, stop=True)
                return mm

            def stage(s, slot, turn):
                if slot == 0:
                    pe.wait_ge(xg_loaded[s], 16 * turn + 16)
                    pe.wait_ge(ug_ready[s], turn + 1)
                    mix(feature_major(s, 0), xg_t[s]).then_inc(ga_done[s], 1)
                if slot == 1:
                    pe.wait_ge(zg_ready[s], turn + 1)
                    pe.wait_ge(gcn_ready[s], turn + 1)
                    for m in range(KD):
                        for k in range(KD):
                            mm = exact_mm(pe, feature_major(s, 1)[:, m, :],
                                          lambda q: wg_r[:, q, 0, k, m * P:(m + 1) * P],
                                          lambda q: zg[s][:, q, k, :], k == 0, k == KD - 1)
                    mm.then_inc(g0_done[s], 1)
                if slot == 3:
                    pe.wait_ge(h1_ready[s], turn + 1)
                    for n in range(TILES):
                        for k in range(KD):
                            mm = exact_mm(pe, token_major(s, 0)[:, n, :],
                                          lambda q: h1[s][:, q, k, n * P:(n + 1) * P],
                                          lambda q: wg_r[:, q, 1, k, :], k == 0, k == KD - 1)
                    mm.then_inc(g1_done[s], 1)
                if slot == 4:
                    pe.wait_ge(ug_ready[s], turn + 2)
                    mix(feature_major(s, 1), ug_t[s]).then_inc(gb_done[s], 1)

            weave(pe, TURNS, plan1, "pe", stage)

    end_phase()

    LS = 2
    COLS = 256
    lb = region(H2_words[:, 0:2 * 4096])
    gate = [lb(GATES, KD * COLS) for _ in range(LS)]
    cell = [lb(KD * COLS) for _ in range(LS)]
    hid = [lb(KD * COLS) for _ in range(LS)]
    lr = region(R[:])
    w_r = lr(2, 2, KD, GATES * D)
    xin = [lr(2, KD, COLS) for _ in range(LS)]
    hin = [lr(2, KD, COLS) for _ in range(LS)]
    order = (0, 2, 1, 3)

    def gates_of(j):
        return [q for q in order if not (q == 1 and j == 0)]

    class Skip:

        def __init__(self, p):
            self.p = p
            self.nw = NODES // p
            self.nb = COLS // self.nw
            self.turns = -(-BATCH // (self.nb * LS))
            self.nb_last = (BATCH - self.nb * LS * (self.turns - 1)) // LS
            self.per_turn = sum(len(gates_of(j)) for j in range(p))
            self.stage = lstm_stage[(p - 1) % 2]
            self.parts = [(w, k) for w in range(1 if p == 1 else 2) for k in range(KD)]
            self.gates_done, self.act_done = sems(f"gates_done{p}_", LS), sems(f"act_done{p}_", LS)
            self.x_hi, self.x_ready = sems(f"x_hi{p}_", LS), sems(f"x_ready{p}_", LS)
            self.cell_ready, self.tanh_ready = sems(f"cell_ready{p}_", LS), sems(f"tanh_ready{p}_", LS)
            self.hid_ready, self.steps = sems(f"hid_ready{p}_", LS), sems(f"lstm_steps{p}_", LS)
            self.w_hi, self.w_ready = psem(f"w_hi{p}"), psem(f"w_ready{p}")

        def graphs(self, turn):
            return self.nb_last if isinstance(turn, int) and turn == self.turns - 1 else self.nb

        def window(self, turn, s, j):
            n = self.graphs(turn)
            last = isinstance(turn, int) and turn == self.turns - 1
            first = (self.turns - 1) * LS * self.nb + s * n if last else (turn * LS + s) * self.nb
            return H[:, :, bass.ds(first, n), j:j + self.p * (self.nw - 1) + 1:self.p]

        def as_window(self, v, turn):
            n = self.graphs(turn)
            return v[:, :, 0:n * self.nw].rearrange("p k (b w) -> p k b w", b=n)

        def run(self, eng, step):
            looped = self.turns - 1 if self.nb_last == self.nb else self.turns - 2
            with eng.Fori(0, looped) as i:
                for j in range(self.p):
                    for s in range(LS):
                        step(i, j, s, (i, j + 1) if j < self.p - 1 else (i + 1, 0))
            for turn in range(looped, self.turns):
                for j in range(self.p):
                    for s in range(LS):
                        after = (turn + 1, 0) if turn < self.turns - 1 else None
                        step(turn, j, s, (turn, j + 1) if j < self.p - 1 else after)

        def wait_for_all(self, eng):
            for s in range(LS):
                eng.wait_ge(self.hid_ready[s], self.turns * self.p + 1)

    skips = [Skip(p) for p in range(1, MAX_SKIP + 1)]

    def blocks_at(q, s):
        return blocks_of(gate[s][:, q, :])

    def gate_ps(s, q, m):
        b = q * KD + m
        return ps[:, 4 * s + b // 2, (b % 2) * COLS:(b % 2 + 1) * COLS]

    with nc.Block() as block:

        @block.sync
        def _(sp):
            for skip in skips:
                p, parts = skip.p, skip.parts
                if p in (1, 2):
                    sp.wait_ge(skip.w_ready, len(parts))
                    sp.dma_start(lstm_stage[(p + 1) % 2][0], t["wih"][p + 1]).then_inc(lstm_loaded[p + 1], 16)
                    sp.dma_start(lstm_stage[(p + 1) % 2][1], t["whh"][p + 1]).then_inc(lstm_loaded[p + 1], 16)
                if p == 3:
                    sp.wait_ge(skip.w_ready, len(parts))
                    sp.dma_start(l2_raw[0], t["L2W1"]).then_inc(l2_loaded, 16)
                    sp.dma_start(l2_raw[1], t["L2W2"]).then_inc(l2_loaded, 16)
                    for dst, name in ((Wq3, "Wq3"), (Wk3, "Wk3"), (Wv3, "Wv3"), (Wo3, "Wo3")):
                        sp.dma_start(dst, t[name]).then_inc(l3_loaded, 16)
                    sp.dma_start(bo3, rows("bo3")).then_inc(l3_loaded, 16)

        @block.scalar
        def _(act):
            for skip in skips:
                p, parts = skip.p, skip.parts
                act.wait_ge(lstm_loaded[p - 1], 16 if p == 1 else 32)

                def split_weights(parts):
                    for w, k in parts:
                        act.activation(w_r[:, 0, w, k, :], skip.stage[w][:, k, :], ACT.Copy).then_inc(skip.w_hi, 1)

                def split_x(s, turn, j):
                    act.activation(skip.as_window(xin[s][:, 0], turn), skip.window(turn, s, j), ACT.Copy)\
                       .then_inc(skip.x_hi[s], 1)

                def step(turn, j, s, nxt):
                    done = sum(len(gates_of(jj)) for jj in range(j))
                    act.wait_ge(skip.hid_ready[s], turn * p + j + 1)
                    for n, q in enumerate(gates_of(j)):
                        act.wait_ge(skip.gates_done[s], turn * skip.per_turn + done + n + 1)
                        for m in range(KD):
                            ins = act.activation(blocks_at(q, s)[:, m, :], gate_ps(s, q, m),
                                                 ACT.Tanh if q == 2 else ACT.Sigmoid,
                                                 bias=lstm_bias[:, p - 1, 2 * q + m:2 * q + m + 1])
                        ins.then_inc(skip.act_done[s], 1)
                    act.wait_ge(skip.cell_ready[s], turn * p + j + 1)
                    act.activation(blocks_at(2, s), blocks_of(cell[s]), ACT.Tanh).then_inc(skip.tanh_ready[s], 1)
                    if nxt:
                        split_x(s, *nxt)

                split_weights(parts[:KD])
                if p > 1:
                    skips[p - 2].wait_for_all(act)
                for s in range(LS):
                    split_x(s, 0, 0)
                split_weights(parts[KD:])
                skip.run(act, step)

        @block.vector
        def _(dve):
            for skip in skips:
                p, parts = skip.p, skip.parts

                def split_weights(parts, first):
                    for n, (w, k) in enumerate(parts):
                        dve.wait_ge(skip.w_hi, first + n + 1)
                        dve.tensor_tensor(w_r[:, 1, w, k, :], skip.stage[w][:, k, :], raw(w_r[:, 0, w, k, :]),
                                          ALU.subtract).then_inc(skip.w_ready, 1)

                ahead(dve, skip.hid_ready)
                per_step = [2 if j < p - 1 else 0 for j in range(p)]
                per_step = [n + (2 if j else 0) for j, n in enumerate(per_step)]

                def split_x(s, turn, j):
                    dve.wait_ge(skip.x_hi[s], turn * p + j + 1)
                    dve.tensor_tensor(skip.as_window(xin[s][:, 1], turn), skip.window(turn, s, j),
                                      skip.as_window(raw(xin[s][:, 0]), turn), ALU.subtract)\
                       .then_inc(skip.x_ready[s], 1)

                def step(turn, j, s, nxt):
                    c = Chain(dve, skip.steps[s], sum(per_step))
                    c.at(turn, sum(per_step[:j]))
                    done = sum(len(gates_of(jj)) for jj in range(j))
                    gi, gf, gg, go = (blocks_at(q, s) for q in range(GATES))
                    cl = blocks_of(cell[s])
                    dve.wait_ge(skip.act_done[s], turn * skip.per_turn + done + 2)
                    if j == 0:
                        dve.tensor_tensor(cl, gi, gg, ALU.mult).then_inc(skip.cell_ready[s], 1)
                    else:
                        c.step(dve.tensor_tensor(gi, gi, gg, ALU.mult))
                        dve.wait_ge(skip.act_done[s], turn * skip.per_turn + done + 3)
                        c.step(dve.tensor_tensor(cl, cl, gf, ALU.mult))
                        c.settle()
                        dve.tensor_tensor(cl, cl, gi, ALU.add).then_inc(skip.cell_ready[s], 1)
                    dve.wait_ge(skip.act_done[s], turn * skip.per_turn + done + len(gates_of(j)))
                    dve.wait_ge(skip.tanh_ready[s], turn * p + j + 1)
                    if j < p - 1:
                        h = blocks_of(hid[s])
                        c.step(dve.tensor_tensor(h, go, gg, ALU.mult))
                        c.settle()
                        c.step(dve.tensor_scalar(hin[s][:, 0], h, 1.0, None, ALU.mult))
                        c.settle()
                        dve.tensor_tensor(hin[s][:, 1], h, raw(hin[s][:, 0]), ALU.subtract)\
                           .then_inc(skip.hid_ready[s], 1)
                    else:
                        dve.tensor_tensor(skip.window(turn, s, j), skip.as_window(go, turn),
                                          skip.as_window(gg, turn), ALU.mult)\
                           .then_inc(skip.hid_ready[s], 1)
                    if nxt:
                        split_x(s, *nxt)

                split_weights(parts[:KD], 0)
                for s in range(LS):
                    split_x(s, 0, 0)
                split_weights(parts[KD:], KD)
                skip.run(dve, step)

        @block.tensor
        def _(pe):
            for skip in skips:
                p, parts = skip.p, skip.parts
                pe.wait_ge(skip.w_ready, KD)

                def step(turn, j, s, nxt):
                    if j == 1:
                        pe.wait_ge(skip.w_ready, len(parts))
                    pe.wait_ge(skip.x_ready[s], turn * p + j + 1)
                    pe.wait_ge(skip.hid_ready[s], turn * p + j + 1)
                    for q in gates_of(j):
                        for m in range(KD):
                            f = slice((q * KD + m) * P, (q * KD + m + 1) * P)
                            operands = [(0, xin, k) for k in range(KD)] + [(1, hin, k) for k in range(KD) if j]
                            for n, (w, src, k) in enumerate(operands):
                                mm = exact_mm(pe, gate_ps(s, q, m), lambda a: w_r[:, a, w, k, f],
                                              lambda a: src[s][:, a, k, :], n == 0, n == len(operands) - 1)
                        mm.then_inc(skip.gates_done[s], 1)

                skip.run(pe, step)

    end_phase()

    cb = region(arena[:, W3_WORDS:])
    hs, ys = ([cb(G2) for _ in S] for _ in range(2))
    hs_f = [blocks_of(v) for v in hs]
    ys_t = [tiles_of(v) for v in ys]
    bn_stats1 = cb(MB, STREAMS * TURNS * 6)
    cr = region(R[:])
    l2w1_r = cr(2, KD, HID2)
    l2w2_r = cr(2, MB, D)
    ag = [cr(2, KD, GROUP) for _ in S]
    (hs_ready, ys_loaded, h_turned, l1_var, l1_rstd, l1_ready, l1_stored, g2_done, ag_hi, ag_ready, up2_done,
     h2_kept, st_taken) = (sems(n) for n in
                           ("hs_ready", "ys_loaded", "h_turned", "l1_var", "l1_rstd", "l1_ready", "l1_stored",
                            "g2_done", "ag_hi", "ag_ready", "up2_done", "h2_kept", "st_taken"))
    l2_hi, l2_ready, bn1_var, bn1_pow, bn_steps = (psem(n) for n in ("l2_hi", "l2_ready", "bn1_var", "bn1_pow",
                                                                     "bn_steps"))
    plan2 = dict(
        period=48, lead=(0, 13, 21, 30),
        pe={1: 1, 3: 21, 4: 35},
        act={0: 0, 2: 17, 3: 26, 4: 42},
        dve={1: 3, 3: 26, 5: 47},
        pool={1: 7},
        sp={3: 24, 5: 36})

    def fold_batch_norm(dve, c, stats, cols, ss, blocks, ready, made, biased):
        for m in range(blocks):
            c.step(dve.bn_aggr(bn_mv[:, m, :], stats[:, m, :]))
        c.settle()
        mv = bn_mv[:, 0:blocks, :]
        if biased:
            c.step(dve.tensor_scalar(bn_tmp[:, 0, 0:blocks], mv[:, :, 0], -1.0, None, ALU.mult))
        else:
            c.step(dve.tensor_tensor(bn_tmp[:, 0, 0:blocks], mv[:, :, 0], cols[:, 0, :], ALU.add))
        c.step(dve.tensor_scalar(bn_tmp[:, 1, 0:blocks], mv[:, :, 1], EPS, None, ALU.add))
        c.settle()
        dve.sem_inc(ready, 1)
        if not biased:
            c.step(dve.tensor_tensor(bn_tmp[:, 0, 0:blocks], cols[:, 0, :], bn_tmp[:, 0, 0:blocks], ALU.subtract))
            c.settle()
        dve.wait_ge(made, 1)
        c.step(dve.tensor_tensor(ss[:, 0, :], bn_tmp[:, 2, 0:blocks], cols[:, 1, :], ALU.mult))
        c.settle()
        c.step(dve.tensor_tensor(bn_tmp[:, 0, 0:blocks], bn_tmp[:, 0, 0:blocks], ss[:, 0, :], ALU.mult))
        c.settle()
        c.step(dve.tensor_tensor(ss[:, 1, :], bn_tmp[:, 0, 0:blocks], cols[:, 2, :], ALU.add))
        c.settle()

    with nc.Block() as block:

        @block.sync
        def _(sp):
            for s in S:
                sp.dma_start(ys_t[s], rows_of_group(state0, s, 0)).then_inc(ys_loaded[s], 16)

            def stage(s, slot, turn):
                if slot == 3:
                    sp.wait_ge(l1_ready[s], turn + 1)
                    sp.dma_start(rows_of_group(state1, s, turn), ys_t[s]).then_inc(l1_stored[s], 16)
                if slot == 5 and not (isinstance(turn, int) and turn == TURNS - 1):
                    sp.wait_ge(l1_stored[s], 16 * turn + 16)
                    alone(sp, waits_passed)
                    sp.wait_ge(g2_done[s], turn + 1)
                    sp.dma_start(ys_t[s], rows_of_group(state0, s, turn + 1)).then_inc(ys_loaded[s], 16)

            weave(sp, TURNS, plan2, "sp", stage)
            for s in S:
                sp.wait_ge(l1_stored[s], 16 * TURNS)

        @block.gpsimd
        def _(pool):
            steps = Steps(pool, "p7_pool", {1: LN_SHIFT})

            def stage(s, slot, turn):
                if slot == 1:
                    ln_reciprocal_and_shift(pool, steps.enter(s, slot, turn), s, l1_var[s], l1_rstd[s], turn + 1)

            weave(pool, TURNS, plan2, "pool", stage)
            pool.wait_ge(bn1_var, 1)
            pool.tensor_tensor(bn_tmp[:, 2, 0:MB], bn_tmp[:, 1, 0:MB], minus_half[:, 0:MB], ALU.pow)\
                .then_inc(bn1_pow, 1)

        @block.scalar
        def _(act):
            act.wait_ge(l2_loaded, 32)
            act.activation(l2w1_r[:, 0], l2_raw[0], ACT.Copy).then_inc(l2_hi, 1)
            act.activation(l2w2_r[:, 0], l2_raw[1], ACT.Copy).then_inc(l2_hi, 1)
            act.wait_ge(l2_ready, 2)
            ahead(act, h2_kept, by=2)

            def stage(s, slot, turn):
                if slot == 0:
                    act.wait_ge(h_turned[s], turn + 1)
                    act.activation(hs_f[s], columns_of(Hflat, s, turn), ACT.Copy).then_inc(hs_ready[s], 1)
                if slot == 2:
                    ln_apply(act, ys_t[s], s, l1_rstd[s], turn + 1).then_inc(l1_ready[s], 1)
                if slot == 3:
                    act.wait_ge(g2_done[s], turn + 1)
                    act.activation(ag[s][:, 0], feature_major(s, 1), ACT.Copy).then_inc(ag_hi[s], 1)
                if slot == 4:
                    act.wait_ge(up2_done[s], turn + 1)
                    alone(act, waits_passed)
                    act.activation(columns_of(Hflat, s, turn), feature_major(s, 0), ACT.Copy).then_inc(h2_kept[s], 1)
                    act.activation(columns_of(H2flat, s, turn), feature_major(s, 1), ACT.Copy)\
                       .then_inc(h2_kept[s], 1)

            weave(act, TURNS, plan2, "act", stage)

        @block.vector
        def _(dve):
            for q, w in enumerate((l2w1_r, l2w2_r)):
                dve.wait_ge(l2_hi, q + 1)
                dve.tensor_tensor(w[:, 1], l2_raw[q], raw(w[:, 0]), ALU.subtract).then_inc(l2_ready, 1)
            steps = Steps(dve, "p7_dve", {1: 1 + LN_STATS})

            def stage(s, slot, turn):
                c = steps.enter(s, slot, turn)
                if slot == 1:
                    dve.wait_ge(h_turned[s], turn + 2)
                    dve.wait_ge(ys_loaded[s], 16 * turn + 16)
                    c.step(dve.tensor_tensor(ys_t[s], token_major(s, 0), ys_t[s], ALU.add))
                    c.settle()
                    ln_statistics(dve, c, ys_t[s], s, l1_var[s])
                if slot == 3:
                    dve.wait_ge(ag_hi[s], turn + 1)
                    dve.tensor_tensor(ag[s][:, 1], feature_major(s, 1), raw(ag[s][:, 0]), ALU.subtract)\
                       .then_inc(ag_ready[s], 1)
                if slot == 5:
                    for h, state in enumerate((Hflat, H2flat)):
                        dve.wait_ge(h2_kept[s], 2 * turn + h + 3)
                        for m in range(KD):
                            dve.bn_stats(bn_stats1[:, KD * h + m, bass.ds((turn * STREAMS + s) * 6, 6)],
                                         columns_of(state, s, turn)[:, m, :]).then_inc(st_taken[s], 1)

            weave(dve, TURNS, plan2, "dve", stage)
            for s in S:
                dve.wait_ge(st_taken[s], MB * TURNS)
            fold_batch_norm(dve, Chain(dve, bn_steps), bn_stats1, bn1_col, bn1_ss, MB, bn1_var, bn1_pow, False)

        @block.tensor
        def _(pe):
            pe.wait_ge(l2_ready, 2)
            ahead(pe, h_turned)

            def stage(s, slot, turn):
                if slot == 1:
                    pe.wait_ge(hs_ready[s], turn + 1)
                    pe.wait_ge(h2_kept[s], 2 * turn + 2)
                    for n in range(TILES):
                        for k in range(KD):
                            mm = pe.transpose(token_major(s, 0)[:, n, k * P:(k + 1) * P],
                                              hs_f[s][:, k, n * P:(n + 1) * P], ident[:])
                    mm.then_inc(h_turned[s], 1)
                if slot == 3:
                    pe.wait_ge(l1_ready[s], turn + 1)
                    for n in range(TILES):
                        for k in range(KD):
                            mm = pe.matmul(feature_major(s, 1)[:, k, n * P:(n + 1) * P],
                                           ys_t[s][:, n, k * P:(k + 1) * P], ahatT[:], start=True, stop=True)
                    mm.then_inc(g2_done[s], 1)
                if slot == 4:
                    pe.wait_ge(ag_ready[s], turn + 1)
                    for m in range(MB):
                        for k in range(KD):
                            mm = exact_mm(pe, feature_major(s, m // KD)[:, m % KD, :],
                                          lambda q: l2w1_r[:, q, k, m * P:(m + 1) * P],
                                          lambda q: ag[s][:, q, k, :], k == 0, k == KD - 1)
                    mm.then_inc(up2_done[s], 1)

            weave(pe, TURNS, plan2, "pe", stage)

    end_phase()

    eb = region(arena[:, W3_WORDS:])
    rf32 = [eb(MB, GROUP) for _ in S]
    bn_stats2 = eb(KD, STREAMS * TURNS * 6)
    er = region(R[:, 2 * KD * HID2 + 2 * MB * D:])
    rr = [er(2, MB, GROUP) for _ in S]
    (r_ready, r_split, dn2_done, out2_ready, st2_taken) = (sems(n) for n in
                                                           ("r_ready", "r_split", "dn2_done", "out2_ready",
                                                            "st2_taken"))
    bn2_var, bn2_pow, bn_steps2 = psem("bn2_var"), psem("bn2_pow"), psem("bn_steps2")
    plan3 = dict(
        period=24, lead=(0, 10, 15, 20),
        pe={2: 3},
        act={0: 0, 2: 22},
        dve={1: 2, 3: 22})

    with nc.Block() as block:

        @block.gpsimd
        def _(pool):
            pool.wait_ge(bn2_var, 1)
            pool.tensor_tensor(bn_tmp[:, 2, 0:KD], bn_tmp[:, 1, 0:KD], minus_half[:, 0:KD], ALU.pow)\
                .then_inc(bn2_pow, 1)

        @block.scalar
        def _(act):
            ahead(act, out2_ready)

            def stage(s, slot, turn):
                if slot == 0:
                    act.wait_ge(r_split[s], turn + 1)
                    for m in range(MB):
                        state = (Hflat, H2flat)[m // KD]
                        ins = act.activation(rf32[s][:, m, :], columns_of(state, s, turn)[:, m % KD, :], ACT.Relu,
                                             bias=bn1_ss[:, 1, m:m + 1], scale=bn1_ss[:, 0, m:m + 1])
                    ins.then_inc(r_ready[s], 1)
                if slot == 2:
                    act.wait_ge(dn2_done[s], turn + 2)
                    alone(act, waits_passed)
                    for m in range(KD):
                        ins = act.activation(columns_of(Hflat, s, turn)[:, m, :], feature_major(s, 0)[:, m, :],
                                             ACT.Identity, bias=bn2_col[:, 0, m:m + 1])
                    ins.then_inc(out2_ready[s], 1)

            weave(act, TURNS, plan3, "act", stage)

        @block.vector
        def _(dve):
            steps = Steps(dve, "p8_dve", {1: 1})
            ahead(dve, r_split)

            def stage(s, slot, turn):
                c = steps.enter(s, slot, turn)
                if slot == 1:
                    dve.wait_ge(r_ready[s], turn + 1)
                    dve.wait_ge(dn2_done[s], turn + 1)
                    c.step(dve.tensor_scalar(rr[s][:, 0], rf32[s], 1.0, None, ALU.mult))
                    c.settle()
                    dve.tensor_tensor(rr[s][:, 1], rf32[s], raw(rr[s][:, 0]), ALU.subtract).then_inc(r_split[s], 1)
                if slot == 3:
                    dve.wait_ge(out2_ready[s], turn + 2)
                    for m in range(KD):
                        dve.bn_stats(bn_stats2[:, m, bass.ds((turn * STREAMS + s) * 6, 6)],
                                     columns_of(Hflat, s, turn)[:, m, :]).then_inc(st2_taken[s], 1)

            weave(dve, TURNS, plan3, "dve", stage)
            for s in S:
                dve.wait_ge(st2_taken[s], KD * TURNS)
            fold_batch_norm(dve, Chain(dve, bn_steps2), bn_stats2, bn2_col, bn2_ss, KD, bn2_var, bn2_pow, True)

        @block.tensor
        def _(pe):
            ahead(pe, dn2_done)

            def stage(s, slot, turn):
                if slot == 2:
                    pe.wait_ge(r_split[s], turn + 2)
                    pe.wait_ge(out2_ready[s], turn + 1)
                    for m in range(KD):
                        for k in range(MB):
                            mm = exact_mm(pe, feature_major(s, 0)[:, m, :],
                                          lambda q: l2w2_r[:, q, k, m * P:(m + 1) * P],
                                          lambda q: rr[s][:, q, k, :], k == 0, k == MB - 1)
                    mm.then_inc(dn2_done[s], 1)

            weave(pe, TURNS, plan3, "pe", stage)

    end_phase()

    db = region(H2_words)
    x3, xT3, x3b, xr = ([db(G2) for _ in S] for _ in range(4))
    qk3 = [db(2, GROUP) for _ in S]
    v3 = [db(TILES, ATT3) for _ in S]
    at3 = [db(TILES, NODES) for _ in S]
    bd3 = [db(TILES, P) for _ in S]
    atT3 = [db(TILES, P) for _ in S]
    hs3 = [db(KD, GROUP) for _ in S]
    rf_t = [tiles_of(v.rearrange("p a n -> p (a n)")) for v in qk3]
    x3_t, x3b_t, xr_t, y3_t = ([tiles_of(v) for v in b] for b in (x3, x3b, xr, xT3))
    xT3_f = [blocks_of(v) for v in xT3]
    (xr_loaded, hn_ready, h9_turned, var9, rstd9, x3_ready, x3b_ready, x3_turned, xT3_ready, qk3_done, qk3_ready,
     v3_done, v3_ready, sc3_done, sc3_ready, exp3_ready, at3_ready, at3_turned, atT3_ready, o3_done, o3T_ready,
     wo3_done, rf_ready, child_done, y3_ready, stored) = (sems("l3_" + n) for n in
                                                          ("xr", "hn", "ht", "var", "rstd", "x3", "x3b", "xt",
                                                           "xT", "qkd", "qkr", "vd", "vr", "scd", "scr", "exr",
                                                           "atr", "att", "atT", "od", "oT", "wod", "rfr", "chd",
                                                           "y3", "stored"))
    rest_made, rest_ready = sems("l3_rest_made"), sems("l3_rest_ready")
    var9b, rstd9b = sems("l3_var_b"), sems("l3_rstd_b")
    bd3_zero = psem("bd3_zero")
    plan4 = dict(
        period=34, lead=(0, 8, 17, 26),
        pe={1: 19, 3: 28, 4: 30, 5: 32, 6: 35, 9: 42, 10: 44, 11: 46, 12: 48},
        act={0: 8, 2: 27, 3: 29, 4: 34, 5: 38, 7: 38, 9: 43, 10: 45, 11: 48, 13: 57},
        dve={1: 23, 6: 35, 8: 42, 11: 47, 12: 51},
        pool={1: 23, 3: 28, 11: 48, 12: 51},
        sp={10: 33, 13: 57})

    with nc.Block() as block:

        @block.sync
        def _(sp):
            ahead(sp, stored, by=16)
            for s in S:
                sp.dma_start(xr_t[s], rows_of_group(state1, s, 0)).then_inc(xr_loaded[s], 16)

            def stage(s, slot, turn):
                if slot == 10 and not (isinstance(turn, int) and turn == TURNS - 1):
                    sp.wait_ge(var9[s], turn + 1)
                    sp.dma_start(xr_t[s], rows_of_group(state1, s, turn + 1)).then_inc(xr_loaded[s], 16)
                if slot == 13:
                    sp.wait_ge(y3_ready[s], turn + 1)
                    sp.dma_start(rows_of_group(out_view, s, turn), y3_t[s]).then_inc(stored[s], 16)

            weave(sp, TURNS, plan4, "sp", stage)
            for s in S:
                sp.wait_ge(stored[s], 16 * TURNS + 16)

        @block.gpsimd
        def _(pool):
            for s in S:
                pool.memset(bd3[s], 0.0).then_inc(bd3_zero, 1)
            steps, tail = Steps(pool, "p9_pool", {1: LN_SHIFT}), Steps(pool, "p9_pool_tail", {12: LN_SHIFT})

            def stage(s, slot, turn):
                if slot == 1:
                    ln_reciprocal_and_shift(pool, steps.enter(s, slot, turn), s, var9[s], rstd9[s], turn + 1)
                if slot == 12:
                    ln_reciprocal_and_shift(pool, tail.enter(s, slot, turn), STREAMS + s, var9b[s], rstd9b[s],
                                            turn + 1)
                if slot == 3:
                    pool.wait_ge(x3_ready[s], turn + 1)
                    pool.tensor_tensor(x3b_t[s], x3_t[s], over_tiles(bo3), ALU.add).then_inc(x3b_ready[s], 1)
                if slot == 11:
                    pool.wait_ge(rest_made[s], turn + 1)
                    pool.tensor_tensor(x3b_t[s], x3b_t[s], x3_t[s], ALU.add).then_inc(rest_ready[s], 1)

            weave(pool, TURNS, plan4, "pool", stage)

        @block.scalar
        def _(act):
            def stage(s, slot, turn):
                if slot == 0:
                    act.wait_ge(h9_turned[s], turn + 1)
                    for m in range(KD):
                        ins = act.activation(hs3[s][:, m, :], columns_of(Hflat, s, turn)[:, m, :],
                                             ACT.Identity, bias=bn2_ss[:, 1, m:m + 1], scale=bn2_ss[:, 0, m:m + 1])
                    ins.then_inc(hn_ready[s], 1)
                if slot == 2:
                    ln_apply(act, x3_t[s], s, rstd9[s], turn + 1).then_inc(x3_ready[s], 1)
                if slot == 3:
                    act.wait_ge(x3_turned[s], turn + 1)
                    act.wait_ge(stored[s], 16 * turn + 16)
                    act.activation(xT3_f[s], feature_major(s, 1), ACT.Copy).then_inc(xT3_ready[s], 1)
                if slot == 4:
                    act.wait_ge(qk3_done[s], turn + 1)
                    for m in range(2):
                        ins = act.activation(qk3[s][:, m, :], feature_major(s, 0)[:, m, :], ACT.Identity,
                                             bias=qk3_bias[:, m:m + 1])
                    ins.then_inc(qk3_ready[s], 1)
                if slot == 5:
                    act.wait_ge(v3_done[s], turn + 1)
                    act.activation(v3[s], token_major(s, 1, ATT3), ACT.Copy).then_inc(v3_ready[s], 1)
                if slot == 7:
                    act.wait_ge(sc3_ready[s], turn + 1)
                    act.activation(at3[s], at3[s], ACT.Exp).then_inc(exp3_ready[s], 1)
                if slot == 9:
                    act.wait_ge(at3_turned[s], turn + 1)
                    act.activation(atT3[s], token_major(s, 0, P), ACT.Copy).then_inc(atT3_ready[s], 1)
                if slot == 10:
                    act.wait_ge(o3_done[s], turn + 1)
                    act.activation(atT3[s], token_major(s, 1, P), ACT.Identity, bias=bv3_col[:, 0:1])\
                       .then_inc(o3T_ready[s], 1)
                if slot == 11:
                    act.wait_ge(rf_ready[s], turn + 2)
                    act.activation(x3b_t[s], rf_t[s], ACT.Copy, scale=rest_gamma[:, 0:1])\
                       .then_inc(rest_made[s], 1)
                if slot == 13:
                    ln_apply(act, y3_t[s], STREAMS + s, rstd9b[s], turn + 1).then_inc(y3_ready[s], 1)

            weave(act, TURNS, plan4, "act", stage)

        @block.vector
        def _(dve):
            dve.wait_ge(bd3_zero, STREAMS)
            steps = Steps(dve, "p9_dve", {1: 1 + LN_STATS, 6: 6, 8: 2})
            tail = Steps(dve, "p9_dve_tail", {12: 1 + LN_STATS})
            ahead(dve, rf_ready)
            rows_b = [slice(NODES * b, NODES * (b + 1)) for b in range(2)]

            def stage(s, slot, turn):
                c = (steps if slot < 12 else tail).enter(s, slot, turn)
                if slot == 1:
                    dve.wait_ge(h9_turned[s], turn + 2)
                    dve.wait_ge(xr_loaded[s], 16 * turn + 16)
                    c.step(dve.tensor_tensor(x3_t[s], token_major(s, 0), xr_t[s], ALU.add))
                    c.settle()
                    ln_statistics(dve, c, x3_t[s], s, var9[s])
                if slot == 6:
                    dve.wait_ge(sc3_done[s], turn + 1)
                    full = [P, TILES, NODES]

                    def spread(v):
                        return v.unsqueeze(1).to_broadcast(full)

                    for r in rows_b:
                        c.step(dve.scalar_tensor_tensor(out=at3[s][r], in0=token_major(s, 0, P)[r, :, r],
                                                        scalar=float(ATT3) ** -0.5,
                                                        in1=alpha_adj[r].unsqueeze(1).to_broadcast(
                                                            [NODES, TILES, NODES]),
                                                        op0=ALU.mult, op1=ALU.add))
                    c.settle()
                    c.step(dve.tensor_tensor(at3[s], at3[s], spread(nz_mask[:]), ALU.mult))
                    c.settle()
                    c.step(dve.tensor_tensor(at3[s], at3[s], spread(nz_neg[:]), ALU.add))
                    c.settle()
                    c.step(dve.tensor_reduce(sm_max[:, s, 0:TILES], at3[s], AX_X, ALU.max))
                    c.settle()
                    c.step(dve.tensor_tensor(at3[s], at3[s], sm_max[:, s, 0:TILES].unsqueeze(2).to_broadcast(full),
                                             ALU.subtract))
                    c.settle()
                    dve.sem_inc(sc3_ready[s], 1)
                if slot == 8:
                    dve.wait_ge(exp3_ready[s], turn + 1)
                    c.step(dve.tensor_reduce(sm_sum[:, s, 0:TILES], at3[s], AX_X, ALU.add))
                    c.settle()
                    c.step(dve.reciprocal(sm_inv[:, s, 0:TILES], sm_sum[:, s, 0:TILES]))
                    c.settle()
                    for r in rows_b:
                        dve.tensor_tensor(bd3[s][r, :, r], at3[s][r],
                                          sm_inv[r, s, 0:TILES].unsqueeze(2).to_broadcast([NODES, TILES, NODES]),
                                          ALU.mult).then_inc(at3_ready[s], 1)
                if slot == 11:
                    dve.wait_ge(wo3_done[s], turn + 1)
                    dve.wait_ge(x3b_ready[s], turn + 1)
                    dve.tensor_tensor(rf_t[s], token_major(s, 0), x3b_t[s], ALU.add).then_inc(rf_ready[s], 1)
                if slot == 12:
                    dve.wait_ge(child_done[s], turn + 1)
                    dve.wait_ge(rest_ready[s], turn + 1)
                    c.step(dve.scalar_tensor_tensor(out=y3_t[s], in0=token_major(s, 1), scalar=parent_gamma[:, 0:1],
                                                    in1=x3b_t[s], op0=ALU.mult, op1=ALU.add))
                    c.settle()
                    ln_statistics(dve, c, y3_t[s], STREAMS + s, var9b[s])
                (steps if slot < 12 else tail).leave(s, slot)

            weave(dve, TURNS, plan4, "dve", stage)

        @block.tensor
        def _(pe):
            pe.wait_ge(l3_loaded, 5 * 16)
            ahead(pe, h9_turned)

            def stage(s, slot, turn):
                if slot == 1:
                    pe.wait_ge(hn_ready[s], turn + 1)
                    pe.wait_ge(rf_ready[s], turn + 1)
                    for n in range(TILES):
                        for k in range(KD):
                            mm = pe.transpose(token_major(s, 0)[:, n, k * P:(k + 1) * P],
                                              hs3[s][:, k, n * P:(n + 1) * P], ident[:])
                    mm.then_inc(h9_turned[s], 1)
                if slot == 3:
                    pe.wait_ge(x3_ready[s], turn + 1)
                    for n in range(TILES):
                        for k in range(KD):
                            mm = pe.transpose(feature_major(s, 1)[:, k, n * P:(n + 1) * P],
                                              x3_t[s][:, n, k * P:(k + 1) * P], ident[:])
                    mm.then_inc(x3_turned[s], 1)
                if slot == 4:
                    pe.wait_ge(xT3_ready[s], turn + 1)
                    for m, w in enumerate((Wq3, Wk3)):
                        for k in range(KD):
                            mm = pe.matmul(feature_major(s, 0)[:, m, :], w[:, k, :], xT3_f[s][:, k, :],
                                           start=(k == 0), stop=(k == KD - 1))
                    mm.then_inc(qk3_done[s], 1)
                if slot == 5:
                    for n in range(TILES):
                        for k in range(KD):
                            mm = pe.matmul(token_major(s, 1, ATT3)[:, n, :], xT3_f[s][:, k, n * P:(n + 1) * P],
                                           Wv3[:, k, :], start=(k == 0), stop=(k == KD - 1))
                    mm.then_inc(v3_done[s], 1)
                if slot == 6:
                    pe.wait_ge(qk3_ready[s], turn + 1)
                    for n in range(TILES):
                        q = slice(n * P, (n + 1) * P)
                        mm = pe.matmul(token_major(s, 0, P)[:, n, :], qk3[s][:, 0, q], qk3[s][:, 1, q],
                                       start=True, stop=True)
                    mm.then_inc(sc3_done[s], 1)
                if slot == 9:
                    pe.wait_ge(at3_ready[s], 2 * turn + 2)
                    for n in range(TILES):
                        mm = pe.transpose(token_major(s, 0, P)[:, n, :], bd3[s][:, n, :], ident[:])
                    mm.then_inc(at3_turned[s], 1)
                if slot == 10:
                    pe.wait_ge(atT3_ready[s], turn + 1)
                    pe.wait_ge(v3_ready[s], turn + 1)
                    for n in range(TILES):
                        mm = pe.matmul(token_major(s, 1, P)[:, n, :], v3[s][:, n, :], atT3[s][:, n, :],
                                       start=True, stop=True)
                    mm.then_inc(o3_done[s], 1)
                if slot == 11:
                    pe.wait_ge(o3T_ready[s], turn + 1)
                    for n in range(TILES):
                        mm = pe.matmul(token_major(s, 0)[:, n, :], atT3[s][:, n, :], Wo3[:], start=True, stop=True)
                    mm.then_inc(wo3_done[s], 1)
                if slot == 12:
                    pe.wait_ge(rf_ready[s], turn + 2)
                    for n in range(TILES):
                        mm = pe.matmul(token_major(s, 1)[:, n, :], adjT[:], rf_t[s][:, n, :], start=True, stop=True)
                    mm.then_inc(child_done[s], 1)

            weave(pe, TURNS, plan4, "pe", stage)


def kernel(**inputs):
    import numpy as np
    import concourse.bacc as bacc
    from concourse.bass_utils import run_bass_kernel_spmd

    a = {k: np.asarray(v) for k, v in inputs.items()}

    def split_rows(w):
        return w.reshape(-1, 128, w.shape[-1]).transpose(1, 0, 2)

    def columns(v):
        return v.reshape(-1, 128).T

    lay = {"x": a["x"].reshape(-1, a["x"].shape[-1]), "adj": a["adj"], "adjT": a["adj"].T}
    for n in ("Wc", "Wq", "Wk", "Wv", "Wo", "W1", "W2"):
        lay[n] = split_rows(a["L0_gnn_" + n])
    for n in ("bc", "g1", "be1", "bo", "g2", "be2", "b2", "g3", "be3"):
        lay[n] = a["L0_gnn_" + n]
    lay["b1"] = columns(a["L0_gnn_b1"])
    lay["Wg0"], lay["Wg1"] = split_rows(a["L1_gnn_Wg0"]), split_rows(a["L1_gnn_Wg1"])
    lay["bg0"], lay["bg1"] = columns(a["L1_gnn_bg0"]), a["L1_gnn_bg1"]
    lay["wih"] = np.stack([split_rows(w.T) for w in a["L1_gnn_Wih"]])
    lay["whh"] = np.stack([split_rows(w.T) for w in a["L1_gnn_Whh"]])
    lay["lstm_bih"] = a["L1_gnn_bih"].reshape(4, 8, 128).transpose(2, 0, 1)
    lay["lstm_bhh"] = a["L1_gnn_bhh"].reshape(4, 8, 128).transpose(2, 0, 1)
    lay["L2W1"], lay["L2W2"] = split_rows(a["L2_gnn_W1"].T), split_rows(a["L2_gnn_W2"].T)
    lay["bn1"] = np.stack([columns(a["L2_gnn_" + n]) for n in ("b1", "g1", "be1")], 1)
    lay["bn2"] = np.stack([columns(a["L2_gnn_" + n]) for n in ("b2", "g2", "be2")], 1)
    for n in ("Wq", "Wk", "Wv"):
        lay[n + "3"] = split_rows(a["L3_gnn_" + n])
    lay["Wo3"] = a["L3_gnn_Wo"]
    lay["qk3b"] = np.stack([a["L3_gnn_bq"], a["L3_gnn_bk"]], 1)
    lay["bv3"], lay["bo3"] = columns(a["L3_gnn_bv"]), a["L3_gnn_bo"]
    lay["alpha"], lay["gamma"] = a["L3_gnn_alpha"].reshape(1), a["L3_gnn_gamma"].reshape(1)

    nc = bacc.Bacc("TRN2", target_bir_lowering=False, num_devices=1)
    arrays, dram = {}, {}
    for n, v in lay.items():
        v = np.ascontiguousarray(v)
        arrays["in_" + n] = v
        dram[n] = nc.dram_tensor("in_" + n, v.shape, mybir.dt.from_np(v.dtype), kind="ExternalInput").ap()
    out = nc.dram_tensor("out_0", a["x"].shape, F32, kind="ExternalOutput").ap()
    build_stack(nc, dram, out)
    return run_bass_kernel_spmd(nc, [arrays], core_ids=[0]).results[0]["out_0"]
```
